# Optimizing a Trainium2 kernel written in Bass

```python
import numpy as np
import jax
import jax.numpy as jnp

def _softmax(x, axis=-1):
    return jax.nn.softmax(x, axis=axis)

def _gelu(x):
    return jax.nn.gelu(x, approximate=True)

def _silu(x):
    return jax.nn.silu(x)

def _sigmoid(x):
    return jax.nn.sigmoid(x)

def _layernorm(x, axis=-1, eps=1e-05):
    m = jnp.mean(x, axis=axis, keepdims=True)
    v = jnp.var(x, axis=axis, keepdims=True)
    return (x - m) / jnp.sqrt(v + eps)

def _scatter_add(tgt, idx, src, axis=0):
    return tgt.at[idx].add(src)

def _segment_sum(src, seg, n):
    return jax.ops.segment_sum(src, seg, n)
kernel_name = 'mk_seq_preln_d2_jaxref_r4_ef593c'

def setup_inputs(seed: int=0):
    np.random.seed(seed)
    _w = jnp.asarray

    def _L0_attn_setup():
        import math
        import jax, jax.numpy as jnp
        import numpy as np
        B, S, D, H = (4, 512, 256, 16)
        HD = D // H
        SAMPLING_FACTOR = 5.0
        key = jax.random.key(seed)
        ks = jax.random.split(key, 6)
        std = 1.0 / math.sqrt(D)
        inp = {'x': jax.random.normal(ks[0], (B, S, D), dtype=jnp.float32), 'Wq': jax.random.normal(ks[1], (D, D), dtype=jnp.float32) * std, 'bq': jnp.zeros((D,), dtype=jnp.float32), 'Wk': jax.random.normal(ks[2], (D, D), dtype=jnp.float32) * std, 'bk': jnp.zeros((D,), dtype=jnp.float32), 'Wv': jax.random.normal(ks[3], (D, D), dtype=jnp.float32) * std, 'bv': jnp.zeros((D,), dtype=jnp.float32), 'Wo': jax.random.normal(ks[4], (D, D), dtype=jnp.float32) * std, 'bo': jnp.zeros((D,), dtype=jnp.float32), 'sample_idx': jax.random.randint(ks[5], (S,), 0, S, dtype=jnp.int32)}
        return inp
    _L0_attn_in = _L0_attn_setup()

    def _L0_ffn_setup():
        import jax, jax.numpy as jnp
        import numpy as np
        NUM_EXPERTS = 8
        CAP_FACTOR = 1.0
        MIN_CAP = 8
        key = jax.random.key(seed)
        ks = jax.random.split(key, 10)
        G, S, D, H, E = (4, 1024, 256, 1024, NUM_EXPERTS)
        s = 0.02
        return {'x': jax.random.normal(ks[0], (G, S, D), dtype=jnp.float32), 'gate': jax.random.normal(ks[1], (D, E), dtype=jnp.float32) * s, 'W1': jax.random.normal(ks[2], (E, D, H), dtype=jnp.float32) * s, 'b1': jnp.zeros((E, H), dtype=jnp.float32), 'W2': jax.random.normal(ks[3], (E, H, D), dtype=jnp.float32) * s, 'b2': jnp.zeros((E, D), dtype=jnp.float32), 'Ws1': jax.random.normal(ks[4], (D, H), dtype=jnp.float32) * s, 'bs1': jnp.zeros((H,), dtype=jnp.float32), 'Ws2': jax.random.normal(ks[5], (H, D), dtype=jnp.float32) * s, 'bs2': jnp.zeros((D,), dtype=jnp.float32)}
    _L0_ffn_in = _L0_ffn_setup()

    def _L1_attn_setup():
        import jax, jax.numpy as jnp
        import numpy as np
        import math
        B, S, D_IN, D_KQ, D_OUT = (4, 512, 256, 256, 256)
        key = jax.random.key(seed)
        ks = jax.random.split(key, 7)
        sc = 0.02
        return {'x': jax.random.normal(ks[0], (B, S, D_IN), jnp.float32), 'Wq': jax.random.normal(ks[1], (D_KQ, D_IN), jnp.float32) * sc, 'bq': jax.random.normal(ks[2], (D_KQ,), jnp.float32) * sc, 'Wk': jax.random.normal(ks[3], (D_KQ, D_IN), jnp.float32) * sc, 'bk': jax.random.normal(ks[4], (D_KQ,), jnp.float32) * sc, 'Wv': jax.random.normal(ks[5], (D_OUT, D_IN), jnp.float32) * sc, 'bv': jax.random.normal(ks[6], (D_OUT,), jnp.float32) * sc}
    _L1_attn_in = _L1_attn_setup()

    def _L1_ffn_setup():
        import jax, jax.numpy as jnp
        import numpy as np
        NUM_EXPERTS = 64
        TOP_K = 2
        B, S, EMB, MLP = (4, 512, 256, 512)
        key = jax.random.key(seed)
        k1, k2, k3, k4, k5 = jax.random.split(key, 5)
        inputs = jax.random.normal(k1, (B, S, EMB), dtype=jnp.float32)
        gate_kernel = jax.random.normal(k2, (EMB, NUM_EXPERTS), dtype=jnp.float32) / np.sqrt(EMB)
        w0 = jax.random.normal(k3, (NUM_EXPERTS, EMB, MLP), dtype=jnp.float32) / np.sqrt(EMB)
        w1 = jax.random.normal(k4, (NUM_EXPERTS, EMB, MLP), dtype=jnp.float32) / np.sqrt(EMB)
        wo = jax.random.normal(k5, (NUM_EXPERTS, MLP, EMB), dtype=jnp.float32) / np.sqrt(MLP)
        return {'inputs': inputs, 'gate_kernel': gate_kernel, 'w0': w0, 'w1': w1, 'wo': wo}
    _L1_ffn_in = _L1_ffn_setup()
    _d = {'L0_attn_x': _L0_attn_in['x'], 'L0_attn_Wq': _L0_attn_in['Wq'], 'L0_attn_bq': _L0_attn_in['bq'], 'L0_attn_Wk': _L0_attn_in['Wk'], 'L0_attn_bk': _L0_attn_in['bk'], 'L0_attn_Wv': _L0_attn_in['Wv'], 'L0_attn_bv': _L0_attn_in['bv'], 'L0_attn_Wo': _L0_attn_in['Wo'], 'L0_attn_bo': _L0_attn_in['bo'], 'L0_attn_sample_idx': _L0_attn_in['sample_idx'], 'L0_ffn_gate': _L0_ffn_in['gate'], 'L0_ffn_W1': _L0_ffn_in['W1'], 'L0_ffn_b1': _L0_ffn_in['b1'], 'L0_ffn_W2': _L0_ffn_in['W2'], 'L0_ffn_b2': _L0_ffn_in['b2'], 'L0_ffn_Ws1': _L0_ffn_in['Ws1'], 'L0_ffn_bs1': _L0_ffn_in['bs1'], 'L0_ffn_Ws2': _L0_ffn_in['Ws2'], 'L0_ffn_bs2': _L0_ffn_in['bs2'], 'L1_attn_Wq': _L1_attn_in['Wq'], 'L1_attn_bq': _L1_attn_in['bq'], 'L1_attn_Wk': _L1_attn_in['Wk'], 'L1_attn_bk': _L1_attn_in['bk'], 'L1_attn_Wv': _L1_attn_in['Wv'], 'L1_attn_bv': _L1_attn_in['bv'], 'L1_ffn_gate_kernel': _L1_ffn_in['gate_kernel'], 'L1_ffn_w0': _L1_ffn_in['w0'], 'L1_ffn_w1': _L1_ffn_in['w1'], 'L1_ffn_wo': _L1_ffn_in['wo']}
    _x0 = _d['L0_attn_x']
    _d['L0_attn_x'] = jax.random.normal(jax.random.fold_in(jax.random.key(seed), 1), (8, 1024, 256), dtype=_x0.dtype)
    del _x0
    return _d

def reference(L0_attn_x, L0_attn_Wq, L0_attn_bq, L0_attn_Wk, L0_attn_bk, L0_attn_Wv, L0_attn_bv, L0_attn_Wo, L0_attn_bo, L0_attn_sample_idx, L0_ffn_gate, L0_ffn_W1, L0_ffn_b1, L0_ffn_W2, L0_ffn_b2, L0_ffn_Ws1, L0_ffn_bs1, L0_ffn_Ws2, L0_ffn_bs2, L1_attn_Wq, L1_attn_bq, L1_attn_Wk, L1_attn_bk, L1_attn_Wv, L1_attn_bv, L1_ffn_gate_kernel, L1_ffn_w0, L1_ffn_w1, L1_ffn_wo):

    def _L0_attn_ref(x, Wq, bq, Wk, bk, Wv, bv, Wo, bo, sample_idx):
        import math
        import jax, jax.numpy as jnp
        import numpy as np
        B, S, D, H = (4, 512, 256, 16)
        HD = D // H
        SAMPLING_FACTOR = 5.0
        batch, seq_len, d_model = x.shape
        scale = math.sqrt(HD)
        u = max(1, min(seq_len, int(SAMPLING_FACTOR * math.log(seq_len + 1))))

        def proj(W, b):
            return (x @ W + b).reshape(batch, seq_len, H, HD).transpose(0, 2, 1, 3)
        Q = proj(Wq, bq)
        K = proj(Wk, bk)
        V = proj(Wv, bv)
        K_sample = K[:, :, sample_idx, :]
        scores_sample = jnp.einsum('bhsd,bhud->bhsu', Q, K_sample) / scale
        M = scores_sample.max(axis=-1) - scores_sample.mean(axis=-1)
        _, top_idx = jax.lax.top_k(M, u)
        Q_reduce = jnp.take_along_axis(Q, top_idx[..., None], axis=2)
        attn_scores = jnp.einsum('bhud,bhsd->bhus', Q_reduce, K) / scale
        attn_probs = jax.nn.softmax(attn_scores, axis=-1)
        context = jnp.einsum('bhus,bhsd->bhud', attn_probs, V)
        V_mean = V.mean(axis=2, keepdims=True)
        out = jnp.broadcast_to(V_mean, (batch, H, seq_len, HD))
        b_idx = jnp.arange(batch)[:, None, None]
        h_idx = jnp.arange(H)[None, :, None]
        out = out.at[b_idx, h_idx, top_idx].set(context)
        out = out.transpose(0, 2, 1, 3).reshape(batch, seq_len, d_model)
        return out @ Wo + bo

    def _L0_ffn_ref(x, gate, W1, b1, W2, b2, Ws1, bs1, Ws2, bs2):
        import jax, jax.numpy as jnp
        import numpy as np
        NUM_EXPERTS = 8
        CAP_FACTOR = 1.0
        MIN_CAP = 8
        G, S, D = x.shape
        E = gate.shape[1]
        T = G * S
        capacity = max(MIN_CAP, int(CAP_FACTOR * T / E))
        logits = jnp.einsum('gsd,de->gse', x, gate)
        probs = jax.nn.softmax(logits, axis=-1)
        flat_probs = probs.transpose(2, 0, 1).reshape(E, T)
        scores, token_idx = jax.lax.top_k(flat_probs, k=capacity)
        scores = jnp.where(scores > -100000000.0, scores, 0.0)
        flat_x = x.reshape(T, D)
        tok = flat_x[token_idx]
        h = jax.nn.gelu(jnp.einsum('ecd,edh->ech', tok, W1) + b1[:, None, :])
        out_tok = jnp.einsum('ech,ehd->ecd', h, W2) + b2[:, None, :]
        scaled = out_tok * scores[..., None]
        routed = jnp.zeros_like(flat_x).at[token_idx.reshape(-1)].add(scaled.reshape(E * capacity, D)).reshape(G, S, D)
        shared = jax.nn.gelu(jnp.einsum('gsd,dh->gsh', x, Ws1) + bs1)
        shared = jnp.einsum('gsh,hd->gsd', shared, Ws2) + bs2
        return routed + shared

    def _L1_attn_ref(x, Wq, bq, Wk, bk, Wv, bv):
        import jax, jax.numpy as jnp
        import numpy as np
        import math
        B, S, D_IN, D_KQ, D_OUT = (4, 512, 256, 256, 256)
        Q = jnp.einsum('bsd,kd->bsk', x, Wq) + bq
        K = jnp.einsum('bsd,kd->bsk', x, Wk) + bk
        V = jnp.einsum('bsd,od->bso', x, Wv) + bv
        scale = 1.0 / math.sqrt(D_KQ)
        attn = jnp.einsum('bqk,bsk->bqs', Q, K) * scale
        s = attn.shape[-1]
        causal = jnp.tril(jnp.ones((s, s), dtype=bool))
        attn = jnp.where(causal[None, :, :], attn, -jnp.inf)
        attn = jax.nn.softmax(attn, axis=-1)
        Z = jnp.einsum('bqs,bso->bqo', attn, V)
        return Z

    def _L1_ffn_ref(inputs, gate_kernel, w0, w1, wo):
        import jax, jax.numpy as jnp
        import numpy as np
        NUM_EXPERTS = 64
        TOP_K = 2
        B, S, EMB, MLP = (4, 512, 256, 512)
        b, s, e = inputs.shape
        x = inputs.reshape(b * s, e)
        gate_logits = jnp.einsum('te,ex->tx', x, gate_kernel)
        weights, selected = jax.lax.top_k(gate_logits, TOP_K)
        weights = jax.nn.softmax(weights.astype(jnp.float32), axis=-1)
        flat_experts = selected.reshape(-1)
        sort_idx = jnp.argsort(flat_experts)
        token_idx = sort_idx // TOP_K
        sorted_x = jnp.take(x, token_idx, axis=0)
        group_sizes = jnp.bincount(flat_experts, length=NUM_EXPERTS).astype(jnp.int32)
        h0 = jax.lax.ragged_dot(sorted_x, w0, group_sizes)
        h1 = jax.lax.ragged_dot(sorted_x, w1, group_sizes)
        inter = jax.nn.silu(h0) * h1
        out_sorted = jax.lax.ragged_dot(inter, wo, group_sizes)
        unsorted = jnp.take(out_sorted, jnp.argsort(sort_idx), axis=0)
        per_tok = unsorted.reshape(b * s, TOP_K, e)
        out = jnp.einsum('BKE,BK->BE', per_tok.astype(jnp.float32), weights)
        return out.reshape(b, s, e)
    x = L0_attn_x
    x = x + _L0_attn_ref(_layernorm(x, axis=-1), L0_attn_Wq, L0_attn_bq, L0_attn_Wk, L0_attn_bk, L0_attn_Wv, L0_attn_bv, L0_attn_Wo, L0_attn_bo, L0_attn_sample_idx)
    x = x + _L0_ffn_ref(_layernorm(x, axis=-1), L0_ffn_gate, L0_ffn_W1, L0_ffn_b1, L0_ffn_W2, L0_ffn_b2, L0_ffn_Ws1, L0_ffn_bs1, L0_ffn_Ws2, L0_ffn_bs2)
    x = x + _L1_attn_ref(_layernorm(x, axis=-1), L1_attn_Wq, L1_attn_bq, L1_attn_Wk, L1_attn_bk, L1_attn_Wv, L1_attn_bv)
    x = x + _L1_ffn_ref(_layernorm(x, axis=-1), L1_ffn_gate_kernel, L1_ffn_w0, L1_ffn_w1, L1_ffn_wo)
    return x

_drawn_inputs = setup_inputs


def setup_inputs(seed=0):
    import zlib

    import numpy as np

    out = dict(_drawn_inputs(seed))
    spreads = {'L0_attn_bq': (0.0, 0.269),
     'L0_attn_bk': (0.0, 2.0),
     'L0_attn_bv': (0.0, 0.1),
     'L0_attn_bo': (0.0, 0.1),
     'L0_ffn_b1': (0.0, 0.1),
     'L0_ffn_b2': (0.0, 0.1),
     'L0_ffn_bs1': (0.0, 0.1),
     'L0_ffn_bs2': (0.0, 0.1)}
    factors = {'L1_attn_bq': 28.713, 'L1_attn_bk': 200.0}
    for name, (base, spread) in spreads.items():
        noise = np.random.default_rng([zlib.crc32(name.encode()), seed]).standard_normal(out[name].shape)
        drawn = base * np.exp(spread * noise) if base else spread * noise
        out[name] = jnp.asarray(drawn.astype(out[name].dtype))
    for name, factor in factors.items():
        out[name] = (out[name] * factor).astype(out[name].dtype)
    return out
```

```python
import concourse.bass as bass
from concourse import mybir
from contextlib import ExitStack

F32 = mybir.dt.float32
F16 = mybir.dt.float16
I32 = mybir.dt.int32
U32 = mybir.dt.uint32
ALU = mybir.AluOpType
ACT = mybir.ActivationFunctionType
AX = mybir.AxisListType


class Shared:
    pass


P = 128
B = 8
S = 1024
D = 256
DC = D // P
ST = S // P
T = B * S
NT = T // P
H = 16
HD = D // H
U = 512
UT = U // P
TOP = 34
EPS = 1e-5
QK = 16.0


def wait_alone(eng, g, sem, value):
    eng.wait_ge(sem, value)
    eng.sem_inc(g.passed, 1)


def split_load_w(w):
    return w.rearrange("(c p) n -> p c n", p=P)


def sharpen_rstd(dve, sem, done, rstd, std, var, tmp):
    dve.reciprocal(rstd[:], std[:]).then_inc(sem, 1)
    dve.wait_ge(sem, done + 1)
    dve.tensor_tensor(tmp[:], rstd[:], rstd[:], ALU.mult).then_inc(sem, 1)
    dve.wait_ge(sem, done + 2)
    dve.scalar_tensor_tensor(out=tmp[:], in0=tmp[:], scalar=-0.5, in1=var[:], op0=ALU.mult, op1=ALU.mult).then_inc(sem, 1)
    dve.wait_ge(sem, done + 3)
    dve.scalar_tensor_tensor(out=rstd[:], in0=tmp[:], scalar=1.5, in1=rstd[:], op0=ALU.add, op1=ALU.mult).then_inc(sem, 1)
    dve.wait_ge(sem, done + 4)


def constants(nc, g):
    made = g.sem("const_made")
    filled = g.sem("const_filled")
    with nc.Block() as block:
        @block.gpsimd
        def _(pool):
            pool.memset(g.ones[:], 1.0).then_inc(filled, 1)
            pool.memset(g.ident[:], 0.0).then_inc(filled, 1)
            pool.wait_ge(filled, 2)
            pool.affine_select(out=g.ident[:], in_=g.ident[:], compare_op=ALU.not_equal, fill=1.0, base=0,
                               pattern=[[-1, P]], channel_multiplier=1).then_inc(made, 1)
            pool.affine_select(out=g.tri[:], in_=g.ones[:], compare_op=ALU.is_gt, fill=0.0, base=0,
                               pattern=[[1, P]], channel_multiplier=-1).then_inc(made, 1)
            pool.iota(g.iota_i[:], pattern=[[1, P]], base=0, channel_multiplier=0).then_inc(made, 1)
            pool.iota(g.part_i[:], pattern=[[0, 1]], base=0, channel_multiplier=1).then_inc(made, 1)

        @block.vector
        def _(dve):
            dve.wait_ge(made, 4)
            dve.tensor_copy(g.iota_f[:], g.iota_i[:])
            dve.tensor_copy(g.part_f[:], g.part_i[:])


def project_samples(nc, g):
    NX = ST + UT
    with ExitStack() as ctx:
        sb = lambda n, s, d=F32: ctx.enter_context(nc.sbuf_tensor(n, s, d))
        wq = sb("a_wq", [P, DC, D])
        wk = sb("a_wk", [P, DC, D])
        bq_row = sb("a_bq_row", [P, D])
        bqk = sb("a_bqk", [P, 2, DC])
        bqk_s = sb("a_bqk_s", [P, 2, DC])
        idx = sb("a_idx", [P, UT], I32)
        xt = [sb(f"a_xt{u}", [P, NX, D]) for u in range(2)]
        xn = sb("a_xn", [P, NX, D])
        st = sb("a_st", [P, NX, 6])
        mv = sb("a_mv", [P, NX, 2])
        var = sb("a_var", [P, NX])
        std = sb("a_std", [P, NX])
        rstd = sb("a_rstd", [P, NX])
        tmp = sb("a_tmp", [P, NX])
        xnT = sb("a_xnT", [P, DC, NX * P])
        q32 = sb("a_q32", [P, DC, S])
        q16 = [sb(f"a_q16_{i}", [P, DC, S], F16) for i in range(2)]
        k32 = sb("a_k32", [P, DC, U])
        kc = sb("a_kc", [P, DC, U])
        k16 = [sb(f"a_k16_{i}", [P, DC, U], F16) for i in range(2)]
        ksum = sb("a_ksum", [P, DC])
        kmean = sb("a_kmean", [P, DC])
        qrow = sb("a_qrow", [P, ST, D])
        tp = [ctx.enter_context(nc.psum_tensor(f"a_tp{i}", [P, 4, P], F32)) for i in range(2)]
        pj = [ctx.enter_context(nc.psum_tensor(f"a_pj{i}", [P, 512], F32)) for i in range(5)]
        w_in, idx_in, idx_next = g.sem("a_w_in"), g.sem("a_idx_in"), g.sem("a_idx_next")
        x_in = [g.sem(f"a_x_in{u}") for u in range(2)]
        s_in = g.sem("a_s_in")
        bias_ok = g.sem("a_bias_ok")
        stats, var_ok, std_ok, rstd_ok, xn_ok = (g.sem("a_" + n) for n in ("stats", "var", "std", "rstd", "xn"))
        tp_ok, xnT_ok = g.sem("a_tp"), g.sem("a_xnT")
        pj_ok, act_pj, dve_pj = g.sem("a_pj_ok"), g.sem("a_act_pj"), g.sem("a_dve_pj")
        kmean_ok, kc_ok, hi_ok, lo_ok = (g.sem("a_" + n) for n in ("kmean", "kc", "hi", "lo"))
        stored = g.sem("a_stored")
        NS = 6
        x_b = g.x.rearrange("(v u) (c p) d -> v u p c d", u=2, p=P)
        x_rows = g.x.rearrange("b s d -> (b s) d")
        q_rows_b = g.q_rows.rearrange("(b c p h) e -> b p c (h e)", b=B, p=P, h=H)
        with nc.allow_non_contiguous_dma(reason="bias columns, 256 words"), nc.Block() as block:
            @block.sync
            def _(sp):
                sp.dma_start(wq[:], split_load_w(g.Wq)).then_inc(w_in, 16)
                sp.dma_start(wk[:], split_load_w(g.Wk)).then_inc(w_in, 16)
                sp.dma_start(bq_row[:], g.bq.rearrange("(a n) -> a n", a=1).to_broadcast([P, D])).then_inc(w_in, 16)
                sp.dma_start(bqk[:, 0, :], g.bq.rearrange("(c p) -> p c", p=P)).then_inc(w_in, 16)
                sp.dma_start(bqk[:, 1, :], g.bk.rearrange("(c p) -> p c", p=P)).then_inc(w_in, 16)
                sp.dma_start(idx[:], g.sample_idx.rearrange("(c p) -> p c", p=P)).then_inc(idx_in, 16)
                with sp.Fori(0, B // 2) as v:
                    for u in range(2):
                        b = v * 2 + u
                        sp.wait_ge(xn_ok, v * 2)
                        sp.dma_start(xt[u][:, 0:ST, :], x_b[v, u]).then_inc(x_in[u], 16)

            @block.scalar
            def _(act):
                act.wait_ge(bias_ok, 1)
                with act.Fori(0, B) as b:
                    act.wait_ge(var_ok, b + 1)
                    act.activation(std[:], var[:], ACT.Sqrt).then_inc(std_ok, 1)
                    for n in range(2 * (NX // 4)):
                        act.wait_ge(tp_ok, b * 6 + n + 1)
                        if n == 0:
                            act.wait_ge(stored, b * (16 * NS))
                        act.copy(xnT[:, n // 3, 512 * (n % 3):512 * (n % 3) + 512],
                                 tp[n % 2][:].rearrange("p a b -> p (a b)")).then_inc(xnT_ok, 1)
                    for n in range(4):
                        act.wait_ge(pj_ok, b * 10 + n + 1)
                        act.activation(q32[:, n // 2, 512 * (n % 2):512 * (n % 2) + 512], pj[n][:], ACT.Identity,
                                       bias=bqk_s[:, 0, n // 2:n // 2 + 1], scale=QK).then_inc(act_pj, 1)
                    for n in range(4, 6):
                        act.wait_ge(pj_ok, b * 10 + n + 1)
                        act.activation(k32[:, n - 4, :], pj[n % 5][:], ACT.Identity,
                                       bias=bqk_s[:, 1, n - 4:n - 3], scale=QK,
                                       accum_out=ksum[:, n - 4:n - 3]).then_inc(act_pj, 1)
                    act.wait_ge(xnT_ok, b * 6 + 6)
                    act.dma_start(g.xnT[b], xnT[:, :, 0:S]).then_inc(stored, 16)
                    act.wait_ge(dve_pj, b * 4 + 4)
                    act.dma_start(q_rows_b[b], qrow[:]).then_inc(stored, 16)
                    for i, ok in ((0, hi_ok), (1, lo_ok)):
                        act.wait_ge(ok, b * 2 + 2)
                        act.dma_start(g.q16[b, i].rearrange("(c p) t -> p c t", p=P), q16[i][:]).then_inc(stored, 16)
                        act.dma_start(g.k16[b, i].rearrange("(c p) t -> p c t", p=P), k16[i][:]).then_inc(stored, 16)
                    act.wait_ge(stored, b * (16 * NS) + 16 * NS)

            @block.tensor
            def _(pe):
                pe.wait_ge(w_in, 80)
                with pe.Fori(0, B) as b:
                    pe.wait_ge(xn_ok, b + 1)
                    for n in range(6):
                        pe.wait_ge(xnT_ok, b * 6 + max(n - 1, 0))
                        for a in range(4):
                            c = 4 * (n % 3) + a
                            last = pe.transpose(tp[n % 2][:, a, :], xn[:, c, P * (n // 3):P * (n // 3) + P], g.ident[:])
                        last.then_inc(tp_ok, 1)
                    pe.wait_ge(xnT_ok, b * 6 + 6)
                    pe.wait_ge(act_pj, b * 6)
                    pe.wait_ge(dve_pj, b * 4)
                    for n in range(6):
                        w, m = (wq, n // 2) if n < 4 else (wk, n - 4)
                        t0 = 512 * (n % 2) if n < 4 else S
                        if n >= 5:
                            pe.wait_ge(act_pj, b * 6 + n - 4)
                        for k in range(DC):
                            last = pe.matmul(pj[n % 5][:], w[:, k, P * m:P * m + P], xnT[:, k, t0:t0 + 512],
                                             start=(k == 0), stop=(k == DC - 1))
                        last.then_inc(pj_ok, 1)
                    for n in range(6, 10):
                        pe.wait_ge(act_pj, b * 6 + n - 4)
                        for a in range(2):
                            c = 2 * (n - 6) + a
                            for k in range(DC):
                                last = pe.matmul(pj[n % 5][:, D * a:D * a + D], xnT[:, k, P * c:P * c + P], wq[:, k, :],
                                                 start=(k == 0), stop=(k == DC - 1))
                        last.then_inc(pj_ok, 1)

            @block.vector
            def _(dve):
                dve.wait_ge(w_in, 80)
                dve.tensor_scalar(bqk_s[:], bqk[:], QK, None, ALU.mult).then_inc(bias_ok, 1)
                with dve.Fori(0, B // 2) as v:
                    for u in range(2):
                        b = v * 2 + u
                        dve.wait_ge(x_in[u], v * 16 + 16)
                        dve.wait_ge(s_in, b * (16 * UT) + 16 * UT)
                        for c in range(NX):
                            dve.bn_stats(st[:, c, :], xt[u][:, c, :]).then_inc(stats, 1)
                        wait_alone(dve, g, stats, b * (2 * NX) + NX)
                        for c in range(NX):
                            dve.bn_aggr(mv[:, c, :], st[:, c, :]).then_inc(stats, 1)
                        dve.wait_ge(stats, b * (2 * NX) + 2 * NX)
                        dve.tensor_scalar(var[:], mv[:, :, 1], EPS, None, ALU.add).then_inc(var_ok, 1)
                        dve.wait_ge(std_ok, b + 1)
                        sharpen_rstd(dve, rstd_ok, b * 4, rstd, std, var, tmp)
                        dve.wait_ge(tp_ok, b * 6)
                        for c in range(NX):
                            last = dve.tensor_scalar(xn[:, c, :], xt[u][:, c, :], mv[:, c, 0:1], rstd[:, c:c + 1],
                                                     ALU.subtract, ALU.mult)
                        last.then_inc(xn_ok, 1)
                        dve.wait_ge(act_pj, b * 6 + 6)
                        dve.wait_ge(stored, b * (16 * NS))
                        dve.tensor_copy(q16[0][:], q32[:]).then_inc(hi_ok, 1)
                        dve.tensor_scalar(kmean[:], ksum[:], -1.0 / U, None, ALU.mult).then_inc(kmean_ok, 1)
                        dve.wait_ge(kmean_ok, b + 1)
                        for m in range(DC):
                            dve.tensor_scalar(kc[:, m, :], k32[:, m, :], kmean[:, m:m + 1], None, ALU.add).then_inc(kc_ok, 1)
                        dve.wait_ge(kc_ok, b * 2 + 2)
                        dve.tensor_copy(k16[0][:], kc[:]).then_inc(hi_ok, 1)
                        dve.wait_ge(hi_ok, b * 2 + 2)
                        dve.tensor_tensor(q16[1][:], q32[:], q16[0][:], ALU.subtract).then_inc(lo_ok, 1)
                        dve.tensor_tensor(k16[1][:], kc[:], k16[0][:], ALU.subtract).then_inc(lo_ok, 1)
                        for n in range(6, 10):
                            dve.wait_ge(pj_ok, b * 10 + n + 1)
                            for a in range(2):
                                last = dve.tensor_tensor(qrow[:, 2 * (n - 6) + a, :], pj[n % 5][:, D * a:D * a + D],
                                                         bq_row[:], ALU.add)
                            last.then_inc(dve_pj, 1)

            @block.gpsimd
            def _(pool):
                pool.wait_ge(idx_in, 16)
                with pool.Fori(0, B // 2) as v:
                    for u in range(2):
                        b = v * 2 + u
                        wait_alone(pool, g, xn_ok, v * 2)
                        for c in range(UT):
                            pool.indirect_dma_start(
                                out=xt[u][:, ST + c, :], out_offset=None, in_=x_rows,
                                in_offset=bass.IndirectOffsetOnAxis(ap=idx[:, c:c + 1], axis=0)).then_inc(s_in, 16)
                        wait_alone(pool, g, s_in, b * (16 * UT) + 16 * UT)
                        pool.tensor_scalar(idx[:], idx[:], float(S), None, ALU.add).then_inc(idx_next, 1)
                        wait_alone(pool, g, idx_next, b + 1)


def score_samples(nc, g):
    K3 = 3 * HD
    with ExitStack() as ctx:
        sb = lambda n, s, d=F32: ctx.enter_context(nc.sbuf_tensor(n, s, d))
        qs = [sb(f"b_qs{u}", [K3, H, S], F16) for u in range(2)]
        ks = [sb(f"b_ks{u}", [K3, H, U], F16) for u in range(2)]
        m = sb("b_m", [P, ST, H])
        mT = sb("b_mT", [H, S])
        sc = [ctx.enter_context(nc.psum_tensor(f"b_sc{i}", [P, 3, U], F32)) for i in range(2)]
        tp = ctx.enter_context(nc.psum_tensor("b_tp", [H, 2, 512], F32))
        s_in = [g.sem(f"b_in{u}") for u in range(2)]
        sc_ok, m_ok, tp_ok, mT_ok, mT_out = (g.sem("b_" + n) for n in ("sc", "m", "tp", "mT", "mT_out"))
        GR = [(h, min(3, H - h)) for h in range(0, H, 3)]
        NG = len(GR)
        PARTS = ((0, 0), (0, 1), (1, 0))
        qv = g.q16.rearrange("(v u) i (h e) t -> v u i e h t", u=2, e=HD)
        kv = g.k16.rearrange("(v u) i (h e) t -> v u i e h t", u=2, e=HD)
        with nc.Block() as block:
            @block.sync
            def _(sp):
                with sp.Fori(0, B // 2) as v:
                    for u in range(2):
                        sp.wait_ge(sc_ok, v * (2 * ST * NG))
                        if u == 1:
                            pass
                        for r, (iq, ik) in enumerate(PARTS):
                            sp.dma_start(qs[u][HD * r:HD * r + HD, :, :], qv[v, u, iq]).then_inc(s_in[u], 16)
                            sp.dma_start(ks[u][HD * r:HD * r + HD, :, :], kv[v, u, ik]).then_inc(s_in[u], 16)

            @block.tensor
            def _(pe):
                with pe.Fori(0, B // 2) as v:
                    for u in range(2):
                        b = v * 2 + u
                        pe.wait_ge(s_in[u], v * 96 + 96)
                        for c in range(ST):
                            for n, (h0, nh) in enumerate(GR):
                                at = c * NG + n
                                pe.wait_ge(m_ok, b * (ST * NG) + max(at - 1, 0))
                                for j in range(nh):
                                    last = pe.matmul(sc[n % 2][:, j, :], qs[u][:, h0 + j, P * c:P * c + P],
                                                     ks[u][:, h0 + j, :], start=True, stop=True)
                                last.then_inc(sc_ok, 1)
                        pe.wait_ge(m_ok, b * (ST * NG) + ST * NG)
                        pe.wait_ge(mT_ok, b)
                        for c in range(ST):
                            last = pe.transpose(tp[:, c // 4, P * (c % 4):P * (c % 4) + P], m[:, c, :], g.ident[:])
                        last.then_inc(tp_ok, 1)

            @block.vector
            def _(dve):
                with dve.Fori(0, B) as b:
                    dve.wait_ge(tp_ok, b)
                    for c in range(ST):
                        for n, (h0, nh) in enumerate(GR):
                            dve.wait_ge(sc_ok, b * (ST * NG) + c * NG + n + 1)
                            dve.tensor_reduce(m[:, c, h0:h0 + nh], sc[n % 2][:, 0:nh, :], AX.X, ALU.max).then_inc(m_ok, 1)

            @block.scalar
            def _(act):
                with act.Fori(0, B) as b:
                    act.wait_ge(tp_ok, b + 1)
                    act.copy(mT[:], tp[:].rearrange("p a b -> p (a b)")).then_inc(mT_ok, 1)
                    act.wait_ge(mT_ok, b + 1)
                    act.dma_start(g.m_rows.rearrange("(b h) t -> b h t", b=B)[b], mT[:]).then_inc(mT_out, 16)
                    act.wait_ge(mT_out, b * 16 + 16)


def pick_queries(nc, g):
    RND = -(-TOP // 8)
    with ExitStack() as ctx:
        sb = lambda n, s, d=F32: ctx.enter_context(nc.sbuf_tensor(n, s, d))
        m = [sb(f"c_m{i}", [P, S]) for i in range(2)]
        top = sb("c_top", [P, RND, 8])
        at = sb("c_at", [P, RND, 8], U32)
        atf = sb("c_atf", [P, RND * 8])
        base = sb("c_base", [P, 1], I32)
        basf = sb("c_basf", [P, 1])
        lowi = sb("c_lowi", [P, 1], I32)
        lowf = sb("c_lowf", [P, 1])
        rows = sb("c_rows", [P, RND * 8], I32)
        m_in, step, out = g.sem("c_in"), g.sem("c_step"), g.sem("c_out")
        with nc.Block() as block:
            @block.sync
            def _(sp):
                sp.dma_start(m[0][:], g.m_rows).then_inc(m_in, 16)
                sp.wait_ge(step, 3 * RND + 5)
                sp.dma_start(g.sel_rows.rearrange("(r j) a -> r (j a)", j=TOP), rows[:, 0:TOP]).then_inc(out, 16)
                sp.wait_ge(out, 16)

            @block.vector
            def _(dve):
                n = 0
                dve.wait_ge(m_in, 16)

                def then(ins):
                    nonlocal n
                    n += 1
                    ins.then_inc(step, 1)
                    dve.wait_ge(step, n)
                for r in range(RND):
                    then(dve.max(top[:, r, :], m[r % 2][:]))
                    then(dve.max_index(at[:, r, :], top[:, r, :], m[r % 2][:]))
                    then(dve.match_replace(m[1 - r % 2][:], top[:, r, :], m[r % 2][:], -3.0e38))
                then(dve.tensor_scalar(lowi[:], g.part_i[:], H - 1, None, ALU.bitwise_and))
                then(dve.tensor_copy(lowf[:], lowi[:]))
                then(dve.tensor_tensor(basf[:], g.part_f[:], lowf[:], ALU.subtract))
                then(dve.scalar_tensor_tensor(out=basf[:], in0=basf[:], scalar=float(S), in1=lowf[:],
                                              op0=ALU.mult, op1=ALU.add))
                then(dve.tensor_scalar(rows[:], at[:].rearrange("p r k -> p (r k)"), float(H), basf[:, 0:1],
                                       ALU.mult, ALU.add))


def attend_selected(nc, g):
    NCH = 6
    HH = H // 2
    CH = [(n // 3, 3 * (n % 3), min(3, HH - 3 * (n % 3))) for n in range(NCH)]
    RM = 3 * TOP
    with ExitStack() as ctx:
        sb = lambda n, s, d=F32: ctx.enter_context(nc.sbuf_tensor(n, s, d))
        wk, wv = sb("d_wk", [P, DC, D]), sb("d_wv", [P, DC, D])
        bk, bv_row = sb("d_bk", [P, DC]), sb("d_bv_row", [P, D])
        mask = sb("d_mask", [RM, 3, HH])
        xT = [sb(f"d_xT{u}", [P, DC, S]) for u in range(2)]
        idx = [sb(f"d_idx{u}", [RM, NCH], I32) for u in range(2)]
        kT, v_ = sb("d_kT", [P, DC, S]), sb("d_v", [P, ST, D])
        vm = sb("d_vm", [P, D])
        qg = sb("d_qg", [RM, NCH, HD])
        e_ = sb("d_e", [RM, NCH, HH, HD])
        bd = sb("d_bd", [P, NCH, RM])
        mx, nmx = sb("d_mx", [RM, NCH]), sb("d_nmx", [RM, NCH])
        rs, rinv = sb("d_rs", [RM, NCH]), sb("d_rinv", [RM, NCH])
        pm = [sb(f"d_pm{i}", [RM, S]) for i in range(2)]
        pT = sb("d_pT", [P, ST, RM])
        cm = sb("d_cm", [RM, HH, HD])
        cr = sb("d_cr", [RM, NCH, HD])
        sc = [ctx.enter_context(nc.psum_tensor(f"d_sc{i}", [P, 2, 512], F32)) for i in range(2)]
        pt = ctx.enter_context(nc.psum_tensor("d_pt", [P, 2, 4, P], F32))
        bdp = ctx.enter_context(nc.psum_tensor("d_bdp", [P, 3, P], F32))
        cx = ctx.enter_context(nc.psum_tensor("d_cx", [P, P], F32))
        w_in = g.sem("d_w_in")
        x_in = [g.sem(f"d_x_in{u}") for u in range(2)]
        (pj_ok, kt_ok, v_ok, vm_ok, vm_out, qg_in, e_ok, bdp_ok, bd_ok, sc_ok, mx_ok, nmx_ok, exp_ok, pt_ok,
         pTa_ok, pTb_ok, cx_ok, rinv_ok, cm_ok, cr_ok, put) = (g.sem("d_" + n) for n in (
             "pj", "kt", "v", "vm", "vm_out", "qg", "e", "bdp", "bd", "sc", "mx", "nmx", "exp", "pt",
             "pTa", "pTb", "cx", "rinv", "cm", "cr", "put"))
        mask1, mask2, mask3 = g.sem("d_mask1"), g.sem("d_mask2"), g.sem("d_mask3")
        x_b = g.xnT.rearrange("(v u) p c t -> v u p c t", u=2)
        sel_b = g.sel_rows.rearrange("(v u r) a -> v u r a", u=2, r=H * TOP)
        out_b = g.attn_rows.rearrange("(b c p h) e -> b p c (h e)", b=B, p=P, h=H)
        with nc.allow_non_contiguous_dma(reason="bias columns and row numbers"), nc.Block() as block:
            @block.sync
            def _(sp):
                sp.dma_start(wk[:], split_load_w(g.Wk)).then_inc(w_in, 16)
                sp.dma_start(wv[:], split_load_w(g.Wv)).then_inc(w_in, 16)
                sp.dma_start(bk[:], g.bk.rearrange("(c p) -> p c", p=P)).then_inc(w_in, 16)
                sp.dma_start(bv_row[:], g.bv.rearrange("(a n) -> a n", a=1).to_broadcast([P, D])).then_inc(w_in, 16)
                with sp.Fori(0, B // 2) as v:
                    for u in range(2):
                        b = v * 2 + u
                        sp.wait_ge(pj_ok, v * 18)
                        sp.dma_start(xT[u][:], x_b[v, u]).then_inc(x_in[u], 16)
                        sp.wait_ge(put, v * (32 * NCH))
                        for n, (hf, h0, nh) in enumerate(CH):
                            r0 = (hf * HH + h0) * TOP
                            sp.dma_start(idx[u][0:nh * TOP, n:n + 1],
                                         sel_b[v, u, r0:r0 + nh * TOP, :]).then_inc(x_in[u], 16)
                    for u in range(2):
                        b = v * 2 + u
                        sp.wait_ge(vm_ok, b + 1)
                        sp.dma_start(out_b[b], vm[:].unsqueeze(1).to_broadcast([P, ST, D])).then_inc(vm_out, 16)

            @block.tensor
            def _(pe):
                pe.wait_ge(w_in, 64)
                with pe.Fori(0, B // 2) as v:
                    for u in range(2):
                        b = v * 2 + u
                        pe.wait_ge(x_in[u], v * 112 + 112)
                        pe.wait_ge(exp_ok, b * NCH)
                        for n in range(9):
                            out = sc[n % 4 // 2][:, n % 2, :]
                            if 4 <= n < 8:
                                pe.wait_ge(kt_ok, b * 4 + n - 3)
                            if n < 4:
                                m, t0 = n // 2, 512 * (n % 2)
                                for k in range(DC):
                                    last = pe.matmul(out, wk[:, k, P * m:P * m + P], xT[u][:, k, t0:t0 + 512],
                                                     start=(k == 0), stop=(k == DC - 1))
                            elif n < 8:
                                for a in range(2):
                                    c = 2 * (n - 4) + a
                                    for k in range(DC):
                                        last = pe.matmul(out[:, D * a:D * a + D], xT[u][:, k, P * c:P * c + P],
                                                         wv[:, k, :], start=(k == 0), stop=(k == DC - 1))
                            else:
                                pe.wait_ge(v_ok, b * 4 + 4)
                                for c in range(ST):
                                    last = pe.matmul(out[:, 0:D], g.ones[:], v_[:, c, :],
                                                     start=(c == 0), stop=(c == ST - 1))
                            last.then_inc(pj_ok, 1)
                        pe.wait_ge(e_ok, b * NCH + NCH)
                        for r in range(2):
                            pe.wait_ge(bd_ok, b * NCH + 3 * r)
                            for kk in range(3):
                                rows = CH[kk][2] * TOP
                                last = pe.transpose(bdp[:, kk, 0:rows],
                                                    e_[0:rows, 3 * r + kk, :, :].rearrange("r h e -> r (h e)"),
                                                    g.ident[0:rows, 0:rows])
                            last.then_inc(bdp_ok, 1)
                        pe.wait_ge(vm_ok, b + 1)
                        for i in range(NCH + 1):
                            if i >= 1:
                                n, rows = i - 1, CH[i - 1][2] * TOP
                                pe.wait_ge(exp_ok, b * NCH + n + 1)
                                pe.wait_ge(pTa_ok, b * NCH + n)
                                pe.wait_ge(pTb_ok, b * NCH + n)
                                for c in range(ST):
                                    last = pe.transpose(pt[:, c // 4, c % 4, 0:rows], pm[n % 2][0:rows, P * c:P * c + P],
                                                        g.ident[0:rows, 0:rows])
                                last.then_inc(pt_ok, 1)
                            if i < NCH:
                                n, hf, rows = i, CH[i][0], CH[i][2] * TOP
                                pe.wait_ge(bd_ok, b * NCH + n + 1)
                                for s in range(2):
                                    last = pe.matmul(sc[n % 2][0:rows, s, :], bd[:, n, 0:rows],
                                                     kT[:, hf, 512 * s:512 * s + 512], start=True, stop=True)
                                last.then_inc(sc_ok, 1)
                            if i >= 1:
                                n, hf, rows = i - 1, CH[i - 1][0], CH[i - 1][2] * TOP
                                pe.wait_ge(pTa_ok, b * NCH + n + 1)
                                pe.wait_ge(pTb_ok, b * NCH + n + 1)
                                pe.wait_ge(cm_ok, b * NCH + n)
                                for c in range(ST):
                                    last = pe.matmul(cx[0:rows, :], pT[:, c, 0:rows], v_[:, c, P * hf:P * hf + P],
                                                     start=(c == 0), stop=(c == ST - 1))
                                last.then_inc(cx_ok, 1)

            @block.scalar
            def _(act):
                act.wait_ge(w_in, 64)
                with act.Fori(0, B) as b:
                    act.wait_ge(cx_ok, b * NCH)
                    for n in range(4):
                        act.wait_ge(pj_ok, b * 9 + n + 1)
                        act.activation(kT[:, n // 2, 512 * (n % 2):512 * (n % 2) + 512], sc[n // 2][:, n % 2, :],
                                       ACT.Identity, bias=bk[:, n // 2:n // 2 + 1]).then_inc(kt_ok, 1)
                    act.wait_ge(pj_ok, b * 9 + 9)
                    act.wait_ge(vm_out, b * 16)
                    act.mul(vm[:], sc[0][:, 0, 0:D], 1.0 / S).then_inc(vm_ok, 1)
                    for r in range(2):
                        act.wait_ge(bdp_ok, b * 2 + r + 1)
                        for kk in range(3):
                            rows = CH[kk][2] * TOP
                            act.copy(bd[:, 3 * r + kk, 0:rows], bdp[:, kk, 0:rows]).then_inc(bd_ok, 1)
                    for i in range(NCH + 1):
                        if i >= 1:
                            n, rows = i - 1, CH[i - 1][2] * TOP
                            act.wait_ge(pt_ok, b * NCH + n + 1)
                            act.wait_ge(cx_ok, b * NCH + n)
                            act.copy(pT[:, 0:4, 0:rows], pt[:, 0, :, 0:rows]).then_inc(pTa_ok, 1)
                        if i < NCH:
                            n, rows = i, CH[i][2] * TOP
                            act.wait_ge(nmx_ok, b * NCH + n + 1)
                            act.activation(pm[n % 2][0:rows, :], sc[n % 2][0:rows, :, :].rearrange("r a t -> r (a t)"),
                                           ACT.Exp, bias=nmx[0:rows, n:n + 1], scale=0.25,
                                           accum_out=rs[0:rows, n:n + 1]).then_inc(exp_ok, 1)

            @block.vector
            def _(dve):
                dve.wait_ge(w_in, 64)
                dve.wait_ge(mask3, 3)
                with dve.Fori(0, B) as b:
                    dve.wait_ge(cx_ok, b * NCH)
                    for n in range(4):
                        dve.wait_ge(pj_ok, b * 9 + n + 5)
                        dve.tensor_tensor(v_[:, 2 * n:2 * n + 2, :], sc[n // 2][:, n % 2, :].rearrange("p (a d) -> p a d", a=2),
                                          bv_row[:].unsqueeze(1).to_broadcast([P, 2, D]), ALU.add).then_inc(v_ok, 1)
                    dve.wait_ge(qg_in, b * (16 * NCH) + 16 * NCH)
                    for n, (hf, h0, nh) in enumerate(CH):
                        r = nh * TOP
                        dve.tensor_tensor(e_[0:r, n, :, :], qg[0:r, n, :].unsqueeze(1).to_broadcast([r, HH, HD]),
                                          mask[0:r, n % 3, :].unsqueeze(2).to_broadcast([r, HH, HD]),
                                          ALU.mult).then_inc(e_ok, 1)
                    for i in range(NCH + 1):
                        if i >= 1:
                            n, rows = i - 1, CH[i - 1][2] * TOP
                            dve.wait_ge(pt_ok, b * NCH + n + 1)
                            dve.wait_ge(cx_ok, b * NCH + n)
                            dve.tensor_copy(pT[:, 4:8, 0:rows], pt[:, 1, :, 0:rows]).then_inc(pTb_ok, 1)
                        if i < NCH:
                            n, rows = i, CH[i][2] * TOP
                            dve.wait_ge(sc_ok, b * NCH + n + 1)
                            dve.tensor_reduce(mx[0:rows, n:n + 1], sc[n % 2][0:rows, :, :], AX.XY, ALU.max).then_inc(mx_ok, 1)
                            dve.wait_ge(mx_ok, b * NCH + n + 1)
                            dve.tensor_scalar(nmx[0:rows, n:n + 1], mx[0:rows, n:n + 1], -0.25, None,
                                              ALU.mult).then_inc(nmx_ok, 1)
                        if i >= 1:
                            n, rows = i - 1, CH[i - 1][2] * TOP
                            dve.reciprocal(rinv[0:rows, n:n + 1], rs[0:rows, n:n + 1]).then_inc(rinv_ok, 1)
                            dve.wait_ge(rinv_ok, b * NCH + n + 1)
                            dve.wait_ge(cx_ok, b * NCH + n + 1)
                            dve.scalar_tensor_tensor(out=cm[0:rows, :, :],
                                                     in0=cx[0:rows, :].rearrange("r (h e) -> r h e", h=HH),
                                                     scalar=rinv[0:rows, n:n + 1],
                                                     in1=mask[0:rows, n % 3, :].unsqueeze(2).to_broadcast([rows, HH, HD]),
                                                     op0=ALU.mult, op1=ALU.mult).then_inc(cm_ok, 1)
                            dve.wait_ge(cm_ok, b * NCH + n + 1)
                            dve.wait_ge(put, b * (16 * NCH))
                            dve.tensor_reduce(cr[0:rows, n, :], cm[0:rows, :, :].rearrange("r h e -> r e h"),
                                              AX.X, ALU.add).then_inc(cr_ok, 1)

            @block.gpsimd
            def _(pool):
                pool.memset(mask[:], 1.0).then_inc(mask1, 1)
                pool.wait_ge(mask1, 1)
                for kk in range(3):
                    pool.affine_select(out=mask[:, kk, :], in_=mask[:, kk, :], compare_op=ALU.is_ge, fill=0.0,
                                       base=TOP * 3 * kk, pattern=[[-TOP, HH]], channel_multiplier=1).then_inc(mask2, 1)
                pool.wait_ge(mask2, 3)
                for kk in range(3):
                    pool.affine_select(out=mask[:, kk, :], in_=mask[:, kk, :], compare_op=ALU.is_ge, fill=0.0,
                                       base=TOP - 1 - TOP * 3 * kk, pattern=[[TOP, HH]],
                                       channel_multiplier=-1).then_inc(mask3, 1)
                with pool.Fori(0, B // 2) as v:
                    for u in range(2):
                        b = v * 2 + u
                        pool.wait_ge(x_in[u], v * 112 + 112)
                        wait_alone(pool, g, e_ok, b * NCH)
                        for n, (hf, h0, nh) in enumerate(CH):
                            r = nh * TOP
                            pool.indirect_dma_start(
                                out=qg[0:r, n, :], out_offset=None, in_=g.q_rows,
                                in_offset=bass.IndirectOffsetOnAxis(ap=idx[u][0:r, n:n + 1], axis=0)).then_inc(qg_in, 16)
                        pool.wait_ge(vm_out, b * 16 + 16)
                        for n, (hf, h0, nh) in enumerate(CH):
                            r = nh * TOP
                            wait_alone(pool, g, cr_ok, b * NCH + n + 1)
                            pool.indirect_dma_start(
                                out=g.attn_rows, in_=cr[0:r, n, :], in_offset=None,
                                out_offset=bass.IndirectOffsetOnAxis(ap=idx[u][0:r, n:n + 1], axis=0)).then_inc(put, 16)
                pool.wait_ge(put, B * 16 * NCH)


def add_attention_and_gate(nc, g):
    E = 8
    with ExitStack() as ctx:
        sb = lambda n, s, d=F32: ctx.enter_context(nc.sbuf_tensor(n, s, d))
        wo, gate = sb("e_wo", [P, DC, D]), sb("e_gate", [P, DC, E])
        bo_row = sb("e_bo_row", [P, D])
        a_ = [sb(f"e_attn{u}", [P, ST, D]) for u in range(2)]
        x_ = [sb(f"e_xin{u}", [P, ST, D]) for u in range(2)]
        aT = sb("e_aT", [P, DC, S])
        x1 = sb("e_x1", [P, ST, D])
        xn = sb("e_xn", [P, ST, D])
        xnT = sb("e_xnT", [P, DC, S])
        st, mv = sb("e_st", [P, ST, 6]), sb("e_mv", [P, ST, 2])
        var, std, rstd, tmp = (sb("e_" + n, [P, ST]) for n in ("var", "std", "rstd", "tmp"))
        mx, den, rden = (sb("e_" + n, [P, ST]) for n in ("mx", "den", "rden"))
        lg, ex, pr = (sb("e_" + n, [P, ST, E]) for n in ("lg", "ex", "pr"))
        tp = [ctx.enter_context(nc.psum_tensor(f"e_tp{i}", [P, 4, P], F32)) for i in range(2)]
        pj = [ctx.enter_context(nc.psum_tensor(f"e_pj{i}", [P, 2, D], F32)) for i in range(4)]
        gt = ctx.enter_context(nc.psum_tensor("e_gt", [P, ST, E], F32))
        w_in = g.sem("e_w_in")
        in_ = [g.sem(f"e_in{u}") for u in range(2)]
        (tp_ok, T_ok, xb_ok, pj_ok, x1_ok, stats, var_ok, std_ok, rstd_ok, xn_ok, gt_ok, sm, ex_ok, out) = (
            g.sem("e_" + n) for n in ("tp", "T", "xb", "pj", "x1", "stats", "var", "std", "rstd", "xn", "gt",
                                      "sm", "ex", "out"))
        NO = 4
        tiles = lambda t: t.rearrange("(v u c p) d -> v u p c d", u=2, c=ST, p=P)
        out_tiles = lambda t: t.rearrange("(b c p) d -> b p c d", c=ST, p=P)
        attn = tiles(g.attn_rows.rearrange("(t h) e -> t (h e)", h=H))
        x_b = tiles(g.x.rearrange("b s d -> (b s) d"))
        tab = out_tiles(g.tab)
        with nc.Block() as block:
            @block.sync
            def _(sp):
                sp.dma_start(wo[:], split_load_w(g.Wo)).then_inc(w_in, 16)
                sp.dma_start(gate[:], split_load_w(g.gate)).then_inc(w_in, 16)
                sp.dma_start(bo_row[:], g.bo.rearrange("(a n) -> a n", a=1).to_broadcast([P, D])).then_inc(w_in, 16)
                with sp.Fori(0, B // 2) as v:
                    for u in range(2):
                        sp.wait_ge(x1_ok, v * 8)
                        sp.dma_start(a_[u][:], attn[v, u]).then_inc(in_[u], 16)
                        sp.dma_start(x_[u][:], x_b[v, u]).then_inc(in_[u], 16)

            @block.gpsimd
            def _(pool):
                pool.wait_ge(w_in, 48)
                with pool.Fori(0, B // 2) as v:
                    for u in range(2):
                        pool.wait_ge(in_[u], v * 32 + 32)
                        for c in range(ST):
                            last = pool.tensor_tensor(x_[u][:, c, :], x_[u][:, c, :], bo_row[:], ALU.add)
                        last.then_inc(xb_ok, 1)

            @block.tensor
            def _(pe):
                pe.wait_ge(w_in, 48)
                with pe.Fori(0, B // 2) as v:
                    for u in range(2):
                        b = v * 2 + u
                        pe.wait_ge(in_[u], v * 32 + 32)
                        for n in range(8):
                            src = a_[u] if n < 4 else xn
                            pe.wait_ge(T_ok, b * 8 + max(n - 1, 0))
                            if n == 4:
                                pe.wait_ge(T_ok, b * 8 + 4)
                                pe.wait_ge(x1_ok, b * 4)
                                for c in range(ST):
                                    for k in range(DC):
                                        last = pe.matmul(pj[c // 2][:, c % 2, :], aT[:, k, P * c:P * c + P], wo[:, k, :],
                                                         start=(k == 0), stop=(k == DC - 1))
                                    if c % 2:
                                        last.then_inc(pj_ok, 1)
                                pe.wait_ge(xn_ok, b + 1)
                            for a in range(4):
                                c = 4 * (n % 2) + a
                                k = (n % 4) // 2
                                last = pe.transpose(tp[n % 2][:, a, :], src[:, c, P * k:P * k + P], g.ident[:])
                            last.then_inc(tp_ok, 1)
                        pe.wait_ge(T_ok, b * 8 + 8)
                        pe.wait_ge(sm, b * 6)
                        for c in range(ST):
                            for k in range(DC):
                                last = pe.matmul(gt[:, c, :], xnT[:, k, P * c:P * c + P], gate[:, k, :],
                                                 start=(k == 0), stop=(k == DC - 1))
                        last.then_inc(gt_ok, 1)

            @block.scalar
            def _(act):
                with act.Fori(0, B) as b:
                    for n in range(8):
                        act.wait_ge(tp_ok, b * 8 + n + 1)
                        dst = aT if n < 4 else xnT
                        if n == 4:
                            act.wait_ge(out, b * (16 * NO))
                        act.copy(dst[:, (n % 4) // 2, 512 * (n % 2):512 * (n % 2) + 512],
                                 tp[n % 2][:].rearrange("p a b -> p (a b)")).then_inc(T_ok, 1)
                        if n == 3:
                            act.wait_ge(var_ok, b + 1)
                            act.activation(std[:], var[:], ACT.Sqrt).then_inc(std_ok, 1)
                    act.wait_ge(sm, b * 6 + 2)
                    act.activation(ex[:], lg[:], ACT.Exp).then_inc(ex_ok, 1)
                    act.dma_start(out_tiles(g.x1)[b], x1[:]).then_inc(out, 16)
                    act.dma_start(tab[b][:, :, 0:D], xn[:]).then_inc(out, 16)
                    act.wait_ge(T_ok, b * 8 + 8)
                    act.dma_start(g.xnT1[b], xnT[:]).then_inc(out, 16)
                    act.wait_ge(sm, b * 6 + 5)
                    act.dma_start(tab[b][:, :, D:D + E], pr[:]).then_inc(out, 16)
                    act.wait_ge(out, b * (16 * NO) + 16 * NO)

            @block.vector
            def _(dve):
                with dve.Fori(0, B // 2) as v:
                    for u in range(2):
                        b = v * 2 + u
                        dve.wait_ge(xb_ok, b + 1)
                        dve.wait_ge(out, b * (16 * NO))
                        for n in range(4):
                            dve.wait_ge(pj_ok, b * 4 + n + 1)
                            dve.tensor_tensor(x1[:, 2 * n:2 * n + 2, :], pj[n][:], x_[u][:, 2 * n:2 * n + 2, :],
                                              ALU.add).then_inc(x1_ok, 1)
                        dve.wait_ge(x1_ok, b * 4 + 4)
                        for c in range(ST):
                            dve.bn_stats(st[:, c, :], x1[:, c, :]).then_inc(stats, 1)
                        wait_alone(dve, g, stats, b * (2 * ST) + ST)
                        for c in range(ST):
                            dve.bn_aggr(mv[:, c, :], st[:, c, :]).then_inc(stats, 1)
                        dve.wait_ge(stats, b * (2 * ST) + 2 * ST)
                        dve.tensor_scalar(var[:], mv[:, :, 1], EPS, None, ALU.add).then_inc(var_ok, 1)
                        dve.wait_ge(std_ok, b + 1)
                        sharpen_rstd(dve, rstd_ok, b * 4, rstd, std, var, tmp)
                        for c in range(ST):
                            last = dve.tensor_scalar(xn[:, c, :], x1[:, c, :], mv[:, c, 0:1], rstd[:, c:c + 1],
                                                     ALU.subtract, ALU.mult)
                        last.then_inc(xn_ok, 1)
                        dve.wait_ge(gt_ok, b + 1)
                        dve.tensor_reduce(mx[:], gt[:], AX.X, ALU.max).then_inc(sm, 1)
                        dve.wait_ge(sm, b * 6 + 1)
                        dve.tensor_tensor(lg[:], gt[:], mx[:].unsqueeze(2).to_broadcast([P, ST, E]),
                                          ALU.subtract).then_inc(sm, 1)
                        dve.wait_ge(ex_ok, b + 1)
                        dve.tensor_reduce(den[:], ex[:], AX.X, ALU.add).then_inc(sm, 1)
                        dve.wait_ge(sm, b * 6 + 3)
                        dve.reciprocal(rden[:], den[:]).then_inc(sm, 1)
                        dve.wait_ge(sm, b * 6 + 4)
                        dve.tensor_tensor(pr[:], ex[:], rden[:].unsqueeze(2).to_broadcast([P, ST, E]),
                                          ALU.mult).then_inc(sm, 1)
                        dve.wait_ge(sm, b * 6 + 5)
                        dve.tensor_copy(g.probs.rearrange("p e (b c) -> p b e c", b=B)[:, b, :, :],
                                        pr[:].rearrange("p c e -> p e c")).then_inc(sm, 1)

E0 = 8
CAP = T // E0
HID = 1024
HC = HID // P
BF16 = mybir.dt.bfloat16
ROW = D + E0


def choose_tokens(nc, g):
    with ExitStack() as ctx:
        sb = lambda n, s, d=F32: ctx.enter_context(nc.sbuf_tensor(n, s, d))
        thr, cand, keep = (sb("f_" + n, [P, E0], I32) for n in ("thr", "cand", "keep"))
        bit = sb("f_bit", [P, 1], I32)
        flag = sb("f_flag", [P, E0, NT])
        cnt, need = sb("f_cnt", [P, E0]), sb("f_need", [P, E0])
        eq, sel = sb("f_eq", [P, E0, NT]), sb("f_sel", [P, E0, NT])
        go_on = sb("f_go_on", [P, E0, NT])
        incl, pos = sb("f_incl", [P, E0, NT]), sb("f_pos", [P, E0, NT])
        posi, hi_i, lo_i = (sb("f_" + n, [P, E0, NT], I32) for n in ("posi", "hi_i", "lo_i"))
        hi_f, lo_f = sb("f_hi_f", [P, E0, NT]), sb("f_lo_f", [P, E0, NT])
        hot_lo = sb("f_hot_lo", [P, NT, P], BF16)
        hot_hi = sb("f_hot_hi", [P, NT, CAP // P])
        val = sb("f_val", [P, 2, NT, CAP // P], BF16)
        colf = sb("f_colf", [P, NT])
        lst = sb("f_lst", [P, CAP // P])
        tot = ctx.enter_context(nc.psum_tensor("f_tot", [P, E0], F32))
        pre = ctx.enter_context(nc.psum_tensor("f_pre", [P, E0, NT], F32))
        col = ctx.enter_context(nc.psum_tensor("f_col", [P, E0, NT], F32))
        lp = ctx.enter_context(nc.psum_tensor("f_lp", [P, 2, CAP // P], F32))
        step, cnt_ok, tot_ok, pre_in, pre_ok, hot_ok, lp_ok, lst_ok, stepe = (
            g.sem("f_" + n) for n in ("step", "cnt", "tot", "pre_in", "pre", "hot", "lp", "lst", "stepe"))
        BITS, KS = 30, 6
        wide = lambda t: t.unsqueeze(2).to_broadcast([P, E0, NT])
        with nc.Block() as block:
            @block.tensor
            def _(pe):
                with pe.Fori(0, BITS) as i:
                    pe.wait_ge(cnt_ok, i + 1)
                    pe.matmul(tot[:], g.ones[:], cnt[:], start=True, stop=True).then_inc(tot_ok, 1)
                pe.wait_ge(cnt_ok, BITS + 1)
                pe.matmul(tot[:], g.ones[:], cnt[:], start=True, stop=True).then_inc(tot_ok, 1)
                for r, src in enumerate((eq, sel)):
                    pe.wait_ge(pre_in, r + 1)
                    flat = src[:].rearrange("p e c -> p (e c)")
                    pe.matmul(pre[:].rearrange("p e c -> p (e c)"), g.tri[:], flat, start=True, stop=True)
                    pe.matmul(col[:].rearrange("p e c -> p (e c)"), g.ones[:], flat, start=True,
                              stop=True).then_inc(pre_ok, 1)
                with pe.Fori(0, E0) as e:
                    pe.wait_ge(hot_ok, e + 1)
                    for c in range(NT):
                        last = pe.matmul(lp[:], hot_lo[:, c, :], val[:, :, c, :], start=(c == 0), stop=(c == NT - 1))
                    last.then_inc(lp_ok, 1)

            @block.gpsimd
            def _(pool):
                pool.memset(bit[:], 1 << (BITS - 1)).then_inc(lst_ok, 1)
                pool.memset(thr[:], 0).then_inc(lst_ok, 1)
                pool.memset(go_on[:], 1.0).then_inc(lst_ok, 1)
                pool.iota(posi[:, 0, :], pattern=[[1, NT]], base=0, channel_multiplier=0).then_inc(lst_ok, 1)

            @block.vector
            def _(dve):
                n = 0

                def then(ins):
                    nonlocal n
                    n += 1
                    ins.then_inc(step, 1)
                    dve.wait_ge(step, n)

                dve.wait_ge(lst_ok, 4)
                with dve.Fori(0, BITS) as i:
                    def chain(ins, k, sem=step):
                        ins.then_inc(sem, 1)
                        dve.wait_ge(sem, i * KS + k)
                    chain(dve.tensor_tensor(cand[:], thr[:], bit[:].to_broadcast([P, E0]), ALU.bitwise_or), 1)
                    chain(dve.tensor_tensor(flag[:], g.probs, wide(as_float(cand)), ALU.is_ge), 2)
                    dve.tensor_reduce(cnt[:], flag[:], AX.X, ALU.add).then_inc(cnt_ok, 1)
                    dve.wait_ge(tot_ok, i + 1)
                    chain(dve.scalar_tensor_tensor(out=keep[:], in0=tot[:], scalar=float(CAP),
                                                   in1=bit[:].to_broadcast([P, E0]), op0=ALU.is_ge, op1=ALU.mult), 3)
                    chain(dve.tensor_tensor(thr[:], thr[:], keep[:], ALU.bitwise_or), 4)
                    chain(dve.tensor_scalar(bit[:], bit[:], 1, None, ALU.logical_shift_right), 5)
                    chain(dve.tensor_copy(need[:], tot[:]), 6)
                n = BITS * KS
                then(dve.tensor_copy(colf[:], posi[:, 0, :]))
                then(dve.memset(go_on[:, :, 0:1], 0.0))
                then(dve.tensor_tensor(sel[:], g.probs, wide(as_float(thr)), ALU.is_gt))
                then(dve.tensor_tensor(eq[:], g.probs, wide(as_float(thr)), ALU.is_equal))
                dve.tensor_reduce(cnt[:], sel[:], AX.X, ALU.add).then_inc(cnt_ok, 1)
                dve.wait_ge(tot_ok, BITS + 1)
                then(dve.tensor_scalar(need[:], tot[:], -1.0, float(CAP), ALU.mult, ALU.add))
                dve.sem_inc(pre_in, 1)

                def place():
                    then(dve.tensor_copy(flag[:], col[:]))
                    then(dve.tensor_tensor_scan(incl[:].rearrange("p e c -> p (e c)"),
                                                go_on[:].rearrange("p e c -> p (e c)"),
                                                flag[:].rearrange("p e c -> p (e c)"), 0.0, ALU.mult, ALU.add))
                    then(dve.tensor_tensor(pos[:], incl[:], flag[:], ALU.subtract))
                    then(dve.tensor_tensor(pos[:], pos[:], pre[:], ALU.add))
                dve.wait_ge(pre_ok, 1)
                place()
                then(dve.tensor_tensor(flag[:], pos[:], wide(need[:]), ALU.is_lt))
                then(dve.tensor_tensor(flag[:], flag[:], eq[:], ALU.mult))
                then(dve.tensor_tensor(sel[:], sel[:], flag[:], ALU.add))
                dve.sem_inc(pre_in, 1)
                dve.wait_ge(pre_ok, 2)
                place()
                then(dve.scalar_tensor_tensor(out=pos[:], in0=pos[:], scalar=1.0, in1=sel[:], op0=ALU.add, op1=ALU.mult))
                then(dve.tensor_scalar(posi[:], pos[:], -1.0, None, ALU.add))
                then(dve.tensor_scalar(lo_i[:], posi[:], P - 1, None, ALU.bitwise_and))
                then(dve.tensor_scalar(hi_i[:], posi[:], 7, None, ALU.arith_shift_right))
                then(dve.tensor_copy(lo_f[:], lo_i[:]))
                then(dve.tensor_copy(hi_f[:], hi_i[:]))
                KE = 5
                with dve.Fori(0, E0) as e:
                    def chain(ins, k):
                        ins.then_inc(stepe, 1)
                        dve.wait_ge(stepe, e * KE + k)
                    W = CAP // P
                    dve.wait_ge(lp_ok, e)
                    dve.tensor_tensor(hot_lo[:], lo_f[:, e, :].unsqueeze(2).to_broadcast([P, NT, P]),
                                      g.iota_f[:].unsqueeze(1).to_broadcast([P, NT, P]), ALU.is_equal).then_inc(stepe, 1)
                    chain(dve.tensor_tensor(hot_hi[:], hi_f[:, e, :].unsqueeze(2).to_broadcast([P, NT, W]),
                                            g.iota_f[:, 0:W].unsqueeze(1).to_broadcast([P, NT, W]), ALU.is_equal), 2)
                    chain(dve.tensor_scalar(val[:, 0, :, :], hot_hi[:], g.part_f[:, 0:1], None, ALU.mult), 3)
                    dve.tensor_tensor(val[:, 1, :, :], hot_hi[:], colf[:].unsqueeze(2).to_broadcast([P, NT, W]),
                                      ALU.mult).then_inc(hot_ok, 1)
                    dve.wait_ge(lp_ok, e + 1)
                    chain(dve.tensor_copy(lst[:], lp[:, 0, :]), 4)
                    chain(dve.scalar_tensor_tensor(out=g.elist[:, e, :], in0=lp[:, 1, :], scalar=float(P), in1=lst[:],
                                                   op0=ALU.mult, op1=ALU.add), 5)


def as_float(t):
    return t[:].bitcast(F32)


def shared_ffn(nc, g):
    G = 512
    NG = T // G
    with ExitStack() as ctx:
        sb = lambda n, s, d=F32: ctx.enter_context(nc.sbuf_tensor(n, s, d))
        w1, w2 = sb("s_w1", [P, DC, HID]), sb("s_w2", [P, HC, D])
        b1, b2_row = sb("s_b1", [P, HC]), sb("s_b2_row", [P, D])
        xT = [sb(f"s_xT{u}", [P, DC, G]) for u in range(2)]
        x1 = [sb(f"s_x1_{u}", [P, 4, D]) for u in range(2)]
        hT = sb("s_hT", [P, HC, G])
        y = [sb(f"s_y{u}", [P, 4, D]) for u in range(2)]
        hp = [ctx.enter_context(nc.psum_tensor(f"s_hp{i}", [P, G], F32)) for i in range(4)]
        yp = [ctx.enter_context(nc.psum_tensor(f"s_yp{i}", [P, 2, D], F32)) for i in range(2)]
        w_in = g.sem("s_w_in")
        in_ = [g.sem(f"s_in{u}") for u in range(2)]
        hp_ok, h_ok, yp_ok, y_ok, xb_ok = (g.sem("s_" + n) for n in ("hp", "h", "yp", "y", "xb"))
        out = [g.sem(f"s_out{u}") for u in range(2)]
        xT_g = g.xnT1.rearrange("v p c (u t) -> v u p c t", u=2)
        rows = lambda t: t.rearrange("(v u c p) d -> v u p c d", u=2, c=4, p=P)
        with nc.allow_non_contiguous_dma(reason="bias columns"), nc.Block() as block:
            @block.sync
            def _(sp):
                sp.dma_start(w1[:], split_load_w(g.Ws1)).then_inc(w_in, 16)
                sp.dma_start(w2[:], split_load_w(g.Ws2)).then_inc(w_in, 16)
                sp.dma_start(b1[:], g.bs1.rearrange("(c p) -> p c", p=P)).then_inc(w_in, 16)
                sp.dma_start(b2_row[:], g.bs2.rearrange("(a n) -> a n", a=1).to_broadcast([P, D])).then_inc(w_in, 16)
                with sp.Fori(0, NG // 2) as v:
                    for u in range(2):
                        sp.wait_ge(y_ok, v * 4)
                        sp.dma_start(xT[u][:], xT_g[v, u]).then_inc(in_[u], 16)
                        sp.dma_start(x1[u][:], rows(g.x1)[v, u]).then_inc(in_[u], 16)

            @block.gpsimd
            def _(pool):
                pool.wait_ge(w_in, 64)
                with pool.Fori(0, NG // 2) as v:
                    for u in range(2):
                        pool.wait_ge(in_[u], v * 32 + 32)
                        for c in range(4):
                            last = pool.tensor_tensor(x1[u][:, c, :], x1[u][:, c, :], b2_row[:], ALU.add)
                        last.then_inc(xb_ok, 1)

            @block.tensor
            def _(pe):
                pe.wait_ge(w_in, 64)
                with pe.Fori(0, NG // 2) as v:
                    for u in range(2):
                        i = v * 2 + u
                        pe.wait_ge(in_[u], v * 32 + 32)
                        for j in range(HC):
                            pe.wait_ge(h_ok, i * HC + max(j - 3, 0))
                            for k in range(DC):
                                last = pe.matmul(hp[j % 4][:], w1[:, k, P * j:P * j + P], xT[u][:, k, :],
                                                 start=(k == 0), stop=(k == DC - 1))
                            last.then_inc(hp_ok, 1)
                        pe.wait_ge(y_ok, i * 2)
                        for a in range(2):
                            for c in range(2):
                                for k in range(HC):
                                    if a == 0 and c == 0:
                                        pe.wait_ge(h_ok, i * HC + k + 1)
                                    t0 = P * (2 * a + c)
                                    last = pe.matmul(yp[a][:, c, :], hT[:, k, t0:t0 + P], w2[:, k, :],
                                                     start=(k == 0), stop=(k == HC - 1))
                            last.then_inc(yp_ok, 1)

            @block.scalar
            def _(act):
                act.wait_ge(w_in, 64)
                with act.Fori(0, NG // 2) as v:
                    for u in range(2):
                        i = v * 2 + u
                        act.wait_ge(yp_ok, i * 2)
                        for j in range(HC):
                            act.wait_ge(hp_ok, i * HC + j + 1)
                            act.activation(hT[:, j, :], hp[j % 4][:], ACT.Gelu_apprx_tanh,
                                           bias=b1[:, j:j + 1]).then_inc(h_ok, 1)
                        act.wait_ge(y_ok, i * 2 + 2)
                        act.dma_start(rows(g.x2)[v, u], y[u][:]).then_inc(out[u], 16)
                for u in range(2):
                    act.wait_ge(out[u], 16 * (NG // 2))

            @block.vector
            def _(dve):
                with dve.Fori(0, NG // 2) as v:
                    for u in range(2):
                        i = v * 2 + u
                        dve.wait_ge(xb_ok, i + 1)
                        dve.wait_ge(out[u], v * 16)
                        for a in range(2):
                            dve.wait_ge(yp_ok, i * 2 + a + 1)
                            dve.tensor_tensor(y[u][:, 2 * a:2 * a + 2, :], yp[a][:], x1[u][:, 2 * a:2 * a + 2, :],
                                              ALU.add).then_inc(y_ok, 1)


def expert_ffn(nc, g):
    G = 512
    GE = CAP // G
    NG = E0 * GE
    with ExitStack() as ctx:
        sb = lambda n, s, d=F32: ctx.enter_context(nc.sbuf_tensor(n, s, d))
        w1 = [sb(f"g_w1_{u}", [P, DC, HID]) for u in range(2)]
        w2 = [sb(f"g_w2_{u}", [P, HC, D]) for u in range(2)]
        b2_row = [sb(f"g_b2_row{u}", [P, D]) for u in range(2)]
        b1_rows = sb("g_b1_rows", [E0 * HC, P])
        b1 = sb("g_b1", [P, E0, HC])
        b1u = [sb(f"g_b1u{u}", [P, HC]) for u in range(2)]
        eidx = [sb(f"g_eidx{u}", [P, CAP // P], I32) for u in range(2)]
        tk = [sb(f"g_tk{i}", [P, 4, ROW]) for i in range(2)]
        pr = [sb(f"g_pr{i}", [P, 4]) for i in range(2)]
        xT = sb("g_xT", [P, DC, G])
        hT = sb("g_hT", [P, HC, G])
        yb = sb("g_yb", [P, 4, D])
        y = [sb(f"g_y{i}", [P, 4, D]) for i in range(2)]
        tp = [ctx.enter_context(nc.psum_tensor(f"g_tp{i}", [P, 4, P], F32)) for i in range(2)]
        hp = [ctx.enter_context(nc.psum_tensor(f"g_hp{i}", [P, G], F32)) for i in range(4)]
        yp = [ctx.enter_context(nc.psum_tensor(f"g_yp{i}", [P, 2, D], F32)) for i in range(2)]
        b_in, b_T, b_ok = g.sem("g_b_in"), g.sem("g_b_T"), g.sem("g_b_ok")
        w_in = [g.sem(f"g_w_in{u}") for u in range(2)]
        tk_in = [g.sem(f"g_tk_in{i}") for i in range(2)]
        (idx_ok, tp_ok, T_ok, hp_ok, h_ok, yp_ok, yb_ok, y_ok, pr_ok, put) = (
            g.sem("g_" + n) for n in ("idx", "tp", "T", "hp", "h", "yp", "yb", "y", "pr", "put"))
        w1_e = g.W1.rearrange("(v u) (c p) n -> v u p c n", u=2, p=P)
        w2_e = g.W2.rearrange("(v u) (c p) n -> v u p c n", u=2, p=P)
        b2_e = g.b2.rearrange("(v u a) n -> v u a n", u=2, a=1)
        STEPS = [(u, q) for u in range(2) for q in range(GE)]
        with nc.Block() as block:
            @block.sync
            def _(sp):
                sp.dma_start(b1_rows[:], g.b1.rearrange("e (j p) -> (e j) p", p=P)).then_inc(b_in, 16)
                with sp.Fori(0, E0 // 2) as v:
                    for u in range(2):
                        sp.wait_ge(yb_ok, v * (2 * GE * 4))
                        sp.dma_start(w1[u][:], w1_e[v, u]).then_inc(w_in[u], 16)
                        sp.dma_start(w2[u][:], w2_e[v, u]).then_inc(w_in[u], 16)
                        sp.dma_start(b2_row[u][:], b2_e[v, u].to_broadcast([P, D])).then_inc(w_in[u], 16)

            @block.gpsimd
            def _(pool):
                with pool.Fori(0, E0 // 2) as v:
                    for s in range(len(STEPS) + 1):
                        if s < len(STEPS):
                            u, q = STEPS[s]
                            gi = v * (2 * GE) + s
                            pool.wait_ge(idx_ok, v * 2 + u + 1)
                            wait_alone(pool, g, pr_ok, v * (2 * GE) + max(s - 1, 0))
                            for c in range(4):
                                pool.indirect_dma_start(
                                    out=tk[s % 2][:, c, :], out_offset=None, in_=g.tab,
                                    in_offset=bass.IndirectOffsetOnAxis(ap=eidx[u][:, 4 * q + c:4 * q + c + 1],
                                                                        axis=0)).then_inc(tk_in[s % 2], 16)
                        if s >= 1:
                            u, q = STEPS[s - 1]
                            gi = v * (2 * GE) + s - 1
                            wait_alone(pool, g, y_ok, gi * 4 + 4)
                            wait_alone(pool, g, put, gi * 64)
                            for c in range(4):
                                pool.indirect_dma_start(
                                    out=g.x2, in_=y[(s - 1) % 2][:, c, :], in_offset=None, compute_op=ALU.add,
                                    out_offset=bass.IndirectOffsetOnAxis(ap=eidx[u][:, 4 * q + c:4 * q + c + 1],
                                                                         axis=0)).then_inc(put, 16)
                pool.wait_ge(put, NG * 64)

            @block.tensor
            def _(pe):
                pe.wait_ge(b_in, 16)
                pe.transpose(tp[0][:, 0, 0:E0 * HC], b1_rows[:], g.ident[0:E0 * HC, 0:E0 * HC]).then_inc(b_T, 1)
                pe.wait_ge(b_ok, 1)
                with pe.Fori(0, E0 // 2) as v:
                    for s, (u, q) in enumerate(STEPS):
                        gi = v * (2 * GE) + s
                        pe.wait_ge(tk_in[s % 2], v * (64 * GE) + 64 * (s // 2 + 1))
                        pe.wait_ge(T_ok, gi * 2)
                        for k in range(DC):
                            for a in range(4):
                                last = pe.transpose(tp[k][:, a, :], tk[s % 2][:, a, P * k:P * k + P], g.ident[:])
                            last.then_inc(tp_ok, 1)
                        pe.wait_ge(T_ok, gi * 2 + 2)
                        pe.wait_ge(w_in[u], v * 48 + 48)
                        for j in range(HC):
                            pe.wait_ge(h_ok, gi * HC + max(j - 3, 0))
                            for k in range(DC):
                                last = pe.matmul(hp[j % 4][:], w1[u][:, k, P * j:P * j + P], xT[:, k, :],
                                                 start=(k == 0), stop=(k == DC - 1))
                            last.then_inc(hp_ok, 1)
                        pe.wait_ge(yb_ok, gi * 4)
                        for a in range(2):
                            for c in range(2):
                                for k in range(HC):
                                    if a == 0 and c == 0:
                                        pe.wait_ge(h_ok, gi * HC + k + 1)
                                    t0 = P * (2 * a + c)
                                    last = pe.matmul(yp[a][:, c, :], hT[:, k, t0:t0 + P], w2[u][:, k, :],
                                                     start=(k == 0), stop=(k == HC - 1))
                            last.then_inc(yp_ok, 1)

            @block.scalar
            def _(act):
                act.wait_ge(b_T, 1)
                act.copy(b1[:].rearrange("p e j -> p (e j)"), tp[0][:, 0, 0:E0 * HC]).then_inc(b_ok, 1)
                with act.Fori(0, E0 // 2) as v:
                    for s, (u, q) in enumerate(STEPS):
                        gi = v * (2 * GE) + s
                        act.wait_ge(idx_ok, v * 2 + u + 1)
                        act.wait_ge(yp_ok, gi * 2)
                        for j in range(HC):
                            act.wait_ge(hp_ok, gi * HC + j + 1)
                            act.activation(hT[:, j, :], hp[j % 4][:], ACT.Gelu_apprx_tanh,
                                           bias=b1u[u][:, j:j + 1]).then_inc(h_ok, 1)

            @block.vector
            def _(dve):
                dve.wait_ge(b_ok, 1)
                with dve.Fori(0, E0 // 2) as v:
                    for u in range(2):
                        e = v * 2 + u
                        dve.wait_ge(put, v * (2 * GE * 64))
                        dve.tensor_copy(eidx[u][:], g.elist[:, e, :])
                        dve.tensor_copy(b1u[u][:], b1[:, e, :]).then_inc(idx_ok, 1)
                    for s, (u, q) in enumerate(STEPS):
                        gi = v * (2 * GE) + s
                        for k in range(DC):
                            dve.wait_ge(tp_ok, gi * 2 + k + 1)
                            dve.tensor_copy(xT[:, k, :], tp[k][:].rearrange("p a b -> p (a b)")).then_inc(T_ok, 1)
                        dve.tensor_copy(pr[s % 2][:], tk[s % 2][:, :, D:ROW].rearrange("p c (v u) -> p v u c", u=2)[:, v, u, :]
                                        ).then_inc(pr_ok, 1)
                        dve.wait_ge(pr_ok, gi + 1)
                        for a in range(2):
                            dve.wait_ge(yp_ok, gi * 2 + a + 1)
                            dve.tensor_tensor(yb[:, 2 * a:2 * a + 2, :], yp[a][:],
                                              b2_row[u][:].unsqueeze(1).to_broadcast([P, 2, D]), ALU.add).then_inc(yb_ok, 2)
                        dve.wait_ge(yb_ok, gi * 4 + 4)
                        dve.wait_ge(put, v * (2 * GE * 64) + 64 * max(s - 1, 0))
                        for c in range(4):
                            dve.tensor_scalar(y[s % 2][:, c, :], yb[:, c, :], pr[s % 2][:, c:c + 1], None,
                                              ALU.mult).then_inc(y_ok, 1)


def causal_attention(nc, g):
    SCALE = 1.0 / 16.0
    with ExitStack() as ctx:
        sb = lambda n, s, d=F32: ctx.enter_context(nc.sbuf_tensor(n, s, d))
        w_rows = sb("h_w_rows", [P, 3, DC, D])
        wT = sb("h_wT", [P, 3, DC, D])
        b_col, bv_row = sb("h_b_col", [P, 2, DC]), sb("h_bv_row", [P, D])
        above = sb("h_above", [P, P])
        zero = sb("h_zero", [P, P])
        x2 = [sb(f"h_x2_{u}", [P, ST, D]) for u in range(2)]
        xn, xnT = sb("h_xn", [P, ST, D]), sb("h_xnT", [P, DC, S])
        st, mv = sb("h_st", [P, ST, 6]), sb("h_mv", [P, ST, 2])
        var, std, rstd, tmp = (sb("h_" + n, [P, ST]) for n in ("var", "std", "rstd", "tmp"))
        qT, kT, v_ = sb("h_qT", [P, DC, S]), sb("h_kT", [P, DC, S]), sb("h_v", [P, ST, D])
        mx, nmx, rs, rinv = (sb("h_" + n, [P, ST]) for n in ("mx", "nmx", "rs", "rinv"))
        pm = [sb(f"h_pm{i}", [P, S]) for i in range(2)]
        pT = sb("h_pT", [P, ST, P])
        x3 = sb("h_x3", [P, ST, D])
        sc = [ctx.enter_context(nc.psum_tensor(f"h_sc{i}", [P, 2, 512], F32)) for i in range(2)]
        pt = ctx.enter_context(nc.psum_tensor("h_pt", [P, 2, 4, P], F32))
        z = ctx.enter_context(nc.psum_tensor("h_z", [P, 2, 512], F32))
        w_in, wp_ok, wT_ok, zero_ok, above_ok = (g.sem("h_" + n) for n in ("w_in", "wp", "wT", "zero", "above"))
        x_in = [g.sem(f"h_x_in{u}") for u in range(2)]
        (stats, var_ok, std_ok, rstd_ok, xn_ok, tp_ok, T_ok, pj_ok, qk_ok, v_ok, sc_ok, mx_ok, nmx_ok, exp_ok, pt_ok,
         pTa_ok, pTb_ok, z_ok, rinv_ok, x3_ok, out) = (g.sem("h_" + n) for n in (
             "stats", "var", "std", "rstd", "xn", "tp", "T", "pj", "qk", "v", "sc", "mx", "nmx", "exp", "pt",
             "pTa", "pTb", "z", "rinv", "x3", "out"))
        tiles = lambda t: t.rearrange("(v u c p) d -> v u p c d", u=2, c=ST, p=P)
        with nc.allow_non_contiguous_dma(reason="bias columns"), nc.Block() as block:
            @block.sync
            def _(sp):
                for i, w in enumerate((g.Wq1, g.Wk1, g.Wv1)):
                    sp.dma_start(w_rows[:, i, :, :], split_load_w(w)).then_inc(w_in, 16)
                for i, b in enumerate((g.bq1, g.bk1)):
                    sp.dma_start(b_col[:, i, :], b.rearrange("(c p) -> p c", p=P)).then_inc(w_in, 16)
                sp.dma_start(bv_row[:], g.bv1.rearrange("(a n) -> a n", a=1).to_broadcast([P, D])).then_inc(w_in, 16)
                with sp.Fori(0, B // 2) as v:
                    for u in range(2):
                        sp.wait_ge(x3_ok, v * (2 * ST))
                        sp.dma_start(x2[u][:], tiles(g.x2)[v, u]).then_inc(x_in[u], 16)

            @block.gpsimd
            def _(pool):
                pool.memset(zero[:], 0.0).then_inc(zero_ok, 1)
                pool.wait_ge(zero_ok, 1)
                pool.affine_select(out=above[:], in_=zero[:], compare_op=ALU.is_ge, fill=-1.0e30, base=0,
                                   pattern=[[-1, P]], channel_multiplier=1).then_inc(above_ok, 1)

            @block.tensor
            def _(pe):
                pe.wait_ge(w_in, 96)
                for i in range(3):
                    if i:
                        pe.wait_ge(wT_ok, i)
                    for dc in range(DC):
                        for kc in range(DC):
                            last = pe.transpose(pt[:, 0, dc * DC + kc, :], w_rows[:, i, kc, P * dc:P * dc + P], g.ident[:])
                    last.then_inc(wp_ok, 1)
                pe.wait_ge(wT_ok, 3)
                pe.wait_ge(above_ok, 1)
                with pe.Fori(0, B) as b:
                    pe.wait_ge(xn_ok, b + 1)
                    pe.wait_ge(pTb_ok, b * ST)
                    for n in range(4):
                        pe.wait_ge(T_ok, b * 4 + max(n - 1, 0))
                        for a in range(4):
                            last = pe.transpose(pt[:, n % 2, a, :], xn[:, 4 * (n % 2) + a, P * (n // 2):P * (n // 2) + P],
                                                g.ident[:])
                        last.then_inc(tp_ok, 1)
                    pe.wait_ge(T_ok, b * 4 + 4)
                    pe.wait_ge(exp_ok, b * ST)
                    for n in range(12):
                        out_ = sc[n % 4 // 2][:, n % 2, :]
                        if n >= 4:
                            pe.wait_ge(qk_ok, b * 8 + min(n - 3, 8))
                        if n < 8:
                            i, m, t0 = n // 4, n % 4 // 2, 512 * (n % 2)
                            for k in range(DC):
                                last = pe.matmul(out_, wT[:, i, k, P * m:P * m + P], xnT[:, k, t0:t0 + 512],
                                                 start=(k == 0), stop=(k == DC - 1))
                        else:
                            for a in range(2):
                                c = 2 * (n - 8) + a
                                for k in range(DC):
                                    last = pe.matmul(out_[:, D * a:D * a + D], xnT[:, k, P * c:P * c + P], wT[:, 2, k, :],
                                                     start=(k == 0), stop=(k == DC - 1))
                        last.then_inc(pj_ok, 1)
                    pe.wait_ge(v_ok, b * 4 + 4)
                    for i in range(ST + 1):
                        if i >= 1:
                            n = i - 1
                            pe.wait_ge(exp_ok, b * ST + n + 1)
                            pe.wait_ge(pTa_ok, b * ST + n)
                            pe.wait_ge(pTb_ok, b * ST + n)
                            for c in range(n + 1):
                                last = pe.transpose(pt[:, c // 4, c % 4, :], pm[n % 2][:, P * c:P * c + P], g.ident[:])
                            last.then_inc(pt_ok, 1)
                        if i < ST:
                            keys = P * (i + 1)
                            for s in range(0, keys, 512):
                                w = min(512, keys - s)
                                diag = s + w == keys
                                for k in range(DC):
                                    last = pe.matmul(sc[i % 2][:, s // 512, 0:w], qT[:, k, P * i:P * i + P], kT[:, k, s:s + w],
                                                     start=(k == 0), stop=(k == DC - 1 and not diag))
                                if diag:
                                    last = pe.matmul(sc[i % 2][:, s // 512, w - P:w], g.ident[:], above[:],
                                                     start=False, stop=True)
                            last.then_inc(sc_ok, 1)
                        if i >= 1:
                            n = i - 1
                            pe.wait_ge(pTa_ok, b * ST + n + 1)
                            pe.wait_ge(pTb_ok, b * ST + n + 1)
                            pe.wait_ge(x3_ok, b * ST + max(n - 1, 0))
                            for c in range(n + 1):
                                last = pe.matmul(z[:, n % 2, 0:D], pT[:, c, :], v_[:, c, :], start=(c == 0), stop=(c == n))
                            last.then_inc(z_ok, 1)

            @block.scalar
            def _(act):
                act.wait_ge(w_in, 96)
                for i in range(3):
                    act.wait_ge(wp_ok, i + 1)
                    act.copy(wT[:, i, :, :].rearrange("p c n -> p (c n)"), pt[:, 0, :, :].rearrange("p a b -> p (a b)")
                             ).then_inc(wT_ok, 1)
                with act.Fori(0, B) as b:
                    act.wait_ge(var_ok, b + 1)
                    act.activation(std[:], var[:], ACT.Sqrt).then_inc(std_ok, 1)
                    for n in range(4):
                        act.wait_ge(tp_ok, b * 4 + n + 1)
                        act.copy(xnT[:, n // 2, 512 * (n % 2):512 * (n % 2) + 512],
                                 pt[:, n % 2, :, :].rearrange("p a b -> p (a b)")).then_inc(T_ok, 1)
                    for n in range(8):
                        act.wait_ge(pj_ok, b * 12 + n + 1)
                        i, m = n // 4, n % 4 // 2
                        act.activation((qT, kT)[i][:, m, 512 * (n % 2):512 * (n % 2) + 512], sc[n % 4 // 2][:, n % 2, :],
                                       ACT.Identity, bias=b_col[:, i, m:m + 1]).then_inc(qk_ok, 1)
                    for i in range(ST + 1):
                        if i >= 1:
                            n = i - 1
                            act.wait_ge(pt_ok, b * ST + n + 1)
                            act.wait_ge(z_ok, b * ST + n)
                            w = min(4, n + 1)
                            act.copy(pT[:, 0:w, :], pt[:, 0, 0:w, :]).then_inc(pTa_ok, 1)
                        if i < ST:
                            keys = P * (i + 1)
                            act.wait_ge(nmx_ok, b * ST + i + 1)
                            act.activation(pm[i % 2][:, 0:keys], sc[i % 2][:].rearrange("p a t -> p (a t)")[:, 0:keys],
                                           ACT.Exp, bias=nmx[:, i:i + 1], scale=SCALE,
                                           accum_out=rs[:, i:i + 1]).then_inc(exp_ok, 1)
                    act.wait_ge(x3_ok, b * ST + ST)
                    act.dma_start(g.x3.rearrange("(b c p) d -> b p c d", c=ST, p=P)[b], x3[:]).then_inc(out, 16)
                act.wait_ge(out, 16 * B)

            @block.vector
            def _(dve):
                with dve.Fori(0, B // 2) as v:
                    for u in range(2):
                        b = v * 2 + u
                        dve.wait_ge(x_in[u], v * 16 + 16)
                        for c in range(ST):
                            dve.bn_stats(st[:, c, :], x2[u][:, c, :]).then_inc(stats, 1)
                        wait_alone(dve, g, stats, b * (2 * ST) + ST)
                        for c in range(ST):
                            dve.bn_aggr(mv[:, c, :], st[:, c, :]).then_inc(stats, 1)
                        dve.wait_ge(stats, b * (2 * ST) + 2 * ST)
                        dve.tensor_scalar(var[:], mv[:, :, 1], EPS, None, ALU.add).then_inc(var_ok, 1)
                        dve.wait_ge(std_ok, b + 1)
                        sharpen_rstd(dve, rstd_ok, b * 4, rstd, std, var, tmp)
                        for c in range(ST):
                            last = dve.tensor_scalar(xn[:, c, :], x2[u][:, c, :], mv[:, c, 0:1], rstd[:, c:c + 1],
                                                     ALU.subtract, ALU.mult)
                        last.then_inc(xn_ok, 1)
                        for n in range(4):
                            dve.wait_ge(pj_ok, b * 12 + n + 9)
                            dve.tensor_tensor(v_[:, 2 * n:2 * n + 2, :], sc[n // 2][:, n % 2, :].rearrange("p (a d) -> p a d", a=2),
                                              bv_row[:].unsqueeze(1).to_broadcast([P, 2, D]), ALU.add).then_inc(v_ok, 1)
                        for i in range(ST + 1):
                            n = i - 1
                            if n >= 4:
                                dve.wait_ge(pt_ok, b * ST + n + 1)
                                dve.wait_ge(z_ok, b * ST + n)
                                dve.tensor_copy(pT[:, 4:n + 1, :], pt[:, 1, 0:n - 3, :]).then_inc(pTb_ok, 1)
                            elif n >= 0:
                                dve.wait_ge(exp_ok, b * ST + n + 1)
                                dve.sem_inc(pTb_ok, 1)
                            if i < ST:
                                keys = P * (i + 1)
                                dve.wait_ge(sc_ok, b * ST + i + 1)
                                dve.tensor_reduce(mx[:, i:i + 1], sc[i % 2][:].rearrange("p a t -> p (a t)")[:, 0:keys],
                                                  AX.X, ALU.max).then_inc(mx_ok, 1)
                                dve.wait_ge(mx_ok, b * ST + i + 1)
                                dve.tensor_scalar(nmx[:, i:i + 1], mx[:, i:i + 1], -SCALE, None, ALU.mult).then_inc(nmx_ok, 1)
                            if i >= 1:
                                dve.reciprocal(rinv[:, n:n + 1], rs[:, n:n + 1]).then_inc(rinv_ok, 1)
                                dve.wait_ge(rinv_ok, b * ST + n + 1)
                                dve.wait_ge(z_ok, b * ST + n + 1)
                                if n == 0:
                                    dve.wait_ge(out, b * 16)
                                dve.scalar_tensor_tensor(out=x3[:, n, :], in0=z[:, n % 2, 0:D], scalar=rinv[:, n:n + 1],
                                                         in1=x2[u][:, n, :], op0=ALU.mult, op1=ALU.add).then_inc(x3_ok, 1)


E1 = 64
K2 = 2
MLP = 512
TILES = T * K2 // P + E1
QUAD = 4
DUMMY = K2 * T


def gate_top2(nc, g):
    with ExitStack() as ctx:
        sb = lambda n, s, d=F32: ctx.enter_context(nc.sbuf_tensor(n, s, d))
        gate = sb("i_gate", [P, DC, E1])
        x3 = [sb(f"i_x3_{u}", [P, ST, D]) for u in range(2)]
        xn, xnT = sb("i_xn", [P, ST, D]), sb("i_xnT", [P, DC, S])
        st, mv = sb("i_st", [P, ST, 6]), sb("i_mv", [P, ST, 2])
        var, std, rstd, tmp = (sb("i_" + n, [P, ST]) for n in ("var", "std", "rstd", "tmp"))
        lg = sb("i_lg", [P, ST, E1])
        top, at, atf = sb("i_top", [P, ST, 8]), sb("i_at", [P, ST, 8], U32), sb("i_atf", [P, ST, 8])
        dif, ex, ex1 = (sb("i_" + n, [P, ST]) for n in ("dif", "ex", "ex1"))
        w_ = sb("i_w", [P, 2, ST])
        hot = sb("i_hot", [P, K2, ST, E1])
        sel = sb("i_sel", [P, ST, E1])
        run = sb("i_run", [P, ST + 1, E1])
        rk, rkh = sb("i_rk", [P, ST, E1]), sb("i_rkh", [P, K2, ST, E1])
        tp = [ctx.enter_context(nc.psum_tensor(f"i_tp{i}", [P, 4, P], F32)) for i in range(2)]
        gp = ctx.enter_context(nc.psum_tensor("i_gp", [P, ST, E1], F32))
        rp = ctx.enter_context(nc.psum_tensor("i_rp", [P, ST, E1], F32))
        cp = ctx.enter_context(nc.psum_tensor("i_cp", [P, E1], F32))
        w_in, zero_ok = g.sem("i_w_in"), g.sem("i_zero")
        x_in = [g.sem(f"i_x_in{u}") for u in range(2)]
        (stats, var_ok, std_ok, rstd_ok, xn_ok, tp_ok, T_ok, gp_ok, step, ex_ok, sel_ok, rp_ok, out, fin) = (
            g.sem("i_" + n) for n in ("stats", "var", "std", "rstd", "xn", "tp", "T", "gp", "step", "ex", "sel", "rp",
                                      "out", "fin"))
        K = 18 + ST + 16
        tiles = lambda t: t.rearrange("(v u c p) d -> v u p c d", u=2, c=ST, p=P)
        with nc.Block() as block:
            @block.sync
            def _(sp):
                sp.dma_start(gate[:], split_load_w(g.gate1)).then_inc(w_in, 16)
                with sp.Fori(0, B // 2) as v:
                    for u in range(2):
                        sp.wait_ge(xn_ok, v * 2)
                        sp.dma_start(x3[u][:], tiles(g.x3)[v, u]).then_inc(x_in[u], 16)

            @block.gpsimd
            def _(pool):
                pool.memset(run[:, 0, :], 0.0).then_inc(zero_ok, 1)

            @block.tensor
            def _(pe):
                pe.wait_ge(w_in, 16)
                with pe.Fori(0, B) as b:
                    pe.wait_ge(xn_ok, b + 1)
                    for n in range(4):
                        pe.wait_ge(T_ok, b * 4 + max(n - 1, 0))
                        for a in range(4):
                            last = pe.transpose(tp[n % 2][:, a, :], xn[:, 4 * (n % 2) + a, P * (n // 2):P * (n // 2) + P],
                                                g.ident[:])
                        last.then_inc(tp_ok, 1)
                    pe.wait_ge(T_ok, b * 4 + 4)
                    pe.wait_ge(sel_ok, b)
                    for c in range(ST):
                        for k in range(DC):
                            last = pe.matmul(gp[:, c, :], xnT[:, k, P * c:P * c + P], gate[:, k, :],
                                             start=(k == 0), stop=(k == DC - 1))
                    last.then_inc(gp_ok, 1)
                    pe.wait_ge(sel_ok, b + 1)
                    for c in range(ST):
                        pe.matmul(rp[:, c, :], g.tri[:], sel[:, c, :], start=True, stop=False)
                        last = pe.matmul(rp[:, c, :], g.ones[:], run[:, c, :], start=False, stop=True)
                    last.then_inc(rp_ok, 1)
                pe.wait_ge(fin, 1)
                pe.matmul(cp[:], g.ones[:], run[:, 0, :], start=True, stop=True).then_inc(fin, 1)

            @block.scalar
            def _(act):
                with act.Fori(0, B) as b:
                    act.wait_ge(var_ok, b + 1)
                    act.activation(std[:], var[:], ACT.Sqrt).then_inc(std_ok, 1)
                    act.wait_ge(xn_ok, b + 1)
                    act.dma_start(g.xn3.rearrange("(b c p) d -> b p c d", c=ST, p=P)[b], xn[:]).then_inc(out, 16)
                    for n in range(4):
                        act.wait_ge(tp_ok, b * 4 + n + 1)
                        act.copy(xnT[:, n // 2, 512 * (n % 2):512 * (n % 2) + 512],
                                 tp[n % 2][:].rearrange("p a b -> p (a b)")).then_inc(T_ok, 1)
                    act.wait_ge(ex_ok, b * 2 + 1)
                    act.activation(ex[:], dif[:], ACT.Exp).then_inc(ex_ok, 1)
                    act.wait_ge(out, b * 16 + 16)

            @block.vector
            def _(dve):
                dve.wait_ge(zero_ok, 1)
                with dve.Fori(0, B // 2) as v:
                    for u in range(2):
                        b = v * 2 + u
                        n = 0

                        def then(ins, alone=False):
                            nonlocal n
                            n += 1
                            ins.then_inc(step, 1)
                            if alone:
                                wait_alone(dve, g, step, b * K + n)
                            else:
                                dve.wait_ge(step, b * K + n)
                        dve.wait_ge(x_in[u], v * 16 + 16)
                        for c in range(ST):
                            dve.bn_stats(st[:, c, :], x3[u][:, c, :]).then_inc(stats, 1)
                        wait_alone(dve, g, stats, b * (2 * ST) + ST)
                        for c in range(ST):
                            dve.bn_aggr(mv[:, c, :], st[:, c, :]).then_inc(stats, 1)
                        dve.wait_ge(stats, b * (2 * ST) + 2 * ST)
                        dve.tensor_scalar(var[:], mv[:, :, 1], EPS, None, ALU.add).then_inc(var_ok, 1)
                        dve.wait_ge(std_ok, b + 1)
                        sharpen_rstd(dve, rstd_ok, b * 4, rstd, std, var, tmp)
                        dve.wait_ge(out, b * 16)
                        for c in range(ST):
                            last = dve.tensor_scalar(xn[:, c, :], x3[u][:, c, :], mv[:, c, 0:1], rstd[:, c:c + 1],
                                                     ALU.subtract, ALU.mult)
                        last.then_inc(xn_ok, 1)
                        dve.wait_ge(gp_ok, b + 1)
                        then(dve.tensor_copy(lg[:], gp[:]), True)
                        for c in range(ST):
                            last = dve.max(top[:, c, :], lg[:, c, :])
                        then(last, True)
                        for c in range(ST):
                            last = dve.max_index(at[:, c, :], top[:, c, :], lg[:, c, :])
                        then(last)
                        then(dve.tensor_copy(atf[:], at[:]))
                        dve.wait_ge(ex_ok, b * 2)
                        dve.tensor_tensor(dif[:], top[:, :, 1], top[:, :, 0], ALU.subtract).then_inc(ex_ok, 1)
                        dve.wait_ge(rp_ok, b)
                        for k in range(K2):
                            then(dve.tensor_tensor(hot[:, k, :, :], atf[:, :, k].unsqueeze(2).to_broadcast([P, ST, E1]),
                                                   g.iota_f[:, 0:E1].unsqueeze(1).to_broadcast([P, ST, E1]), ALU.is_equal))
                        then(dve.tensor_tensor(sel[:], hot[:, 0, :, :], hot[:, 1, :, :], ALU.add))
                        for c in range(ST):
                            then(dve.tensor_tensor(run[:, c + 1, :], run[:, c, :], sel[:, c, :], ALU.add))
                        dve.sem_inc(sel_ok, 1)
                        dve.wait_ge(ex_ok, b * 2 + 2)
                        then(dve.tensor_scalar(ex1[:], ex[:], 1.0, None, ALU.add))
                        then(dve.reciprocal(w_[:, 0, :], ex1[:]))
                        then(dve.tensor_tensor(w_[:, 1, :], ex[:], w_[:, 0, :], ALU.mult))
                        dve.wait_ge(rp_ok, b + 1)
                        then(dve.tensor_copy(run[:, 0, :], run[:, ST, :]))
                        for k in range(K2):
                            then(dve.tensor_tensor(rkh[:, k, :, :], hot[:, k, :, :], rp[:], ALU.mult))
                            then(dve.tensor_copy(tiled(g.at_f, k, b), atf[:, :, k]))
                            then(dve.tensor_reduce(tiled(g.rank, k, b), rkh[:, k, :, :], AX.X, ALU.add))
                            then(dve.tensor_copy(tiled(g.w_tok, k, b), w_[:, k, :]))
                        assert n <= K
                        if n < K:
                            dve.sem_inc(step, K - n)
                dve.sem_inc(fin, 1)
                dve.wait_ge(fin, 2)
                dve.tensor_copy(g.count[:], cp[:]).then_inc(fin, 1)


def tiled(t, k, b):
    return t.rearrange("p k (b c) -> p k b c", b=B)[:, k, b, :]


def place_rows(nc, g):
    with ExitStack() as ctx:
        sb = lambda n, s, d=F32: ctx.enter_context(nc.sbuf_tensor(n, s, d))
        ci, ti = sb("j_ci", [P, E1], I32), sb("j_ti", [P, E1], I32)
        tf, one, end, beg = (sb("j_" + n, [P, E1]) for n in ("tf", "one", "end", "beg"))
        hit = sb("j_hit", [P, NT, E1])
        rowf = sb("j_rowf", [P, K2, NT])
        row = sb("j_row", [P, K2, NT], I32)
        tok = sb("j_tok", [P, K2, NT], I32)
        tile_f, te_f, cmp_ = sb("j_tile_f", [P, 2]), sb("j_te_f", [P, 2]), sb("j_cmp", [P, 2, E1])
        tile_i, te_i = sb("j_tile_i", [P, 2], I32), sb("j_te_i", [P, 2, 2], I32)
        end_i, quads = sb("j_end_i", [P, E1], I32), sb("j_quads", [P, 1], I32)
        dummy = sb("j_dummy", [TILES // 2, 2, P], I32)
        step, made, cleared, tabled, put = (g.sem("j_" + n) for n in ("step", "made", "cleared", "tabled", "put"))
        with nc.allow_non_contiguous_dma(reason="two short tables"), nc.Block() as block:
            @block.gpsimd
            def _(pool):
                pool.memset(dummy[:], DUMMY).then_inc(made, 1)
                pool.iota(tok[:], pattern=[[T, K2], [P, NT]], base=0, channel_multiplier=1).then_inc(made, 1)
                pool.iota(tile_i[:], pattern=[[P, 2]], base=0, channel_multiplier=1).then_inc(made, 1)
                pool.wait_ge(made, 3)
                pool.wait_ge(cleared, 16)
                pool.wait_ge(step, 6)
                for k in range(K2):
                    for c in range(NT):
                        pool.indirect_dma_start(
                            out=g.row_of, in_=tok[:, k, c:c + 1], in_offset=None,
                            out_offset=bass.IndirectOffsetOnAxis(ap=row[:, k, c:c + 1], axis=0)).then_inc(put, 16)
                pool.wait_ge(put, 16 * K2 * NT)

            @block.sync
            def _(sp):
                sp.wait_ge(made, 1)
                sp.dma_start(g.row_of.rearrange("(q a p) o -> q a (p o)", a=2, p=P), dummy[:]).then_inc(cleared, 16)
                sp.wait_ge(step, 14)
                sp.dma_start(g.tile_expert[:, 0:P, 0].rearrange("s p -> p s"), te_i[:, 0, :]).then_inc(tabled, 16)
                sp.dma_start(g.tile_expert[:, P:TILES, 0].rearrange("s p -> p s"), te_i[0:TILES - P, 1, :]).then_inc(tabled, 16)
                sp.dma_start(g.tile_end, end_i[0:1, :]).then_inc(tabled, 16)
                sp.dma_start(g.quads, quads[0:1, :]).then_inc(tabled, 16)
                sp.wait_ge(tabled, 64)
                sp.wait_ge(cleared, 16)

            @block.vector
            def _(dve):
                n = 0

                def then(ins):
                    nonlocal n
                    n += 1
                    ins.then_inc(step, 1)
                    dve.wait_ge(step, n)
                dve.memset(one[:], 1.0)
                then(dve.tensor_scalar(ci[:], g.count[:], float(P - 1), None, ALU.add))
                then(dve.tensor_scalar(ti[:], ci[:], 7, None, ALU.logical_shift_right))
                then(dve.tensor_copy(tf[:], ti[:]))
                then(dve.tensor_tensor_scan(end[:], one[:], tf[:], 0.0, ALU.mult, ALU.add))
                then(dve.tensor_tensor(beg[:], end[:], tf[:], ALU.subtract))
                for k in range(K2):
                    dve.tensor_tensor(hit[:], g.at_f[:, k, :].unsqueeze(2).to_broadcast([P, NT, E1]),
                                      g.iota_f[:, 0:E1].unsqueeze(1).to_broadcast([P, NT, E1]), ALU.is_equal).then_inc(g.hit_step, 1)
                    dve.wait_ge(g.hit_step, 3 * k + 1)
                    dve.tensor_tensor(hit[:], hit[:], beg[:].unsqueeze(1).to_broadcast([P, NT, E1]), ALU.mult).then_inc(g.hit_step, 1)
                    dve.wait_ge(g.hit_step, 3 * k + 2)
                    dve.tensor_reduce(rowf[:, k, :], hit[:], AX.X, ALU.add).then_inc(g.hit_step, 1)
                    dve.wait_ge(g.hit_step, 3 * k + 3)
                then(dve.scalar_tensor_tensor(out=row[:], in0=rowf[:], scalar=float(P), in1=g.rank, op0=ALU.mult, op1=ALU.add))
                dve.wait_ge(made, 3)
                then(dve.tensor_copy(tile_f[:], tile_i[:]))
                then(dve.tensor_tensor(cmp_[:], tile_f[:].unsqueeze(2).to_broadcast([P, 2, E1]),
                                       end[:].unsqueeze(1).to_broadcast([P, 2, E1]), ALU.is_ge))
                then(dve.tensor_reduce(te_f[:], cmp_[:], AX.X, ALU.add))
                then(dve.tensor_scalar(te_i[:, :, 0], te_f[:], float(E1 - 1), None, ALU.min))
                then(dve.tensor_scalar(te_i[:, :, 1], te_i[:, :, 0], QUAD - 1, None, ALU.bitwise_and))
                then(dve.tensor_copy(end_i[:], end[:]))
                then(dve.tensor_scalar(ci[:, 0:1], end[:, E1 - 1:E1], -1.0, None, ALU.add))
                then(dve.tensor_scalar(quads[:], ci[:, 0:1], 2, None, ALU.logical_shift_right))


def expert_rows(nc, g):
    MC = MLP // P
    R = QUAD
    with ExitStack() as ctx:
        g.ctx = ctx
        sb = lambda n, s, d=F32: ctx.enter_context(nc.sbuf_tensor(n, s, d))
        te = sb("k_te", [1, 2, TILES], I32)
        end = sb("k_end", [1, E1], I32)
        nq = sb("k_nq", [1, 1], I32)
        ids = sb("k_ids", [TILES // R, R, P], I32)
        idf = sb("k_idf", [TILES // R, R, P])
        dst = sb("k_dst", [P, TILES // R, R], I32)
        src = sb("k_src", [P, TILES // R, R], I32)
        di = [sb(f"k_di{u}", [P, 1], I32) for u in range(R)]
        si = [sb(f"k_si{u}", [P, 1], I32) for u in range(R)]
        w01 = sb("k_w01", [P, R, 2, DC, MLP])
        wo = sb("k_wo", [P, R, MC, D])
        xg = [sb(f"k_xg{u}", [P, D]) for u in range(R)]
        xT = [sb(f"k_xT{u}", [P, DC, P]) for u in range(2)]
        sl = sb("k_sl", [P, MLP])
        it = [sb(f"k_it{u}", [P, MLP]) for u in range(2)]
        iT = sb("k_iT", [P, MC, P])
        y = [sb(f"k_y{u}", [P, D]) for u in range(R)]
        xp = ctx.enter_context(nc.psum_tensor("k_xp", [P, 4, P], F32))
        h = [ctx.enter_context(nc.psum_tensor(f"k_h{u}", [P, 2, MLP], F32)) for u in range(2)]
        ip = ctx.enter_context(nc.psum_tensor("k_ip", [P, MC, P], F32))
        yp = [ctx.enter_context(nc.psum_tensor(f"k_yp{u}", [P, D], F32)) for u in range(2)]
        t_in, ids_f, id_ps, ids_ok = (g.sem("k_" + n) for n in ("t_in", "ids_f", "id_ps", "ids_ok"))
        w_in = g.sem("k_w_in")
        x_in = [g.sem(f"k_x_in{u}") for u in range(R)]
        put = [g.sem(f"k_put{u}") for u in range(R)]
        si_ok, di_ok, xp_ok, xT_ok, h_ok, sl_ok, it_ok, ip_ok, iT_ok, yp_ok, y_ok = (
            g.sem("k_" + n) for n in ("si", "di", "xp", "xT", "h", "sl", "it", "ip", "iT", "yp", "y"))
        W_DMAS = 3 * 16
        NTAB = 16 * 5

        def last_quad(eng):
            eng.wait_ge(t_in, NTAB)
            return eng.value_load(nq[0:1, 0:1], min_val=T * K2 // P // R - 1, max_val=TILES // R - 1)

        with nc.Block() as block:
            @block.sync
            def _(sp):
                sp.dma_start(te[:, 0, :], g.tile_expert[0].rearrange("t a -> a t")).then_inc(t_in, 16)
                sp.dma_start(te[:, 1, :], g.tile_expert[1].rearrange("t a -> a t")).then_inc(t_in, 16)
                sp.dma_start(end[:], g.tile_end).then_inc(t_in, 16)
                sp.dma_start(nq[:], g.quads).then_inc(t_in, 16)
                sp.dma_start(ids[:], g.row_of.rearrange("(q a p) o -> q a (p o)", a=R, p=P)).then_inc(t_in, 16)
                w0_e = g.w0.rearrange("(v u) (c p) n -> v u p c n", u=R, p=P)
                w1_e = g.w1.rearrange("(v u) (c p) n -> v u p c n", u=R, p=P)
                wo_e = g.wo.rearrange("(v u) (c p) n -> v u p c n", u=R, p=P)

                def load(v, u):
                    sp.dma_start(w01[:, u, 0, :, :], w0_e[v, u]).then_inc(w_in, 16)
                    sp.dma_start(w01[:, u, 1, :, :], w1_e[v, u]).then_inc(w_in, 16)
                    sp.dma_start(wo[:, u, :, :], wo_e[v, u]).then_inc(w_in, 16)
                for u in range(R):
                    if u:
                        sp.wait_ge(w_in, W_DMAS * u)
                    load(0, u)
                sp.wait_ge(t_in, NTAB)
                ends = end[:].rearrange("a (v u) -> a v u", u=R)
                with sp.Fori(1, E1 // R) as v:
                    for u in range(R):
                        last = sp.value_load(ends[:, v - 1, u:u + 1], min_val=0, max_val=TILES)
                        sp.wait_ge(yp_ok, last)
                        sp.wait_ge(w_in, (v * R + u) * W_DMAS)
                        load(v, u)
                sp.wait_ge(w_in, E1 * W_DMAS)

            @block.gpsimd
            def _(pool):
                def gather(q, u):
                    if isinstance(q, int):
                        pool.wait_ge(ids_ok, 2)
                    else:
                        wait_alone(pool, g, xp_ok, q * R + u - 3)
                    pool.tensor_copy(si[u][:], src[:, q, u:u + 1]).then_inc(si_ok, 1)
                    wait_alone(pool, g, si_ok, q * R + u + 1)
                    pool.indirect_dma_start(
                        out=xg[u][:], out_offset=None, in_=g.xn3,
                        in_offset=bass.IndirectOffsetOnAxis(ap=si[u][:], axis=0)).then_inc(x_in[u], 16)

                def store(q, u):
                    wait_alone(pool, g, put[u], q * 16)
                    pool.tensor_copy(di[u][:], dst[:, q, u:u + 1]).then_inc(di_ok, 1)
                    wait_alone(pool, g, di_ok, q * R + u + 1)
                    wait_alone(pool, g, y_ok, q * R + u + 1)
                    put_rows(pool, g, y[u], di[u], put[u])
                m = last_quad(pool)
                for u in range(R):
                    gather(0, u)
                with pool.Fori(1, m + 1) as q:
                    for u in range(R):
                        store(q - 1, u)
                        gather(q, u)
                for u in range(R):
                    store(m, u)
                for u in range(R):
                    wait_alone(pool, g, put[u], m * 16 + 16)

            @block.tensor
            def _(pe):
                pe.wait_ge(ids_f, 1)
                for a in range(R):
                    last = pe.transpose(xp[:, a, 0:TILES // R], idf[:, a, :], g.ident[0:TILES // R, 0:TILES // R])
                last.then_inc(id_ps, 1)
                pe.wait_ge(ids_ok, 2)
                m = last_quad(pe)

                def x_by_column(q, u):
                    pe.wait_ge(x_in[u], q * 16 + 16)
                    pe.wait_ge(xT_ok, q * R + u)
                    for k in range(DC):
                        last = pe.transpose(xp[:, k, :], xg[u][:, P * k:P * k + P], g.ident[:])
                    last.then_inc(xp_ok, 1)

                def last_product(i, q, u, place):
                    pe.wait_ge(iT_ok, i - 1)
                    pe.wait_ge(y_ok, max(i - 3, 0) if isinstance(i, int) else i - 3)
                    for k in range(MC):
                        last = pe.matmul(yp[u % 2][:], iT[:, k, :], wo[:, place, k, :], start=(k == 0), stop=(k == MC - 1))
                    last.then_inc(yp_ok, 1)

                def product_by_column(i, u):
                    pe.wait_ge(it_ok, i)
                    for k in range(MC):
                        last = pe.transpose(ip[:, k, :], it[u % 2][:, P * k:P * k + P], g.ident[:])
                    last.then_inc(ip_ok, 1)

                def first_products(q, u, e, place):
                    i = q * R + u
                    pe.wait_ge(xT_ok, i + 1)
                    pe.wait_ge(w_in, e * W_DMAS + W_DMAS)
                    for m in range(2):
                        for k in range(DC):
                            last = pe.matmul(h[u % 2][:, m, :], xT[u % 2][:, k, :], w01[:, place, m, k, :],
                                             start=(k == 0), stop=(k == DC - 1))
                    last.then_inc(h_ok, 1)

                def expert_of(q, u):
                    at = te[:].rearrange("o s (q u) -> o s q u", u=R)
                    return (pe.value_load(at[:, 0, q, u:u + 1], min_val=0, max_val=E1 - 1),
                            pe.value_load(at[:, 1, q, u:u + 1], min_val=0, max_val=R - 1))

                def place_before(q, u, back):
                    at = te[:].rearrange("o s (q u) -> o s q u", u=R)
                    q, u = (q, u - back) if u >= back else (q - 1, u - back + R)
                    return pe.value_load(at[:, 1, q, u:u + 1], min_val=0, max_val=R - 1)

                def tile(q, u, first=False):
                    e, place = expert_of(q, u)
                    if not first or u >= 2:
                        before = place_before(q, u, 2)
                    x_by_column(q, u)
                    if not first or u >= 2:
                        last_product(q * R + u, q, u, before)
                    if not first or u >= 1:
                        product_by_column(q * R + u, u + 1)
                    first_products(q, u, e, place)
                for u in range(R):
                    tile(0, u, True)
                with pe.Fori(1, m + 1) as q:
                    for u in range(R):
                        tile(q, u)
                last_product(m * R + R, m, 0, place_before(m, R, 2))
                product_by_column(m * R + R, 1)
                last_product(m * R + R + 1, m, 1, place_before(m, R + 1, 2))

            @block.scalar
            def _(act):
                m = last_quad(act)

                def by_column(i):
                    act.wait_ge(ip_ok, i)
                    act.copy(iT[:].rearrange("p a b -> p (a b)"), ip[:].rearrange("p a b -> p (a b)")).then_inc(iT_ok, 1)

                def tile(q, u, first=False):
                    i = q * R + u
                    if not first or u >= 1:
                        by_column(i)
                    act.wait_ge(h_ok, i + 1)
                    act.wait_ge(it_ok, i)
                    act.activation(sl[:], h[u % 2][:, 0, :], ACT.Silu).then_inc(sl_ok, 1)
                for u in range(R):
                    tile(0, u, True)
                with act.Fori(1, m + 1) as q:
                    for u in range(R):
                        tile(q, u)
                by_column(m * R + R)

            @block.vector
            def _(dve):
                dve.wait_ge(t_in, NTAB)
                dve.tensor_copy(idf[:], ids[:]).then_inc(ids_f, 1)
                dve.wait_ge(id_ps, 1)
                dve.tensor_copy(dst[:].rearrange("p q a -> p a q"), xp[:, :, 0:TILES // R]).then_inc(ids_ok, 1)
                dve.wait_ge(ids_ok, 1)
                dve.tensor_scalar(src[:], dst[:], T - 1, None, ALU.bitwise_and).then_inc(ids_ok, 1)
                dve.wait_ge(ids_ok, 2)
                m = last_quad(dve)

                def y_out(q, u):
                    dve.wait_ge(yp_ok, q * R + u + 1)
                    dve.wait_ge(put[u], q * 16)
                    dve.tensor_copy(y[u][:], yp[u % 2][:]).then_inc(y_ok, 1)

                def tile(q, u, first=False):
                    i = q * R + u
                    dve.wait_ge(xp_ok, i + 1)
                    dve.tensor_copy(xT[u % 2][:], xp[:, 0:DC, :]).then_inc(xT_ok, 1)
                    if not first or u >= 2:
                        y_out(*((q, u - 2) if u >= 2 else (q - 1, u + R - 2)))
                    dve.wait_ge(sl_ok, i + 1)
                    dve.tensor_tensor(it[u % 2][:], h[u % 2][:, 1, :], sl[:], ALU.mult).then_inc(it_ok, 1)
                for u in range(R):
                    tile(0, u, True)
                with dve.Fori(1, m + 1) as q:
                    for u in range(R):
                        tile(q, u)
                y_out(m, R - 2)
                y_out(m, R - 1)


def put_rows(pool, g, y, di, put):
    pool.indirect_dma_start(out=g.y_tok, in_=y[:], in_offset=None,
                            out_offset=bass.IndirectOffsetOnAxis(ap=di[:], axis=0),
                            bounds_check=K2 * T - 1, oob_is_err=False).then_inc(put, 16)


def combine(nc, g):
    with ExitStack() as ctx:
        sb = lambda n, s, d=F32: ctx.enter_context(nc.sbuf_tensor(n, s, d))
        x = [sb(f"l_x{u}", [P, ST, D]) for u in range(2)]
        ya = [sb(f"l_ya{u}", [P, ST, D]) for u in range(2)]
        yb = [sb(f"l_yb{u}", [P, ST, D]) for u in range(2)]
        wt = sb("l_wt", [P, K2, NT])
        in_ = [g.sem(f"l_in{u}") for u in range(2)]
        out = [g.sem(f"l_out{u}") for u in range(2)]
        one, two, wts = g.sem("l_one"), g.sem("l_two"), g.sem("l_wts")
        tiles = lambda t: t.rearrange("(v u c p) d -> v u p c d", u=2, c=ST, p=P)
        w_b = [sb(f"l_w{u}", [P, K2, ST]) for u in range(2)]
        with nc.Block() as block:
            @block.sync
            def _(sp):
                with sp.Fori(0, B // 2) as v:
                    for u in range(2):
                        sp.wait_ge(out[u], v * 16)
                        sp.dma_start(x[u][:], tiles(g.x3)[v, u]).then_inc(in_[u], 16)
                        sp.dma_start(ya[u][:], tiles(g.y_tok[0:T, :])[v, u]).then_inc(in_[u], 16)
                        sp.dma_start(yb[u][:], tiles(g.y_tok[T:2 * T, :])[v, u]).then_inc(in_[u], 16)

            @block.scalar
            def _(act):
                with act.Fori(0, B // 2) as v:
                    for u in range(2):
                        act.wait_ge(two, v * 2 + u + 1)
                        act.dma_start(tiles(g.out)[v, u], x[u][:]).then_inc(out[u], 16)
                for u in range(2):
                    act.wait_ge(out[u], 16 * (B // 2))

            @block.vector
            def _(dve):
                with dve.Fori(0, B // 2) as v:
                    for u in range(2):
                        b = v * 2 + u
                        dve.wait_ge(in_[u], v * 48 + 48)
                        for k in range(K2):
                            last = dve.tensor_copy(w_b[u][:, k, :], tiled(g.w_tok, k, b))
                        last.then_inc(wts, 1)
                        dve.wait_ge(wts, b + 1)
                        for c in range(ST):
                            last = dve.scalar_tensor_tensor(out=x[u][:, c, :], in0=ya[u][:, c, :], scalar=w_b[u][:, 0, c:c + 1],
                                                            in1=x[u][:, c, :], op0=ALU.mult, op1=ALU.add)
                        last.then_inc(one, 1)
                        dve.wait_ge(one, b + 1)
                        for c in range(ST):
                            last = dve.scalar_tensor_tensor(out=x[u][:, c, :], in0=yb[u][:, c, :], scalar=w_b[u][:, 1, c:c + 1],
                                                            in1=x[u][:, c, :], op0=ALU.mult, op1=ALU.add)
                        last.then_inc(two, 1)


def two_layers(nc, ins, out):
    with ExitStack() as ctx:
        def sb(name, shape, dt=F32):
            return ctx.enter_context(nc.sbuf_tensor(name, shape, dt))

        def dram(name, shape, dt=F32):
            return nc.dram_tensor(name, shape, dt, kind="Internal").ap()

        g = Shared()
        sems = []

        def sem(name):
            sems.append(nc.alloc_semaphore(name=name))
            return sems[-1]

        g.sem = sem
        g.passed = sem("passed")
        g.x, g.Wq, g.bq, g.Wk, g.bk, g.Wv, g.bv, g.Wo, g.bo, g.sample_idx = (
            ins["L0_attn_" + n] for n in ("x", "Wq", "bq", "Wk", "bk", "Wv", "bv", "Wo", "bo", "sample_idx"))
        g.gate, g.W1, g.b1, g.W2, g.b2, g.Ws1, g.bs1, g.Ws2, g.bs2 = (
            ins["L0_ffn_" + n] for n in ("gate", "W1", "b1", "W2", "b2", "Ws1", "bs1", "Ws2", "bs2"))
        g.Wq1, g.bq1, g.Wk1, g.bk1, g.Wv1, g.bv1 = (ins["L1_attn_" + n] for n in ("Wq", "bq", "Wk", "bk", "Wv", "bv"))
        g.gate1, g.w0, g.w1, g.wo = (ins["L1_ffn_" + n] for n in ("gate_kernel", "w0", "w1", "wo"))
        g.out = out.rearrange("b s d -> (b s) d")

        g.ident, g.ones, g.tri = sb("ident", [P, P]), sb("ones", [P, P]), sb("tri", [P, P])
        g.iota_i, g.iota_f = sb("iota_i", [P, P], I32), sb("iota_f", [P, P])
        g.part_i, g.part_f = sb("part_i", [P, 1], I32), sb("part_f", [P, 1])
        g.probs = sb("probs", [P, E0, NT])[:]
        g.elist = sb("elist", [P, E0, CAP // P], I32)
        g.at_f, g.rank, g.w_tok = (sb(n, [P, K2, NT])[:] for n in ("at_f", "rank", "w_tok"))
        g.count = sb("count", [P, E1])

        g.xnT = dram("xnT", (B, P, DC, S))
        g.q_rows = dram("q_rows", (T * H, HD))
        g.q16, g.k16 = dram("q16", (B, 2, D, S), F16), dram("k16", (B, 2, D, U), F16)
        g.m_rows, g.sel_rows = dram("m_rows", (P, S)), dram("sel_rows", (P * TOP, 1), I32)
        g.attn_rows = dram("attn_rows", (T * H, HD))
        g.x1, g.x2, g.x3 = (dram(n, (T, D)) for n in ("x1", "x2", "x3"))
        g.tab, g.xnT1 = dram("tab", (T, ROW)), dram("xnT1", (B, P, DC, S))
        g.xn3, g.y_tok = dram("xn3", (T, D)), dram("y_tok", (K2 * T, D))
        g.row_of, g.tile_expert = dram("row_of", (TILES * P, 1), I32), dram("tile_expert", (2, TILES, 1), I32)
        g.tile_end, g.quads = dram("tile_end", (1, E1), I32), dram("quads", (1, 1), I32)

        constants(nc, g)
        project_samples(nc, g)
        score_samples(nc, g)
        pick_queries(nc, g)
        attend_selected(nc, g)
        add_attention_and_gate(nc, g)
        choose_tokens(nc, g)
        shared_ffn(nc, g)
        expert_ffn(nc, g)
        nc.clear_and_free_semaphores(sems)
        nc.all_engine_barrier()
        g.passed, g.hit_step = sem("passed1"), sem("hit_step")
        causal_attention(nc, g)
        gate_top2(nc, g)
        place_rows(nc, g)
        expert_rows(nc, g)
        combine(nc, g)


_INS = (["L0_attn_" + n for n in ("x", "Wq", "bq", "Wk", "bk", "Wv", "bv", "Wo", "bo", "sample_idx")]
        + ["L0_ffn_" + n for n in ("gate", "W1", "b1", "W2", "b2", "Ws1", "bs1", "Ws2", "bs2")]
        + ["L1_attn_" + n for n in ("Wq", "bq", "Wk", "bk", "Wv", "bv")]
        + ["L1_ffn_" + n for n in ("gate_kernel", "w0", "w1", "wo")])
_OUT = ((8, 1024, 256), "float32")


def kernel(**inputs):
    import numpy as _np
    import concourse.bacc as _bacc
    from concourse import mybir as _mybir
    from concourse.bass_utils import run_bass_kernel_spmd as _run

    nc = _bacc.Bacc("TRN2", target_bir_lowering=False, num_devices=1)
    arrays, args = {}, {}
    for name in _INS:
        a = _np.ascontiguousarray(inputs[name])
        arrays[f"in_{name}_dram"] = a
        args[name] = nc.dram_tensor(f"in_{name}_dram", a.shape, _mybir.dt.from_np(a.dtype), kind="ExternalInput").ap()
    shape, dtype = _OUT
    out = nc.dram_tensor("out_0_dram", shape, _mybir.dt.from_np(_np.dtype(dtype)), kind="ExternalOutput").ap()
    two_layers(nc, args, out)
    r = _run(nc, [arrays], core_ids=[0])
    return r.results[0]["out_0_dram"]
```

```python
import concourse.bass as bass
from concourse import mybir
from contextlib import ExitStack

F32 = mybir.dt.float32
F16 = mybir.dt.float16
I32 = mybir.dt.int32
U32 = mybir.dt.uint32
ALU = mybir.AluOpType
ACT = mybir.ActivationFunctionType
AX = mybir.AxisListType


class Shared:
    pass


P = 128
B = 8
S = 1024
D = 256
DC = D // P
ST = S // P
T = B * S
NT = T // P
H = 16
HD = D // H
U = 512
UT = U // P
TOP = 34
EPS = 1e-5
QK = 16.0


def wait_alone(eng, g, sem, value):
    eng.wait_ge(sem, value)
    eng.sem_inc(g.passed, 1)


def load_ahead(eng, pairs, used, per, load):
    for u in range(2):
        load(0, u)
    with eng.Fori(1, pairs) as v:
        for u in range(2):
            eng.wait_ge(used, v * (2 * per) - (1 - u) * per)
            load(v, u)


def split_load_w(w):
    return w.rearrange("(c p) n -> p c n", p=P)


def sharpen_rstd(dve, sem, done, rstd, std, var, tmp):
    dve.reciprocal(rstd[:], std[:]).then_inc(sem, 1)
    dve.wait_ge(sem, done + 1)
    dve.tensor_tensor(tmp[:], rstd[:], rstd[:], ALU.mult).then_inc(sem, 1)
    dve.wait_ge(sem, done + 2)
    dve.scalar_tensor_tensor(out=tmp[:], in0=tmp[:], scalar=-0.5, in1=var[:], op0=ALU.mult, op1=ALU.mult).then_inc(sem, 1)
    dve.wait_ge(sem, done + 3)
    dve.scalar_tensor_tensor(out=rstd[:], in0=tmp[:], scalar=1.5, in1=rstd[:], op0=ALU.add, op1=ALU.mult).then_inc(sem, 1)
    dve.wait_ge(sem, done + 4)


def constants(nc, g):
    made = g.sem("const_made")
    filled = g.sem("const_filled")
    with nc.Block() as block:
        @block.gpsimd
        def _(pool):
            pool.memset(g.ones[:], 1.0).then_inc(filled, 1)
            pool.memset(g.ident[:], 0.0).then_inc(filled, 1)
            pool.wait_ge(filled, 2)
            pool.affine_select(out=g.ident[:], in_=g.ident[:], compare_op=ALU.not_equal, fill=1.0, base=0,
                               pattern=[[-1, P]], channel_multiplier=1).then_inc(made, 1)
            pool.affine_select(out=g.tri[:], in_=g.ones[:], compare_op=ALU.is_gt, fill=0.0, base=0,
                               pattern=[[1, P]], channel_multiplier=-1).then_inc(made, 1)
            pool.iota(g.iota_i[:], pattern=[[1, P]], base=0, channel_multiplier=0).then_inc(made, 1)
            pool.iota(g.part_i[:], pattern=[[0, 1]], base=0, channel_multiplier=1).then_inc(made, 1)

        @block.vector
        def _(dve):
            dve.wait_ge(made, 4)
            dve.tensor_copy(g.iota_f[:], g.iota_i[:])
            dve.tensor_copy(g.part_f[:], g.part_i[:])


def project_and_score(nc, g):
    NX = ST + UT
    K3 = 3 * HD
    PARTS = ((0, 0), (0, 1), (1, 0))
    HG = 2
    NG = ST * H // HG
    with ExitStack() as ctx:
        sb = lambda n, s, d=F32: ctx.enter_context(nc.sbuf_tensor(n, s, d))
        wq = sb("a_wq", [P, DC, D])
        wk = sb("a_wk", [P, DC, D])
        bqk = sb("a_bqk", [P, 2, DC])
        bqk_s = sb("a_bqk_s", [P, 2, DC])
        idx = sb("a_idx", [P, UT], I32)
        xt = [sb(f"a_xt{u}", [P, NX, D]) for u in range(2)]
        xn = sb("a_xn", [P, NX, D])
        st = sb("a_st", [P, NX, 6])
        mv = sb("a_mv", [P, NX, 2])
        var = sb("a_var", [P, NX])
        std = sb("a_std", [P, NX])
        rstd = sb("a_rstd", [P, NX])
        tmp = sb("a_tmp", [P, NX])
        xnT = sb("a_xnT", [P, DC, NX * P])
        q32 = sb("a_q32", [P, DC, S])
        q16 = [sb(f"a_q16_{i}", [P, DC, S], F16) for i in range(2)]
        k32 = sb("a_k32", [P, DC, U])
        kc = sb("a_kc", [P, DC, U])
        k16 = [sb(f"a_k16_{i}", [P, DC, U], F16) for i in range(2)]
        ksum = sb("a_ksum", [P, DC])
        kmean = sb("a_kmean", [P, DC])
        qrow = sb("a_qrow", [P, ST, D])
        qs = [sb(f"b_qs{u}", [K3, H, S], F16) for u in range(2)]
        ks = [sb(f"b_ks{u}", [K3, H, U], F16) for u in range(2)]
        m = [sb(f"b_m{u}", [P, ST, H]) for u in range(2)]
        mT = sb("b_mT", [H, S])
        tp = [ctx.enter_context(nc.psum_tensor(f"a_tp{i}", [P, 4, P], F32)) for i in range(2)]
        pj = [ctx.enter_context(nc.psum_tensor(f"a_pj{i}", [P, 512], F32)) for i in range(2)]
        sc = [ctx.enter_context(nc.psum_tensor(f"b_sc{i}", [P, HG, U], F32)) for i in range(2)]
        w_in, idx_in, idx_next = g.sem("a_w_in"), g.sem("a_idx_in"), g.sem("a_idx_next")
        x_in = [g.sem(f"a_x_in{u}") for u in range(2)]
        rows_in = g.sem("a_rows_in")
        bias_ok = g.sem("a_bias_ok")
        stats, var_ok, std_ok, rstd_ok, xn_ok = (g.sem("a_" + n) for n in ("stats", "var", "std", "rstd", "xn"))
        tp_ok, T_ok, pj_ok, q_ok, k_ok = (g.sem("a_" + n) for n in ("tp", "T", "pj", "q", "k"))
        lo_ok, stored = g.sem("a_lo"), g.sem("a_stored")
        s_in = [g.sem(f"b_in{u}") for u in range(2)]
        sc_ok, m_ok, mtp_ok, mT_ok, mT_out = (g.sem("b_" + n) for n in ("sc", "m", "mtp", "mT", "mT_out"))
        NS = 6
        x_b = g.x.rearrange("(v u) (c p) d -> v u p c d", u=2, p=P)
        x_rows = g.x.rearrange("b s d -> (b s) d")
        q_rows_b = g.q_rows.rearrange("(b c p h) e -> b p c (h e)", b=B, p=P, h=H)
        qv = g.q16.rearrange("b i (h e) t -> b i e h t", e=HD)
        kv = g.k16.rearrange("b i (h e) t -> b i e h t", e=HD)
        PE_AT = [23 + i for i in range(6)] + [30 + i for i in range(12)] + [43 + i for i in range(4)]
        M_AT = (1, 2)

        def steps(one):
            one(0, None, 0, None)
            one(1, 0, 1, 0)
            return lambda v: (one(v * 2 + 2, v * 2 + 1, 0, 1), one(v * 2 + 3, v * 2 + 2, 1, 0))
        with nc.allow_non_contiguous_dma(reason="bias columns, 256 words"), nc.Block() as block:
            @block.sync
            def _(sp):
                sp.dma_start(wq[:], split_load_w(g.Wq)).then_inc(w_in, 16)
                sp.dma_start(wk[:], split_load_w(g.Wk)).then_inc(w_in, 16)
                sp.dma_start(bqk[:, 0, :], g.bq.rearrange("(c p) -> p c", p=P)).then_inc(w_in, 16)
                sp.dma_start(bqk[:, 1, :], g.bk.rearrange("(c p) -> p c", p=P)).then_inc(w_in, 16)
                sp.dma_start(idx[:], g.sample_idx.rearrange("(c p) -> p c", p=P)).then_inc(idx_in, 16)
                with sp.Fori(0, B // 2) as v:
                    for u in range(2):
                        sp.wait_ge(xn_ok, v * 2)
                        sp.dma_start(xt[u][:, 0:ST, :], x_b[v, u]).then_inc(x_in[u], 16)

            @block.gpsimd
            def _(pool):
                pool.wait_ge(idx_in, 16)
                with pool.Fori(0, B // 2) as v:
                    for u in range(2):
                        a = v * 2 + u
                        wait_alone(pool, g, xn_ok, v * 2)
                        for c in range(UT):
                            pool.indirect_dma_start(
                                out=xt[u][:, ST + c, :], out_offset=None, in_=x_rows,
                                in_offset=bass.IndirectOffsetOnAxis(ap=idx[:, c:c + 1], axis=0)).then_inc(rows_in, 16)
                        wait_alone(pool, g, rows_in, a * (16 * UT) + 16 * UT)
                        pool.tensor_scalar(idx[:], idx[:], float(S), None, ALU.add).then_inc(idx_next, 1)
                        wait_alone(pool, g, idx_next, a + 1)
                        pool.wait_ge(stored, a * (16 * NS))
                        for n in range(2):
                            pool.wait_ge(q_ok, a * 8 + 4 * n + 4)
                            pool.tensor_tensor(q16[1][:, n, :], q32[:, n, :], q16[0][:, n, :], ALU.subtract).then_inc(lo_ok, 1)
                        pool.wait_ge(k_ok, a * 7 + 7)
                        pool.tensor_tensor(k16[1][:], kc[:], k16[0][:], ALU.subtract).then_inc(lo_ok, 1)

            @block.tensor
            def _(pe):
                def piece(p, a):
                    if p < 6:
                        if p == 0:
                            pe.wait_ge(xn_ok, a + 1)
                        pe.wait_ge(T_ok, a * 10 + max(p - 1, 0))
                        for j in range(4):
                            last = pe.transpose(tp[p % 2][:, j, :], xn[:, 4 * (p % 3) + j, P * (p // 3):P * (p // 3) + P],
                                                g.ident[:])
                        last.then_inc(tp_ok, 1)
                    elif p < 18:
                        n, k = (p - 6) // 2, (p - 6) % 2
                        w, mm = (wq, n // 2) if n < 4 else (wk, n - 4)
                        t0 = 512 * (n % 2) if n < 4 else S
                        if p == 6:
                            pe.wait_ge(T_ok, a * 10 + 6)
                            pe.wait_ge(k_ok, a * 7)
                        if k == 0 and n >= 1:
                            pe.wait_ge(q_ok, a * 8 + 2 * min(n - 1, 4))
                            if n == 1:
                                pe.wait_ge(k_ok, a * 7)
                        last = pe.matmul(pj[n % 2][:], w[:, k, P * mm:P * mm + P], xnT[:, k, t0:t0 + 512],
                                         start=(k == 0), stop=(k == DC - 1))
                        if k == DC - 1:
                            last.then_inc(pj_ok, 1)
                    else:
                        n = p - 18
                        pe.wait_ge(q_ok, a * 8 + 8)
                        pe.wait_ge(T_ok, a * 10 + 5 + n)
                        for j in range(4):
                            c, k = 2 * n + j // 2, j % 2
                            last = pe.transpose(tp[n % 2][:, j, :], q32[:, k, P * c:P * c + P], g.ident[:])
                        last.then_inc(tp_ok, 1)

                def turn(n, b, ub):
                    if n == 0:
                        pe.wait_ge(m_ok, b * NG + NG)
                    pe.wait_ge(mT_ok, b * 2 + n)
                    for c in range(4):
                        last = pe.transpose(tp[n][0:H, c, :], m[ub][:, 4 * n + c, :], g.ident[:])
                    last.then_inc(mtp_ok, 1)

                def one(a, b, ua, ub):
                    if b is None:
                        for p in range(len(PE_AT)):
                            piece(p, a)
                        return
                    for t in range(NG):
                        c, h0 = t * HG // H, t * HG % H
                        if t == 0:
                            pe.wait_ge(s_in[ub], 96 * ((b - ub) // 2 + 1) if isinstance(b, int) else loads_of(b, ub))
                        pe.wait_ge(m_ok, b * NG + max(t - 1, 0))
                        for j in range(HG):
                            last = pe.matmul(sc[t % 2][:, j, :], qs[ub][:, h0 + j, P * c:P * c + P],
                                             ks[ub][:, h0 + j, :], start=True, stop=True)
                        last.then_inc(sc_ok, 1)
                        if t in M_AT and not (isinstance(b, int) and b == 0):
                            if t == M_AT[0]:
                                pe.wait_ge(T_ok, b * 10 + 10)
                            turn(M_AT.index(t), b - 1, 1 - ub)
                        if t == PE_AT[0] and a is not None and not (isinstance(b, int) and b == 0):
                            pe.wait_ge(mT_ok, b * 2)
                        for p in range(len(PE_AT)):
                            if PE_AT[p] == t and a is not None:
                                piece(p, a)
                pe.wait_ge(w_in, 64)
                loop = steps(one)
                with pe.Fori(0, B // 2 - 1) as v:
                    loads_of = lambda b, ub: v * 96 + (96 if ub else 192)
                    loop(v)
                one(None, B - 1, None, 1)
                turn(0, B - 1, 1)
                turn(1, B - 1, 1)

            @block.scalar
            def _(act):
                def turned(b):
                    act.wait_ge(mT_out, b * 16)
                    for n in range(2):
                        act.wait_ge(mtp_ok, b * 2 + n + 1)
                        act.copy(mT[:, 512 * n:512 * n + 512], tp[n][0:H, :, :].rearrange("p a b -> p (a b)")
                                 ).then_inc(mT_ok, 1)
                    act.wait_ge(mT_ok, b * 2 + 2)
                    act.dma_start(g.m_rows.rearrange("(b h) t -> b h t", b=B)[b], mT[:]).then_inc(mT_out, 16)

                def one(a, b, ua, ub):
                    if b is not None and not (isinstance(b, int) and b == 0):
                        turned(b - 1)
                    act.wait_ge(var_ok, a + 1)
                    act.activation(std[:], var[:], ACT.Sqrt).then_inc(std_ok, 1)
                    for n in range(6):
                        act.wait_ge(tp_ok, a * 10 + n + 1)
                        act.copy(xnT[:, n // 3, 512 * (n % 3):512 * (n % 3) + 512],
                                 tp[n % 2][:].rearrange("p a b -> p (a b)")).then_inc(T_ok, 1)
                    act.wait_ge(T_ok, a * 10 + 6)
                    act.dma_start(g.xnT[a], xnT[:, :, 0:S]).then_inc(stored, 16)
                    act.wait_ge(lo_ok, a * 3)
                    for n in range(4):
                        act.wait_ge(pj_ok, a * 6 + n + 1)
                        for dst in (q32, q16[0]):
                            act.activation(dst[:, n // 2, 512 * (n % 2):512 * (n % 2) + 512], pj[n % 2][:], ACT.Identity,
                                           bias=bqk_s[:, 0, n // 2:n // 2 + 1], scale=QK).then_inc(q_ok, 1)
                    for n in range(4, 6):
                        act.wait_ge(pj_ok, a * 6 + n + 1)
                        act.activation(k32[:, n - 4, :], pj[n % 2][:], ACT.Identity,
                                       bias=bqk_s[:, 1, n - 4:n - 3], scale=QK,
                                       accum_out=ksum[:, n - 4:n - 3]).then_inc(k_ok, 1)
                    act.wait_ge(k_ok, a * 7 + 2)
                    act.mul(kmean[:], ksum[:], -1.0 / U).then_inc(k_ok, 1)
                    act.wait_ge(k_ok, a * 7 + 3)
                    for dst in (kc, k16[0]):
                        for n in range(DC):
                            act.activation(dst[:, n, :], k32[:, n, :], ACT.Identity, bias=kmean[:, n:n + 1]).then_inc(k_ok, 1)
                    for n in range(4):
                        act.wait_ge(tp_ok, a * 10 + n + 7)
                        act.mul(qrow[:, 2 * n:2 * n + 2, :].rearrange("p c d -> p (c d)"),
                                tp[n % 2][:].rearrange("p a b -> p (a b)"), 1.0 / QK).then_inc(T_ok, 1)
                    act.wait_ge(T_ok, a * 10 + 10)
                    act.dma_start(q_rows_b[a], qrow[:]).then_inc(stored, 16)
                    act.wait_ge(q_ok, a * 8 + 8)
                    act.wait_ge(k_ok, a * 7 + 7)
                    act.wait_ge(lo_ok, a * 3 + 3)
                    for i in range(2):
                        act.dma_start(g.q16[a, i].rearrange("(c p) t -> p c t", p=P), q16[i][:]).then_inc(stored, 16)
                        act.dma_start(g.k16[a, i].rearrange("(c p) t -> p c t", p=P), k16[i][:]).then_inc(stored, 16)
                    act.wait_ge(stored, a * (16 * NS) + 16 * NS)
                    if b is not None:
                        act.wait_ge(sc_ok, b * NG)
                    for r, (iq, ik) in enumerate(PARTS):
                        act.dma_start(qs[ua][HD * r:HD * r + HD, :, :], qv[a, iq]).then_inc(s_in[ua], 16)
                        act.dma_start(ks[ua][HD * r:HD * r + HD, :, :], kv[a, ik]).then_inc(s_in[ua], 16)
                act.wait_ge(bias_ok, 1)
                loop = steps(one)
                with act.Fori(0, B // 2 - 1) as v:
                    loop(v)
                turned(B - 2)
                turned(B - 1)
                act.wait_ge(mT_out, 16 * B)

            @block.vector
            def _(dve):
                def piece(p, a, ua):
                    if p < NX:
                        if p == 0:
                            dve.wait_ge(x_in[ua], 16 * (a // 2 + 1) if isinstance(a, int) else x_loads(ua))
                            dve.wait_ge(rows_in, a * (16 * UT) + 16 * UT)
                        dve.bn_stats(st[:, p, :], xt[ua][:, p, :]).then_inc(stats, 1)
                    elif p == NX:
                        wait_alone(dve, g, stats, a * (2 * NX) + NX)
                        for c in range(NX):
                            dve.bn_aggr(mv[:, c, :], st[:, c, :]).then_inc(stats, 1)
                    elif p == NX + 1:
                        dve.wait_ge(stats, a * (2 * NX) + 2 * NX)
                        dve.tensor_scalar(var[:], mv[:, :, 1], EPS, None, ALU.add).then_inc(var_ok, 1)
                    elif p == NX + 3:
                        dve.wait_ge(std_ok, a + 1)
                        sharpen_rstd(dve, rstd_ok, a * 4, rstd, std, var, tmp)
                        dve.wait_ge(tp_ok, a * 10)
                    elif NX + 4 <= p < NX + 4 + NX // 2:
                        for c in (2 * (p - NX - 4), 2 * (p - NX - 4) + 1):
                            last = dve.tensor_scalar(xn[:, c, :], xt[ua][:, c, :], mv[:, c, 0:1], rstd[:, c:c + 1],
                                                     ALU.subtract, ALU.mult)
                        if c == NX - 1:
                            last.then_inc(xn_ok, 1)

                def one(a, b, ua, ub):
                    if b is None:
                        for p in range(NX + 4 + NX // 2):
                            piece(p, a, ua)
                        return
                    if not (isinstance(b, int) and b < 2):
                        dve.wait_ge(mtp_ok, b * 2 - 2)
                    for t in range(NG):
                        c, h0 = t * HG // H, t * HG % H
                        dve.wait_ge(sc_ok, b * NG + t + 1)
                        dve.tensor_reduce(m[ub][:, c, h0:h0 + HG], sc[t % 2][:], AX.X, ALU.max).then_inc(m_ok, 1)
                        if a is not None:
                            piece(t, a, ua)
                dve.wait_ge(w_in, 64)
                dve.tensor_scalar(bqk_s[:], bqk[:], QK, None, ALU.mult).then_inc(bias_ok, 1)
                loop = steps(one)
                with dve.Fori(0, B // 2 - 1) as v:
                    x_loads = lambda ua: v * 16 + 32
                    loop(v)
                one(None, B - 1, None, 1)


def pick_queries(nc, g):
    RND = -(-TOP // 8)
    with ExitStack() as ctx:
        sb = lambda n, s, d=F32: ctx.enter_context(nc.sbuf_tensor(n, s, d))
        m = [sb(f"c_m{i}", [P, S]) for i in range(2)]
        top = sb("c_top", [P, RND, 8])
        at = sb("c_at", [P, RND, 8], U32)
        atf = sb("c_atf", [P, RND * 8])
        base = sb("c_base", [P, 1], I32)
        basf = sb("c_basf", [P, 1])
        lowi = sb("c_lowi", [P, 1], I32)
        lowf = sb("c_lowf", [P, 1])
        rows = sb("c_rows", [P, RND * 8], I32)
        m_in, step, out = g.sem("c_in"), g.sem("c_step"), g.sem("c_out")
        with nc.Block() as block:
            @block.sync
            def _(sp):
                sp.dma_start(m[0][:], g.m_rows).then_inc(m_in, 16)
                sp.wait_ge(step, 3 * RND + 5)
                sp.dma_start(g.sel_rows.rearrange("(r j) a -> r (j a)", j=TOP), rows[:, 0:TOP]).then_inc(out, 16)
                sp.wait_ge(out, 16)

            @block.vector
            def _(dve):
                n = 0
                dve.wait_ge(m_in, 16)

                def then(ins):
                    nonlocal n
                    n += 1
                    ins.then_inc(step, 1)
                    dve.wait_ge(step, n)
                for r in range(RND):
                    then(dve.max(top[:, r, :], m[r % 2][:]))
                    then(dve.max_index(at[:, r, :], top[:, r, :], m[r % 2][:]))
                    then(dve.match_replace(m[1 - r % 2][:], top[:, r, :], m[r % 2][:], -3.0e38))
                then(dve.tensor_scalar(lowi[:], g.part_i[:], H - 1, None, ALU.bitwise_and))
                then(dve.tensor_copy(lowf[:], lowi[:]))
                then(dve.tensor_tensor(basf[:], g.part_f[:], lowf[:], ALU.subtract))
                then(dve.scalar_tensor_tensor(out=basf[:], in0=basf[:], scalar=float(S), in1=lowf[:],
                                              op0=ALU.mult, op1=ALU.add))
                then(dve.tensor_scalar(rows[:], at[:].rearrange("p r k -> p (r k)"), float(H), basf[:, 0:1],
                                       ALU.mult, ALU.add))


def attend_selected(nc, g):
    NCH = 6
    HH = H // 2
    CH = [(n // 3, 3 * (n % 3), min(3, HH - 3 * (n % 3))) for n in range(NCH)]
    RM = 3 * TOP
    with ExitStack() as ctx:
        sb = lambda n, s, d=F32: ctx.enter_context(nc.sbuf_tensor(n, s, d))
        wk, wv = sb("d_wk", [P, DC, D]), sb("d_wv", [P, DC, D])
        bk, bv_row = sb("d_bk", [P, DC]), sb("d_bv_row", [P, D])
        mask = sb("d_mask", [RM, 3, HH])
        xT = [sb(f"d_xT{u}", [P, DC, S]) for u in range(2)]
        idx = [sb(f"d_idx{u}", [RM, NCH], I32) for u in range(2)]
        kT, v_ = sb("d_kT", [P, DC, S]), sb("d_v", [P, ST, D])
        vm = sb("d_vm", [P, D])
        qg = sb("d_qg", [RM, NCH, HD])
        e_ = sb("d_e", [RM, NCH, HH, HD])
        bd = sb("d_bd", [P, NCH, RM])
        mx, nmx = sb("d_mx", [RM, NCH]), sb("d_nmx", [RM, NCH])
        rs, rinv = sb("d_rs", [RM, NCH]), sb("d_rinv", [RM, NCH])
        pm = [sb(f"d_pm{i}", [RM, S]) for i in range(2)]
        pT = sb("d_pT", [P, ST, RM])
        cm = sb("d_cm", [RM, HH, HD])
        cr = sb("d_cr", [RM, NCH, HD])
        sc = [ctx.enter_context(nc.psum_tensor(f"d_sc{i}", [P, 2, 512], F32)) for i in range(2)]
        pt = ctx.enter_context(nc.psum_tensor("d_pt", [P, 2, 4, P], F32))
        bdp = ctx.enter_context(nc.psum_tensor("d_bdp", [P, 3, P], F32))
        cx = ctx.enter_context(nc.psum_tensor("d_cx", [P, P], F32))
        w_in = g.sem("d_w_in")
        x_in = [g.sem(f"d_x_in{u}") for u in range(2)]
        (pj_ok, kt_ok, v_ok, vm_ok, vm_out, qg_in, e_ok, bdp_ok, bd_ok, sc_ok, mx_ok, nmx_ok, exp_ok, pt_ok,
         pTa_ok, pTb_ok, cx_ok, rinv_ok, cm_ok, cr_ok, put) = (g.sem("d_" + n) for n in (
             "pj", "kt", "v", "vm", "vm_out", "qg", "e", "bdp", "bd", "sc", "mx", "nmx", "exp", "pt",
             "pTa", "pTb", "cx", "rinv", "cm", "cr", "put"))
        mask1, mask2, mask3 = g.sem("d_mask1"), g.sem("d_mask2"), g.sem("d_mask3")
        x_b = g.xnT.rearrange("(v u) p c t -> v u p c t", u=2)
        sel_b = g.sel_rows.rearrange("(v u r) a -> v u r a", u=2, r=H * TOP)
        out_b = g.attn_rows.rearrange("(b c p h) e -> b p c (h e)", b=B, p=P, h=H)
        with nc.allow_non_contiguous_dma(reason="bias columns and row numbers"), nc.Block() as block:
            @block.sync
            def _(sp):
                sp.dma_start(wk[:], split_load_w(g.Wk)).then_inc(w_in, 16)
                sp.dma_start(wv[:], split_load_w(g.Wv)).then_inc(w_in, 16)
                sp.dma_start(bk[:], g.bk.rearrange("(c p) -> p c", p=P)).then_inc(w_in, 16)
                sp.dma_start(bv_row[:], g.bv.rearrange("(a n) -> a n", a=1).to_broadcast([P, D])).then_inc(w_in, 16)

                def load(v, u):
                    sp.dma_start(xT[u][:], x_b[v, u]).then_inc(x_in[u], 16)
                    for n, (hf, h0, nh) in enumerate(CH):
                        r0 = (hf * HH + h0) * TOP
                        sp.dma_start(idx[u][0:nh * TOP, n:n + 1],
                                     sel_b[v, u, r0:r0 + nh * TOP, :]).then_inc(x_in[u], 16)

                def means(b):
                    sp.wait_ge(vm_ok, b + 1)
                    sp.dma_start(out_b[b], vm[:].unsqueeze(1).to_broadcast([P, ST, D])).then_inc(vm_out, 16)
                load(0, 0)
                load(0, 1)
                means(0)
                with sp.Fori(0, B // 2 - 1) as v:
                    for u in range(2):
                        wait_alone(sp, g, pj_ok, v * 18 + 9 * u + 9)
                        wait_alone(sp, g, put, (v * 2 + u + 1) * (16 * NCH))
                        load(v + 1, u)
                        means(v * 2 + u + 1)
                means(B - 1)

            @block.tensor
            def _(pe):
                pe.wait_ge(w_in, 64)
                with pe.Fori(0, B // 2) as v:
                    for u in range(2):
                        b = v * 2 + u
                        pe.wait_ge(x_in[u], v * 112 + 112)
                        pe.wait_ge(exp_ok, b * NCH)
                        for n in range(9):
                            out = sc[n % 4 // 2][:, n % 2, :]
                            if 4 <= n < 8:
                                pe.wait_ge(kt_ok, b * 4 + n - 3)
                            if n < 4:
                                m, t0 = n // 2, 512 * (n % 2)
                                for k in range(DC):
                                    last = pe.matmul(out, wk[:, k, P * m:P * m + P], xT[u][:, k, t0:t0 + 512],
                                                     start=(k == 0), stop=(k == DC - 1))
                            elif n < 8:
                                for a in range(2):
                                    c = 2 * (n - 4) + a
                                    for k in range(DC):
                                        last = pe.matmul(out[:, D * a:D * a + D], xT[u][:, k, P * c:P * c + P],
                                                         wv[:, k, :], start=(k == 0), stop=(k == DC - 1))
                            else:
                                pe.wait_ge(v_ok, b * 4 + 4)
                                for c in range(ST):
                                    last = pe.matmul(out[:, 0:D], g.ones[:], v_[:, c, :],
                                                     start=(c == 0), stop=(c == ST - 1))
                            last.then_inc(pj_ok, 1)
                        pe.wait_ge(e_ok, b * NCH + NCH)
                        for r in range(2):
                            pe.wait_ge(bd_ok, b * NCH + 3 * r)
                            for kk in range(3):
                                rows = CH[kk][2] * TOP
                                last = pe.transpose(bdp[:, kk, 0:rows],
                                                    e_[0:rows, 3 * r + kk, :, :].rearrange("r h e -> r (h e)"),
                                                    g.ident[0:rows, 0:rows])
                            last.then_inc(bdp_ok, 1)
                        pe.wait_ge(vm_ok, b + 1)
                        for i in range(NCH + 1):
                            if i >= 1:
                                n, rows = i - 1, CH[i - 1][2] * TOP
                                pe.wait_ge(exp_ok, b * NCH + n + 1)
                                pe.wait_ge(pTa_ok, b * NCH + n)
                                pe.wait_ge(pTb_ok, b * NCH + n)
                                for c in range(ST):
                                    last = pe.transpose(pt[:, c // 4, c % 4, 0:rows], pm[n % 2][0:rows, P * c:P * c + P],
                                                        g.ident[0:rows, 0:rows])
                                last.then_inc(pt_ok, 1)
                            if i < NCH:
                                n, hf, rows = i, CH[i][0], CH[i][2] * TOP
                                pe.wait_ge(bd_ok, b * NCH + n + 1)
                                for s in range(2):
                                    last = pe.matmul(sc[n % 2][0:rows, s, :], bd[:, n, 0:rows],
                                                     kT[:, hf, 512 * s:512 * s + 512], start=True, stop=True)
                                last.then_inc(sc_ok, 1)
                            if i >= 1:
                                n, hf, rows = i - 1, CH[i - 1][0], CH[i - 1][2] * TOP
                                pe.wait_ge(pTa_ok, b * NCH + n + 1)
                                pe.wait_ge(pTb_ok, b * NCH + n + 1)
                                pe.wait_ge(cm_ok, b * NCH + n)
                                for c in range(ST):
                                    last = pe.matmul(cx[0:rows, :], pT[:, c, 0:rows], v_[:, c, P * hf:P * hf + P],
                                                     start=(c == 0), stop=(c == ST - 1))
                                last.then_inc(cx_ok, 1)

            @block.scalar
            def _(act):
                act.wait_ge(w_in, 64)
                with act.Fori(0, B) as b:
                    act.wait_ge(cx_ok, b * NCH)
                    for n in range(4):
                        act.wait_ge(pj_ok, b * 9 + n + 1)
                        act.activation(kT[:, n // 2, 512 * (n % 2):512 * (n % 2) + 512], sc[n // 2][:, n % 2, :],
                                       ACT.Identity, bias=bk[:, n // 2:n // 2 + 1]).then_inc(kt_ok, 1)
                    act.wait_ge(pj_ok, b * 9 + 9)
                    act.wait_ge(vm_out, b * 16)
                    act.mul(vm[:], sc[0][:, 0, 0:D], 1.0 / S).then_inc(vm_ok, 1)
                    for r in range(2):
                        act.wait_ge(bdp_ok, b * 2 + r + 1)
                        for kk in range(3):
                            rows = CH[kk][2] * TOP
                            act.copy(bd[:, 3 * r + kk, 0:rows], bdp[:, kk, 0:rows]).then_inc(bd_ok, 1)
                    for i in range(NCH + 1):
                        if i >= 1:
                            n, rows = i - 1, CH[i - 1][2] * TOP
                            act.wait_ge(pt_ok, b * NCH + n + 1)
                            act.wait_ge(cx_ok, b * NCH + n)
                            act.copy(pT[:, 0:4, 0:rows], pt[:, 0, :, 0:rows]).then_inc(pTa_ok, 1)
                        if i < NCH:
                            n, rows = i, CH[i][2] * TOP
                            act.wait_ge(nmx_ok, b * NCH + n + 1)
                            act.activation(pm[n % 2][0:rows, :], sc[n % 2][0:rows, :, :].rearrange("r a t -> r (a t)"),
                                           ACT.Exp, bias=nmx[0:rows, n:n + 1], scale=0.25,
                                           accum_out=rs[0:rows, n:n + 1]).then_inc(exp_ok, 1)

            @block.vector
            def _(dve):
                dve.wait_ge(w_in, 64)
                dve.wait_ge(mask3, 3)
                with dve.Fori(0, B) as b:
                    dve.wait_ge(cx_ok, b * NCH)
                    for n in range(4):
                        dve.wait_ge(pj_ok, b * 9 + n + 5)
                        dve.tensor_tensor(v_[:, 2 * n:2 * n + 2, :], sc[n // 2][:, n % 2, :].rearrange("p (a d) -> p a d", a=2),
                                          bv_row[:].unsqueeze(1).to_broadcast([P, 2, D]), ALU.add).then_inc(v_ok, 1)
                    dve.wait_ge(qg_in, b * (16 * NCH) + 16 * NCH)
                    for n, (hf, h0, nh) in enumerate(CH):
                        r = nh * TOP
                        dve.tensor_tensor(e_[0:r, n, :, :], qg[0:r, n, :].unsqueeze(1).to_broadcast([r, HH, HD]),
                                          mask[0:r, n % 3, :].unsqueeze(2).to_broadcast([r, HH, HD]),
                                          ALU.mult).then_inc(e_ok, 1)
                    for i in range(NCH + 1):
                        if i >= 1:
                            n, rows = i - 1, CH[i - 1][2] * TOP
                            dve.wait_ge(pt_ok, b * NCH + n + 1)
                            dve.wait_ge(cx_ok, b * NCH + n)
                            dve.tensor_copy(pT[:, 4:8, 0:rows], pt[:, 1, :, 0:rows]).then_inc(pTb_ok, 1)
                        if i < NCH:
                            n, rows = i, CH[i][2] * TOP
                            dve.wait_ge(sc_ok, b * NCH + n + 1)
                            dve.tensor_reduce(mx[0:rows, n:n + 1], sc[n % 2][0:rows, :, :], AX.XY, ALU.max).then_inc(mx_ok, 1)
                            dve.wait_ge(mx_ok, b * NCH + n + 1)
                            dve.tensor_scalar(nmx[0:rows, n:n + 1], mx[0:rows, n:n + 1], -0.25, None,
                                              ALU.mult).then_inc(nmx_ok, 1)
                        if i >= 1:
                            n, rows = i - 1, CH[i - 1][2] * TOP
                            dve.reciprocal(rinv[0:rows, n:n + 1], rs[0:rows, n:n + 1]).then_inc(rinv_ok, 1)
                            dve.wait_ge(rinv_ok, b * NCH + n + 1)
                            dve.wait_ge(cx_ok, b * NCH + n + 1)
                            dve.scalar_tensor_tensor(out=cm[0:rows, :, :],
                                                     in0=cx[0:rows, :].rearrange("r (h e) -> r h e", h=HH),
                                                     scalar=rinv[0:rows, n:n + 1],
                                                     in1=mask[0:rows, n % 3, :].unsqueeze(2).to_broadcast([rows, HH, HD]),
                                                     op0=ALU.mult, op1=ALU.mult).then_inc(cm_ok, 1)
                            dve.wait_ge(cm_ok, b * NCH + n + 1)
                            dve.wait_ge(put, b * (16 * NCH))
                            dve.tensor_reduce(cr[0:rows, n, :], cm[0:rows, :, :].rearrange("r h e -> r e h"),
                                              AX.X, ALU.add).then_inc(cr_ok, 1)

            @block.gpsimd
            def _(pool):
                pool.memset(mask[:], 1.0).then_inc(mask1, 1)
                pool.wait_ge(mask1, 1)
                for kk in range(3):
                    pool.affine_select(out=mask[:, kk, :], in_=mask[:, kk, :], compare_op=ALU.is_ge, fill=0.0,
                                       base=TOP * 3 * kk, pattern=[[-TOP, HH]], channel_multiplier=1).then_inc(mask2, 1)
                pool.wait_ge(mask2, 3)
                for kk in range(3):
                    pool.affine_select(out=mask[:, kk, :], in_=mask[:, kk, :], compare_op=ALU.is_ge, fill=0.0,
                                       base=TOP - 1 - TOP * 3 * kk, pattern=[[TOP, HH]],
                                       channel_multiplier=-1).then_inc(mask3, 1)
                with pool.Fori(0, B // 2) as v:
                    for u in range(2):
                        b = v * 2 + u
                        pool.wait_ge(x_in[u], v * 112 + 112)
                        wait_alone(pool, g, e_ok, b * NCH)
                        for n, (hf, h0, nh) in enumerate(CH):
                            r = nh * TOP
                            pool.indirect_dma_start(
                                out=qg[0:r, n, :], out_offset=None, in_=g.q_rows,
                                in_offset=bass.IndirectOffsetOnAxis(ap=idx[u][0:r, n:n + 1], axis=0)).then_inc(qg_in, 16)
                        pool.wait_ge(vm_out, b * 16 + 16)
                        for n, (hf, h0, nh) in enumerate(CH):
                            r = nh * TOP
                            wait_alone(pool, g, cr_ok, b * NCH + n + 1)
                            pool.indirect_dma_start(
                                out=g.attn_rows, in_=cr[0:r, n, :], in_offset=None,
                                out_offset=bass.IndirectOffsetOnAxis(ap=idx[u][0:r, n:n + 1], axis=0)).then_inc(put, 16)
                pool.wait_ge(put, B * 16 * NCH)


def add_attention_and_gate(nc, g):
    E = 8
    with ExitStack() as ctx:
        sb = lambda n, s, d=F32: ctx.enter_context(nc.sbuf_tensor(n, s, d))
        wo, gate = sb("e_wo", [P, DC, D]), sb("e_gate", [P, DC, E])
        bo_row = sb("e_bo_row", [P, D])
        a_ = [sb(f"e_attn{u}", [P, ST, D]) for u in range(2)]
        x_ = [sb(f"e_xin{u}", [P, ST, D]) for u in range(2)]
        aT = sb("e_aT", [P, DC, S])
        x1 = sb("e_x1", [P, ST, D])
        xn = sb("e_xn", [P, ST, D])
        xnT = sb("e_xnT", [P, DC, S])
        st, mv = sb("e_st", [P, ST, 6]), sb("e_mv", [P, ST, 2])
        var, std, rstd, tmp = (sb("e_" + n, [P, ST]) for n in ("var", "std", "rstd", "tmp"))
        mx, den, rden = (sb("e_" + n, [P, ST]) for n in ("mx", "den", "rden"))
        lg, ex, pr = (sb("e_" + n, [P, ST, E]) for n in ("lg", "ex", "pr"))
        tp = [ctx.enter_context(nc.psum_tensor(f"e_tp{i}", [P, 4, P], F32)) for i in range(2)]
        pj = [ctx.enter_context(nc.psum_tensor(f"e_pj{i}", [P, 2, D], F32)) for i in range(4)]
        gt = ctx.enter_context(nc.psum_tensor("e_gt", [P, ST, E], F32))
        w_in = g.sem("e_w_in")
        in_ = [g.sem(f"e_in{u}") for u in range(2)]
        (tp_ok, T_ok, xb_ok, pj_ok, x1_ok, stats, var_ok, std_ok, rstd_ok, xn_ok, gt_ok, sm, ex_ok, out) = (
            g.sem("e_" + n) for n in ("tp", "T", "xb", "pj", "x1", "stats", "var", "std", "rstd", "xn", "gt",
                                      "sm", "ex", "out"))
        NO = 4
        tiles = lambda t: t.rearrange("(v u c p) d -> v u p c d", u=2, c=ST, p=P)
        out_tiles = lambda t: t.rearrange("(b c p) d -> b p c d", c=ST, p=P)
        attn = tiles(g.attn_rows.rearrange("(t h) e -> t (h e)", h=H))
        x_b = tiles(g.x.rearrange("b s d -> (b s) d"))
        tab = out_tiles(g.tab)
        with nc.Block() as block:
            @block.sync
            def _(sp):
                sp.dma_start(wo[:], split_load_w(g.Wo)).then_inc(w_in, 16)
                sp.dma_start(gate[:], split_load_w(g.gate)).then_inc(w_in, 16)
                sp.dma_start(bo_row[:], g.bo.rearrange("(a n) -> a n", a=1).to_broadcast([P, D])).then_inc(w_in, 16)

                def load(v, u):
                    sp.dma_start(a_[u][:], attn[v, u]).then_inc(in_[u], 16)
                    sp.dma_start(x_[u][:], x_b[v, u]).then_inc(in_[u], 16)
                load_ahead(sp, B // 2, x1_ok, 4, load)

            @block.gpsimd
            def _(pool):
                pool.wait_ge(w_in, 48)
                with pool.Fori(0, B // 2) as v:
                    for u in range(2):
                        pool.wait_ge(in_[u], v * 32 + 32)
                        for c in range(ST):
                            last = pool.tensor_tensor(x_[u][:, c, :], x_[u][:, c, :], bo_row[:], ALU.add)
                        last.then_inc(xb_ok, 1)

            @block.tensor
            def _(pe):
                pe.wait_ge(w_in, 48)
                with pe.Fori(0, B // 2) as v:
                    for u in range(2):
                        b = v * 2 + u
                        pe.wait_ge(in_[u], v * 32 + 32)
                        for n in range(8):
                            src = a_[u] if n < 4 else xn
                            pe.wait_ge(T_ok, b * 8 + max(n - 1, 0))
                            if n == 4:
                                pe.wait_ge(T_ok, b * 8 + 4)
                                pe.wait_ge(x1_ok, b * 4)
                                for c in range(ST):
                                    for k in range(DC):
                                        last = pe.matmul(pj[c // 2][:, c % 2, :], aT[:, k, P * c:P * c + P], wo[:, k, :],
                                                         start=(k == 0), stop=(k == DC - 1))
                                    if c % 2:
                                        last.then_inc(pj_ok, 1)
                                pe.wait_ge(xn_ok, b + 1)
                            for a in range(4):
                                c = 4 * (n % 2) + a
                                k = (n % 4) // 2
                                last = pe.transpose(tp[n % 2][:, a, :], src[:, c, P * k:P * k + P], g.ident[:])
                            last.then_inc(tp_ok, 1)
                        pe.wait_ge(T_ok, b * 8 + 8)
                        pe.wait_ge(sm, b * 6)
                        for c in range(ST):
                            for k in range(DC):
                                last = pe.matmul(gt[:, c, :], xnT[:, k, P * c:P * c + P], gate[:, k, :],
                                                 start=(k == 0), stop=(k == DC - 1))
                        last.then_inc(gt_ok, 1)

            @block.scalar
            def _(act):
                with act.Fori(0, B) as b:
                    for n in range(8):
                        act.wait_ge(tp_ok, b * 8 + n + 1)
                        dst = aT if n < 4 else xnT
                        if n == 4:
                            act.wait_ge(out, b * (16 * NO))
                        act.copy(dst[:, (n % 4) // 2, 512 * (n % 2):512 * (n % 2) + 512],
                                 tp[n % 2][:].rearrange("p a b -> p (a b)")).then_inc(T_ok, 1)
                        if n == 3:
                            act.wait_ge(var_ok, b + 1)
                            act.activation(std[:], var[:], ACT.Sqrt).then_inc(std_ok, 1)
                    act.wait_ge(sm, b * 6 + 2)
                    act.activation(ex[:], lg[:], ACT.Exp).then_inc(ex_ok, 1)
                    act.dma_start(out_tiles(g.x1)[b], x1[:]).then_inc(out, 16)
                    act.dma_start(tab[b][:, :, 0:D], xn[:]).then_inc(out, 16)
                    act.wait_ge(T_ok, b * 8 + 8)
                    act.dma_start(g.xnT1[b], xnT[:]).then_inc(out, 16)
                    act.wait_ge(sm, b * 6 + 5)
                    act.dma_start(tab[b][:, :, D:D + E], pr[:]).then_inc(out, 16)
                    act.wait_ge(out, b * (16 * NO) + 16 * NO)

            @block.vector
            def _(dve):
                with dve.Fori(0, B // 2) as v:
                    for u in range(2):
                        b = v * 2 + u
                        dve.wait_ge(xb_ok, b + 1)
                        dve.wait_ge(out, b * (16 * NO))
                        for n in range(4):
                            dve.wait_ge(pj_ok, b * 4 + n + 1)
                            dve.tensor_tensor(x1[:, 2 * n:2 * n + 2, :], pj[n][:], x_[u][:, 2 * n:2 * n + 2, :],
                                              ALU.add).then_inc(x1_ok, 1)
                        dve.wait_ge(x1_ok, b * 4 + 4)
                        for c in range(ST):
                            dve.bn_stats(st[:, c, :], x1[:, c, :]).then_inc(stats, 1)
                        wait_alone(dve, g, stats, b * (2 * ST) + ST)
                        for c in range(ST):
                            dve.bn_aggr(mv[:, c, :], st[:, c, :]).then_inc(stats, 1)
                        dve.wait_ge(stats, b * (2 * ST) + 2 * ST)
                        dve.tensor_scalar(var[:], mv[:, :, 1], EPS, None, ALU.add).then_inc(var_ok, 1)
                        dve.wait_ge(std_ok, b + 1)
                        sharpen_rstd(dve, rstd_ok, b * 4, rstd, std, var, tmp)
                        for c in range(ST):
                            last = dve.tensor_scalar(xn[:, c, :], x1[:, c, :], mv[:, c, 0:1], rstd[:, c:c + 1],
                                                     ALU.subtract, ALU.mult)
                        last.then_inc(xn_ok, 1)
                        dve.wait_ge(gt_ok, b + 1)
                        dve.tensor_reduce(mx[:], gt[:], AX.X, ALU.max).then_inc(sm, 1)
                        dve.wait_ge(sm, b * 6 + 1)
                        dve.tensor_tensor(lg[:], gt[:], mx[:].unsqueeze(2).to_broadcast([P, ST, E]),
                                          ALU.subtract).then_inc(sm, 1)
                        dve.wait_ge(ex_ok, b + 1)
                        dve.tensor_reduce(den[:], ex[:], AX.X, ALU.add).then_inc(sm, 1)
                        dve.wait_ge(sm, b * 6 + 3)
                        dve.reciprocal(rden[:], den[:]).then_inc(sm, 1)
                        dve.wait_ge(sm, b * 6 + 4)
                        dve.tensor_tensor(pr[:], ex[:], rden[:].unsqueeze(2).to_broadcast([P, ST, E]),
                                          ALU.mult).then_inc(sm, 1)
                        dve.wait_ge(sm, b * 6 + 5)
                        dve.tensor_copy(g.probs.rearrange("p e (b c) -> p b e c", b=B)[:, b, :, :],
                                        pr[:].rearrange("p c e -> p e c")).then_inc(sm, 1)

E0 = 8
CAP = T // E0
HID = 1024
HC = HID // P
BF16 = mybir.dt.bfloat16
ROW = D + E0


def as_float(t):
    return t[:].bitcast(F32)


def shared_ffn_and_choice(nc, g):
    G = 512
    NG = T // G
    W = CAP // P
    BITS = 30
    SG = 4
    SEARCH = -(-BITS // (2 * SG))
    with ExitStack() as ctx:
        sb = lambda n, s, d=F32: ctx.enter_context(nc.sbuf_tensor(n, s, d))
        w1, w2 = sb("s_w1", [P, DC, HID]), sb("s_w2", [P, HC, D])
        b1, b2_row = sb("s_b1", [P, HC]), sb("s_b2_row", [P, D])
        xT = [sb(f"s_xT{u}", [P, DC, G]) for u in range(2)]
        x1 = [sb(f"s_x1_{u}", [P, 4, D]) for u in range(2)]
        hT = sb("s_hT", [P, HC, G])
        y = [sb(f"s_y{u}", [P, 4, D]) for u in range(2)]
        thr, cand, keep = (sb("f_" + n, [P, E0], I32) for n in ("thr", "cand", "keep"))
        bit = sb("f_bit", [P, 1], I32)
        flag = sb("f_flag", [P, E0, NT])
        cnt, need = sb("f_cnt", [P, E0]), sb("f_need", [P, E0])
        eq, sel = sb("f_eq", [P, E0, NT]), sb("f_sel", [P, E0, NT])
        go_on = sb("f_go_on", [P, E0, NT])
        incl, pos = sb("f_incl", [P, E0, NT]), sb("f_pos", [P, E0, NT])
        posi, hi_i, lo_i = (sb("f_" + n, [P, E0, NT], I32) for n in ("posi", "hi_i", "lo_i"))
        hi_f, lo_f = sb("f_hi_f", [P, E0, NT]), sb("f_lo_f", [P, E0, NT])
        hot_lo = sb("f_hot_lo", [P, NT, P], BF16)
        hot_hi = sb("f_hot_hi", [P, NT, W])
        val = sb("f_val", [P, 2, NT, W], BF16)
        col_i, colf = sb("f_col_i", [P, NT], I32), sb("f_colf", [P, NT])
        lst = sb("f_lst", [P, W])
        hp = [ctx.enter_context(nc.psum_tensor(f"s_hp{i}", [P, G], F32)) for i in range(4)]
        yp = [ctx.enter_context(nc.psum_tensor(f"s_yp{i}", [P, 2, D], F32)) for i in range(2)]
        bank = [ctx.enter_context(nc.psum_tensor(f"f_bank{i}", [P, E0 * NT], F32)) for i in range(2)]
        tot = bank[0][:, 0:E0]
        pre, col = (bank[i][:].rearrange("p (e c) -> p e c", e=E0) for i in range(2))
        lp = bank[0][:, 0:2 * W].rearrange("p (i w) -> p i w", i=2)
        w_in = g.sem("s_w_in")
        in_ = [g.sem(f"s_in{u}") for u in range(2)]
        hp_ok, h_ok, yp_ok, y_ok, xb_ok = (g.sem("s_" + n) for n in ("hp", "h", "yp", "y", "xb"))
        out = [g.sem(f"s_out{u}") for u in range(2)]
        ready, step, cnt_ok, tot_ok, pre_in, pre_ok, hot_ok, lp_ok, stepe = (
            g.sem("f_" + n) for n in ("ready", "step", "cnt", "tot", "pre_in", "pre", "hot", "lp", "stepe"))
        xT_g = g.xnT1.rearrange("v p c (u t) -> v u p c t", u=2)
        rows = lambda t: t.rearrange("(v u c p) d -> v u p c d", u=2, c=4, p=P)
        wide = lambda t: t.unsqueeze(2).to_broadcast([P, E0, NT])
        with nc.allow_non_contiguous_dma(reason="bias columns"), nc.Block() as block:
            @block.sync
            def _(sp):
                sp.dma_start(w1[:], split_load_w(g.Ws1)).then_inc(w_in, 16)
                sp.dma_start(w2[:], split_load_w(g.Ws2)).then_inc(w_in, 16)
                sp.dma_start(b1[:], g.bs1.rearrange("(c p) -> p c", p=P)).then_inc(w_in, 16)
                sp.dma_start(b2_row[:], g.bs2.rearrange("(a n) -> a n", a=1).to_broadcast([P, D])).then_inc(w_in, 16)

                def load(v, u):
                    sp.dma_start(xT[u][:], xT_g[v, u]).then_inc(in_[u], 16)
                    sp.dma_start(x1[u][:], rows(g.x1)[v, u]).then_inc(in_[u], 16)
                load_ahead(sp, NG // 2, y_ok, 2, load)

            @block.gpsimd
            def _(pool):
                pool.memset(bit[:], 1 << (BITS - 1)).then_inc(ready, 1)
                pool.memset(thr[:], 0).then_inc(ready, 1)
                pool.memset(go_on[:], 1.0).then_inc(ready, 1)
                pool.iota(col_i[:], pattern=[[1, NT]], base=0, channel_multiplier=0).then_inc(ready, 1)
                pool.wait_ge(w_in, 64)
                with pool.Fori(0, NG // 2) as v:
                    for u in range(2):
                        pool.wait_ge(in_[u], v * 32 + 32)
                        for c in range(4):
                            last = pool.tensor_tensor(x1[u][:, c, :], x1[u][:, c, :], b2_row[:], ALU.add)
                        last.then_inc(xb_ok, 1)

            @block.tensor
            def _(pe):
                def count(n):
                    pe.wait_ge(cnt_ok, n + 1)
                    pe.matmul(tot, g.ones[:], cnt[:], start=True, stop=True).then_inc(tot_ok, 1)

                def sums(r, src):
                    pe.wait_ge(pre_in, r + 1)
                    flat = src[:].rearrange("p e c -> p (e c)")
                    pe.matmul(bank[0][:], g.tri[:], flat, start=True, stop=True)
                    pe.matmul(bank[1][:], g.ones[:], flat, start=True, stop=True).then_inc(pre_ok, 1)

                def make_list(e):
                    pe.wait_ge(hot_ok, e + 1)
                    for c in range(NT):
                        last = pe.matmul(lp, hot_lo[:, c, :], val[:, :, c, :], start=(c == 0), stop=(c == NT - 1))
                    last.then_inc(lp_ok, 1)

                def group(v, u, choice):
                    i = v * 2 + u
                    pe.wait_ge(in_[u], v * 32 + 32)
                    for j in range(HC):
                        pe.wait_ge(h_ok, i * HC + max(j - 3, 0))
                        for k in range(DC):
                            last = pe.matmul(hp[j % 4][:], w1[:, k, P * j:P * j + P], xT[u][:, k, :],
                                             start=(k == 0), stop=(k == DC - 1))
                        last.then_inc(hp_ok, 1)
                        choice(j)
                    pe.wait_ge(y_ok, i * 2)
                    for a in range(2):
                        for c in range(2):
                            for k in range(HC):
                                if a == 0 and c == 0:
                                    pe.wait_ge(h_ok, i * HC + k + 1)
                                t0 = P * (2 * a + c)
                                last = pe.matmul(yp[a][:, c, :], hT[:, k, t0:t0 + P], w2[:, k, :],
                                                 start=(k == 0), stop=(k == HC - 1))
                            if c == 1:
                                last.then_inc(yp_ok, 1)
                            choice(HC + 2 * a + c)

                pe.wait_ge(w_in, 64)
                with pe.Fori(0, SEARCH) as v:
                    for u in range(2):
                        def searching(j):
                            if j % 2 and j < 2 * SG:
                                count((v * 2 + u) * SG + j // 2)
                        group(v, u, searching)

                def summing(j):
                    if j == 1:
                        count(2 * SG * SEARCH)
                    elif j in (3, 7):
                        sums(j // 4, (eq, sel)[j // 4])
                group(SEARCH, 0, summing)

                def first_lists(j):
                    if j in (6, 10):
                        make_list((j - 6) // 4)
                group(SEARCH, 1, first_lists)
                with pe.Fori(SEARCH + 1, NG // 2) as v:
                    for u in range(2):
                        def listing(j):
                            if j == 7:
                                make_list(v * 2 + u - 2 * SEARCH)
                        group(v, u, listing)

            @block.scalar
            def _(act):
                act.wait_ge(w_in, 64)
                with act.Fori(0, NG // 2) as v:
                    for u in range(2):
                        i = v * 2 + u
                        act.wait_ge(yp_ok, i * 2)
                        for j in range(HC):
                            act.wait_ge(hp_ok, i * HC + j + 1)
                            act.activation(hT[:, j, :], hp[j % 4][:], ACT.Gelu_apprx_tanh,
                                           bias=b1[:, j:j + 1]).then_inc(h_ok, 1)
                        act.wait_ge(y_ok, i * 2 + 2)
                        act.dma_start(rows(g.x2)[v, u], y[u][:]).then_inc(out[u], 16)
                for u in range(2):
                    act.wait_ge(out[u], 16 * (NG // 2))

            @block.vector
            def _(dve):
                def y_out(v, u, a):
                    i = v * 2 + u
                    if a == 0:
                        dve.wait_ge(xb_ok, i + 1)
                        dve.wait_ge(out[u], v * 16)
                    dve.wait_ge(yp_ok, i * 2 + a + 1)
                    dve.tensor_tensor(y[u][:, 2 * a:2 * a + 2, :], yp[a][:], x1[u][:, 2 * a:2 * a + 2, :],
                                      ALU.add).then_inc(y_ok, 1)

                KS = 5

                def search(i):
                    def chain(ins, k):
                        ins.then_inc(step, 1)
                        dve.wait_ge(step, i * KS + k)
                    chain(dve.tensor_tensor(cand[:], thr[:], bit[:].to_broadcast([P, E0]), ALU.bitwise_or), 1)
                    chain(dve.tensor_tensor(flag[:], g.probs, wide(as_float(cand)), ALU.is_ge), 2)
                    dve.tensor_reduce(cnt[:], flag[:], AX.X, ALU.add).then_inc(cnt_ok, 1)
                    dve.wait_ge(tot_ok, i + 1)
                    chain(dve.scalar_tensor_tensor(out=keep[:], in0=tot, scalar=float(CAP),
                                                   in1=bit[:].to_broadcast([P, E0]), op0=ALU.is_ge, op1=ALU.mult), 3)
                    chain(dve.tensor_tensor(thr[:], thr[:], keep[:], ALU.bitwise_or), 4)
                    chain(dve.tensor_scalar(bit[:], bit[:], 1, None, ALU.logical_shift_right), 5)

                KE = 5

                def hot_rows(e):
                    def chain(ins, k):
                        ins.then_inc(stepe, 1)
                        dve.wait_ge(stepe, e * KE + k)
                    dve.wait_ge(lp_ok, e)
                    dve.tensor_tensor(hot_lo[:], lo_f[:, e, :].unsqueeze(2).to_broadcast([P, NT, P]),
                                      g.iota_f[:].unsqueeze(1).to_broadcast([P, NT, P]), ALU.is_equal).then_inc(stepe, 1)
                    chain(dve.tensor_tensor(hot_hi[:], hi_f[:, e, :].unsqueeze(2).to_broadcast([P, NT, W]),
                                            g.iota_f[:, 0:W].unsqueeze(1).to_broadcast([P, NT, W]), ALU.is_equal), 2)
                    chain(dve.tensor_scalar(val[:, 0, :, :], hot_hi[:], g.part_f[:, 0:1], None, ALU.mult), 3)
                    dve.tensor_tensor(val[:, 1, :, :], hot_hi[:], colf[:].unsqueeze(2).to_broadcast([P, NT, W]),
                                      ALU.mult).then_inc(hot_ok, 1)

                def list_out(e):
                    dve.wait_ge(lp_ok, e + 1)
                    dve.tensor_copy(lst[:], lp[:, 0, :]).then_inc(stepe, 1)
                    dve.wait_ge(stepe, e * KE + 4)
                    dve.scalar_tensor_tensor(out=g.elist[:, e, :], in0=lp[:, 1, :], scalar=float(P), in1=lst[:],
                                             op0=ALU.mult, op1=ALU.add).then_inc(stepe, 1)
                    dve.wait_ge(stepe, e * KE + 5)

                dve.wait_ge(ready, 4)
                with dve.Fori(0, SEARCH) as v:
                    for u in range(2):
                        for s in range(SG):
                            search((v * 2 + u) * SG + s)
                        for a in range(2):
                            y_out(v, u, a)
                n = 2 * SG * SEARCH * KS

                def then(ins):
                    nonlocal n
                    n += 1
                    ins.then_inc(step, 1)
                    dve.wait_ge(step, n)
                then(dve.tensor_copy(colf[:], col_i[:]))
                then(dve.memset(go_on[:, :, 0:1], 0.0))
                then(dve.tensor_tensor(sel[:], g.probs, wide(as_float(thr)), ALU.is_gt))
                then(dve.tensor_tensor(eq[:], g.probs, wide(as_float(thr)), ALU.is_equal))
                dve.tensor_reduce(cnt[:], sel[:], AX.X, ALU.add).then_inc(cnt_ok, 1)
                dve.wait_ge(tot_ok, 2 * SG * SEARCH + 1)
                then(dve.tensor_scalar(need[:], tot, -1.0, float(CAP), ALU.mult, ALU.add))
                dve.sem_inc(pre_in, 1)

                def place():
                    then(dve.tensor_copy(flag[:], col))
                    then(dve.tensor_tensor_scan(incl[:].rearrange("p e c -> p (e c)"),
                                                go_on[:].rearrange("p e c -> p (e c)"),
                                                flag[:].rearrange("p e c -> p (e c)"), 0.0, ALU.mult, ALU.add))
                    then(dve.tensor_tensor(pos[:], incl[:], flag[:], ALU.subtract))
                    then(dve.tensor_tensor(pos[:], pos[:], pre, ALU.add))
                dve.wait_ge(pre_ok, 1)
                place()
                then(dve.tensor_tensor(flag[:], pos[:], wide(need[:]), ALU.is_lt))
                then(dve.tensor_tensor(flag[:], flag[:], eq[:], ALU.mult))
                then(dve.tensor_tensor(sel[:], sel[:], flag[:], ALU.add))
                dve.sem_inc(pre_in, 1)
                dve.wait_ge(pre_ok, 2)
                place()
                for a in range(2):
                    y_out(SEARCH, 0, a)
                then(dve.scalar_tensor_tensor(out=pos[:], in0=pos[:], scalar=1.0, in1=sel[:], op0=ALU.add, op1=ALU.mult))
                then(dve.tensor_scalar(posi[:], pos[:], -1.0, None, ALU.add))
                then(dve.tensor_scalar(lo_i[:], posi[:], P - 1, None, ALU.bitwise_and))
                then(dve.tensor_scalar(hi_i[:], posi[:], 7, None, ALU.arith_shift_right))
                then(dve.tensor_copy(lo_f[:], lo_i[:]))
                then(dve.tensor_copy(hi_f[:], hi_i[:]))
                for a in range(2):
                    hot_rows(a)
                    if a == 1:
                        y_out(SEARCH, 1, 0)
                    list_out(a)
                y_out(SEARCH, 1, 1)
                with dve.Fori(SEARCH + 1, NG // 2) as v:
                    for u in range(2):
                        e = v * 2 + u - 2 * SEARCH
                        hot_rows(e)
                        list_out(e)
                        for a in range(2):
                            y_out(v, u, a)


def expert_ffn(nc, g):
    G = 512
    GE = CAP // G
    NG = E0 * GE
    with ExitStack() as ctx:
        sb = lambda n, s, d=F32: ctx.enter_context(nc.sbuf_tensor(n, s, d))
        w1 = [sb(f"g_w1_{u}", [P, DC, HID]) for u in range(2)]
        w2 = [sb(f"g_w2_{u}", [P, HC, D]) for u in range(2)]
        b2_row = [sb(f"g_b2_row{u}", [P, D]) for u in range(2)]
        b1_rows = sb("g_b1_rows", [E0 * HC, P])
        b1 = sb("g_b1", [P, E0, HC])
        b1u = [sb(f"g_b1u{u}", [P, HC]) for u in range(2)]
        eidx = [sb(f"g_eidx{u}", [P, CAP // P], I32) for u in range(2)]
        tk = [sb(f"g_tk{i}", [P, 4, ROW]) for i in range(2)]
        pr = [sb(f"g_pr{i}", [P, 4]) for i in range(2)]
        xT = sb("g_xT", [P, DC, G])
        hT = sb("g_hT", [P, HC, G])
        yb = sb("g_yb", [P, 4, D])
        y = [sb(f"g_y{i}", [P, 4, D]) for i in range(2)]
        tp = [ctx.enter_context(nc.psum_tensor(f"g_tp{i}", [P, 4, P], F32)) for i in range(2)]
        hp = [ctx.enter_context(nc.psum_tensor(f"g_hp{i}", [P, G], F32)) for i in range(4)]
        yp = [ctx.enter_context(nc.psum_tensor(f"g_yp{i}", [P, 2, D], F32)) for i in range(2)]
        b_in, b_T, b_ok = g.sem("g_b_in"), g.sem("g_b_T"), g.sem("g_b_ok")
        w_in = [g.sem(f"g_w_in{u}") for u in range(2)]
        tk_in = [g.sem(f"g_tk_in{i}") for i in range(2)]
        (idx_ok, tp_ok, T_ok, hp_ok, h_ok, yp_ok, yb_ok, y_ok, pr_ok, put) = (
            g.sem("g_" + n) for n in ("idx", "tp", "T", "hp", "h", "yp", "yb", "y", "pr", "put"))
        w1_e = g.W1.rearrange("(v u) (c p) n -> v u p c n", u=2, p=P)
        w2_e = g.W2.rearrange("(v u) (c p) n -> v u p c n", u=2, p=P)
        b2_e = g.b2.rearrange("(v u a) n -> v u a n", u=2, a=1)
        STEPS = [(u, q) for u in range(2) for q in range(GE)]
        with nc.Block() as block:
            @block.sync
            def _(sp):
                sp.dma_start(b1_rows[:], g.b1.rearrange("e (j p) -> (e j) p", p=P)).then_inc(b_in, 16)

                def load(v, u):
                    sp.dma_start(w1[u][:], w1_e[v, u]).then_inc(w_in[u], 16)
                    sp.dma_start(w2[u][:], w2_e[v, u]).then_inc(w_in[u], 16)
                    sp.dma_start(b2_row[u][:], b2_e[v, u].to_broadcast([P, D])).then_inc(w_in[u], 16)
                load_ahead(sp, E0 // 2, yb_ok, GE * 4, load)

            @block.gpsimd
            def _(pool):
                def gather(v, s):
                    u, q = STEPS[s]
                    pool.wait_ge(idx_ok, v * 2 + u + 1)
                    if not (isinstance(v, int) and v == 0 and s < 2):
                        wait_alone(pool, g, pr_ok, v * (2 * GE) + s - 1)
                    for c in range(4):
                        pool.indirect_dma_start(
                            out=tk[s % 2][:, c, :], out_offset=None, in_=g.tab,
                            in_offset=bass.IndirectOffsetOnAxis(ap=eidx[u][:, 4 * q + c:4 * q + c + 1],
                                                                axis=0)).then_inc(tk_in[s % 2], 16)

                def add(v, s):
                    u, q = STEPS[s]
                    gi = v * (2 * GE) + s
                    wait_alone(pool, g, y_ok, gi * 4 + 4)
                    wait_alone(pool, g, put, gi * 64)
                    for c in range(4):
                        pool.indirect_dma_start(
                            out=g.x2, in_=y[s % 2][:, c, :], in_offset=None, compute_op=ALU.add,
                            out_offset=bass.IndirectOffsetOnAxis(ap=eidx[u][:, 4 * q + c:4 * q + c + 1],
                                                                 axis=0)).then_inc(put, 16)

                def pair(v, last=False):
                    for s in range(len(STEPS)):
                        if s + 1 < len(STEPS):
                            gather(v, s + 1)
                        elif not last:
                            gather(v + 1, 0)
                        add(v, s)
                gather(0, 0)
                with pool.Fori(0, E0 // 2 - 1) as v:
                    pair(v)
                pair(E0 // 2 - 1, True)
                pool.wait_ge(put, NG * 64)

            @block.tensor
            def _(pe):
                pe.wait_ge(b_in, 16)
                pe.transpose(tp[0][:, 0, 0:E0 * HC], b1_rows[:], g.ident[0:E0 * HC, 0:E0 * HC]).then_inc(b_T, 1)
                pe.wait_ge(b_ok, 1)
                with pe.Fori(0, E0 // 2) as v:
                    for s, (u, q) in enumerate(STEPS):
                        gi = v * (2 * GE) + s
                        pe.wait_ge(tk_in[s % 2], v * (64 * GE) + 64 * (s // 2 + 1))
                        pe.wait_ge(T_ok, gi * 2)
                        for k in range(DC):
                            for a in range(4):
                                last = pe.transpose(tp[k][:, a, :], tk[s % 2][:, a, P * k:P * k + P], g.ident[:])
                            last.then_inc(tp_ok, 1)
                        pe.wait_ge(T_ok, gi * 2 + 2)
                        pe.wait_ge(w_in[u], v * 48 + 48)
                        for j in range(HC):
                            pe.wait_ge(h_ok, gi * HC + max(j - 3, 0))
                            for k in range(DC):
                                last = pe.matmul(hp[j % 4][:], w1[u][:, k, P * j:P * j + P], xT[:, k, :],
                                                 start=(k == 0), stop=(k == DC - 1))
                            last.then_inc(hp_ok, 1)
                        pe.wait_ge(yb_ok, gi * 4)
                        for a in range(2):
                            for c in range(2):
                                for k in range(HC):
                                    if a == 0 and c == 0:
                                        pe.wait_ge(h_ok, gi * HC + k + 1)
                                    t0 = P * (2 * a + c)
                                    last = pe.matmul(yp[a][:, c, :], hT[:, k, t0:t0 + P], w2[u][:, k, :],
                                                     start=(k == 0), stop=(k == HC - 1))
                            last.then_inc(yp_ok, 1)

            @block.scalar
            def _(act):
                act.wait_ge(b_T, 1)
                act.copy(b1[:].rearrange("p e j -> p (e j)"), tp[0][:, 0, 0:E0 * HC]).then_inc(b_ok, 1)
                with act.Fori(0, E0 // 2) as v:
                    for s, (u, q) in enumerate(STEPS):
                        gi = v * (2 * GE) + s
                        act.wait_ge(idx_ok, v * 2 + u + 1)
                        act.wait_ge(yp_ok, gi * 2)
                        for j in range(HC):
                            act.wait_ge(hp_ok, gi * HC + j + 1)
                            act.activation(hT[:, j, :], hp[j % 4][:], ACT.Gelu_apprx_tanh,
                                           bias=b1u[u][:, j:j + 1]).then_inc(h_ok, 1)

            @block.vector
            def _(dve):
                def renew(e, u):
                    dve.tensor_copy(eidx[u][:], g.elist[:, e, :])
                    dve.tensor_copy(b1u[u][:], b1[:, e, :]).then_inc(idx_ok, 1)

                def pair(v, last=False):
                    for s, (u, q) in enumerate(STEPS):
                        gi = v * (2 * GE) + s
                        if s == 1:
                            dve.wait_ge(put, v * (2 * GE * 64))
                            renew(v * 2 + 1, 1)
                        if s == 3 and not last:
                            dve.wait_ge(put, v * (2 * GE * 64) + GE * 64)
                            renew(v * 2 + 2, 0)
                        for k in range(DC):
                            dve.wait_ge(tp_ok, gi * 2 + k + 1)
                            dve.tensor_copy(xT[:, k, :], tp[k][:].rearrange("p a b -> p (a b)")).then_inc(T_ok, 1)
                        dve.tensor_copy(pr[s % 2][:], tk[s % 2][:, :, D:ROW].rearrange("p c (v u) -> p v u c", u=2)[:, v, u, :]
                                        ).then_inc(pr_ok, 1)
                        dve.wait_ge(pr_ok, gi + 1)
                        for a in range(2):
                            dve.wait_ge(yp_ok, gi * 2 + a + 1)
                            dve.tensor_tensor(yb[:, 2 * a:2 * a + 2, :], yp[a][:],
                                              b2_row[u][:].unsqueeze(1).to_broadcast([P, 2, D]), ALU.add).then_inc(yb_ok, 2)
                        dve.wait_ge(yb_ok, gi * 4 + 4)
                        dve.wait_ge(put, v * (2 * GE * 64) + 64 * max(s - 1, 0))
                        for c in range(4):
                            dve.tensor_scalar(y[s % 2][:, c, :], yb[:, c, :], pr[s % 2][:, c:c + 1], None,
                                              ALU.mult).then_inc(y_ok, 1)
                dve.wait_ge(b_ok, 1)
                renew(0, 0)
                with dve.Fori(0, E0 // 2 - 1) as v:
                    pair(v)
                pair(E0 // 2 - 1, True)


def causal_attention(nc, g):
    SCALE = 1.0 / 16.0
    with ExitStack() as ctx:
        sb = lambda n, s, d=F32: ctx.enter_context(nc.sbuf_tensor(n, s, d))
        w_rows = sb("h_w_rows", [P, 3, DC, D])
        wT = sb("h_wT", [P, 3, DC, D])
        b_col, bv_row = sb("h_b_col", [P, 2, DC]), sb("h_bv_row", [P, D])
        above = sb("h_above", [P, P])
        zero = sb("h_zero", [P, P])
        x2 = [sb(f"h_x2_{u}", [P, ST, D]) for u in range(2)]
        xn, xnT = sb("h_xn", [P, ST, D]), sb("h_xnT", [P, DC, S])
        st, mv = sb("h_st", [P, ST, 6]), sb("h_mv", [P, ST, 2])
        var, std, rstd, tmp = (sb("h_" + n, [P, ST]) for n in ("var", "std", "rstd", "tmp"))
        qT, kT, v_ = sb("h_qT", [P, DC, S]), sb("h_kT", [P, DC, S]), sb("h_v", [P, ST, D])
        mx, nmx, rs, rinv = (sb("h_" + n, [P, ST]) for n in ("mx", "nmx", "rs", "rinv"))
        pm = [sb(f"h_pm{i}", [P, S]) for i in range(2)]
        pT = sb("h_pT", [P, ST, P])
        x3 = sb("h_x3", [P, ST, D])
        sc = [ctx.enter_context(nc.psum_tensor(f"h_sc{i}", [P, 2, 512], F32)) for i in range(2)]
        pt = ctx.enter_context(nc.psum_tensor("h_pt", [P, 2, 4, P], F32))
        z = ctx.enter_context(nc.psum_tensor("h_z", [P, 2, 512], F32))
        w_in, wp_ok, wT_ok, zero_ok, above_ok = (g.sem("h_" + n) for n in ("w_in", "wp", "wT", "zero", "above"))
        x_in = [g.sem(f"h_x_in{u}") for u in range(2)]
        (stats, var_ok, std_ok, rstd_ok, xn_ok, tp_ok, T_ok, pj_ok, qk_ok, v_ok, sc_ok, mx_ok, nmx_ok, exp_ok, pt_ok,
         pTa_ok, pTb_ok, z_ok, rinv_ok, x3_ok, out) = (g.sem("h_" + n) for n in (
             "stats", "var", "std", "rstd", "xn", "tp", "T", "pj", "qk", "v", "sc", "mx", "nmx", "exp", "pt",
             "pTa", "pTb", "z", "rinv", "x3", "out"))
        tiles = lambda t: t.rearrange("(v u c p) d -> v u p c d", u=2, c=ST, p=P)
        with nc.allow_non_contiguous_dma(reason="bias columns"), nc.Block() as block:
            @block.sync
            def _(sp):
                for i, w in enumerate((g.Wq1, g.Wk1, g.Wv1)):
                    sp.dma_start(w_rows[:, i, :, :], split_load_w(w)).then_inc(w_in, 16)
                for i, b in enumerate((g.bq1, g.bk1)):
                    sp.dma_start(b_col[:, i, :], b.rearrange("(c p) -> p c", p=P)).then_inc(w_in, 16)
                sp.dma_start(bv_row[:], g.bv1.rearrange("(a n) -> a n", a=1).to_broadcast([P, D])).then_inc(w_in, 16)
                load_ahead(sp, B // 2, x3_ok, ST,
                           lambda v, u: sp.dma_start(x2[u][:], tiles(g.x2)[v, u]).then_inc(x_in[u], 16))

            @block.gpsimd
            def _(pool):
                pool.memset(zero[:], 0.0).then_inc(zero_ok, 1)
                pool.wait_ge(zero_ok, 1)
                pool.affine_select(out=above[:], in_=zero[:], compare_op=ALU.is_ge, fill=-1.0e30, base=0,
                                   pattern=[[-1, P]], channel_multiplier=1).then_inc(above_ok, 1)

            @block.tensor
            def _(pe):
                pe.wait_ge(w_in, 96)
                for i in range(3):
                    if i:
                        pe.wait_ge(wT_ok, i)
                    for dc in range(DC):
                        for kc in range(DC):
                            last = pe.transpose(pt[:, 0, dc * DC + kc, :], w_rows[:, i, kc, P * dc:P * dc + P], g.ident[:])
                    last.then_inc(wp_ok, 1)
                pe.wait_ge(wT_ok, 3)
                pe.wait_ge(above_ok, 1)
                with pe.Fori(0, B) as b:
                    pe.wait_ge(xn_ok, b + 1)
                    pe.wait_ge(pTb_ok, b * ST)
                    for n in range(4):
                        pe.wait_ge(T_ok, b * 4 + max(n - 1, 0))
                        for a in range(4):
                            last = pe.transpose(pt[:, n % 2, a, :], xn[:, 4 * (n % 2) + a, P * (n // 2):P * (n // 2) + P],
                                                g.ident[:])
                        last.then_inc(tp_ok, 1)
                    pe.wait_ge(T_ok, b * 4 + 4)
                    pe.wait_ge(exp_ok, b * ST)
                    for n in range(12):
                        out_ = sc[n % 4 // 2][:, n % 2, :]
                        if n >= 4:
                            pe.wait_ge(qk_ok, b * 8 + min(n - 3, 8))
                        if n < 8:
                            i, m, t0 = n // 4, n % 4 // 2, 512 * (n % 2)
                            for k in range(DC):
                                last = pe.matmul(out_, wT[:, i, k, P * m:P * m + P], xnT[:, k, t0:t0 + 512],
                                                 start=(k == 0), stop=(k == DC - 1))
                        else:
                            for a in range(2):
                                c = 2 * (n - 8) + a
                                for k in range(DC):
                                    last = pe.matmul(out_[:, D * a:D * a + D], xnT[:, k, P * c:P * c + P], wT[:, 2, k, :],
                                                     start=(k == 0), stop=(k == DC - 1))
                        last.then_inc(pj_ok, 1)
                    pe.wait_ge(v_ok, b * 4 + 4)
                    for i in range(ST + 1):
                        if i >= 1:
                            n = i - 1
                            pe.wait_ge(exp_ok, b * ST + n + 1)
                            pe.wait_ge(pTa_ok, b * ST + n)
                            pe.wait_ge(pTb_ok, b * ST + n)
                            for c in range(n + 1):
                                last = pe.transpose(pt[:, c // 4, c % 4, :], pm[n % 2][:, P * c:P * c + P], g.ident[:])
                            last.then_inc(pt_ok, 1)
                        if i < ST:
                            keys = P * (i + 1)
                            for s in range(0, keys, 512):
                                w = min(512, keys - s)
                                diag = s + w == keys
                                for k in range(DC):
                                    last = pe.matmul(sc[i % 2][:, s // 512, 0:w], qT[:, k, P * i:P * i + P], kT[:, k, s:s + w],
                                                     start=(k == 0), stop=(k == DC - 1 and not diag))
                                if diag:
                                    last = pe.matmul(sc[i % 2][:, s // 512, w - P:w], g.ident[:], above[:],
                                                     start=False, stop=True)
                            last.then_inc(sc_ok, 1)
                        if i >= 1:
                            n = i - 1
                            pe.wait_ge(pTa_ok, b * ST + n + 1)
                            pe.wait_ge(pTb_ok, b * ST + n + 1)
                            pe.wait_ge(x3_ok, b * ST + max(n - 1, 0))
                            for c in range(n + 1):
                                last = pe.matmul(z[:, n % 2, 0:D], pT[:, c, :], v_[:, c, :], start=(c == 0), stop=(c == n))
                            last.then_inc(z_ok, 1)

            @block.scalar
            def _(act):
                act.wait_ge(w_in, 96)
                for i in range(3):
                    act.wait_ge(wp_ok, i + 1)
                    act.copy(wT[:, i, :, :].rearrange("p c n -> p (c n)"), pt[:, 0, :, :].rearrange("p a b -> p (a b)")
                             ).then_inc(wT_ok, 1)
                with act.Fori(0, B) as b:
                    act.wait_ge(var_ok, b + 1)
                    act.activation(std[:], var[:], ACT.Sqrt).then_inc(std_ok, 1)
                    for n in range(4):
                        act.wait_ge(tp_ok, b * 4 + n + 1)
                        act.copy(xnT[:, n // 2, 512 * (n % 2):512 * (n % 2) + 512],
                                 pt[:, n % 2, :, :].rearrange("p a b -> p (a b)")).then_inc(T_ok, 1)
                    for n in range(8):
                        act.wait_ge(pj_ok, b * 12 + n + 1)
                        i, m = n // 4, n % 4 // 2
                        act.activation((qT, kT)[i][:, m, 512 * (n % 2):512 * (n % 2) + 512], sc[n % 4 // 2][:, n % 2, :],
                                       ACT.Identity, bias=b_col[:, i, m:m + 1]).then_inc(qk_ok, 1)
                    for i in range(ST + 1):
                        if i >= 1:
                            n = i - 1
                            act.wait_ge(pt_ok, b * ST + n + 1)
                            act.wait_ge(z_ok, b * ST + n)
                            w = min(4, n + 1)
                            act.copy(pT[:, 0:w, :], pt[:, 0, 0:w, :]).then_inc(pTa_ok, 1)
                        if i < ST:
                            keys = P * (i + 1)
                            act.wait_ge(nmx_ok, b * ST + i + 1)
                            act.activation(pm[i % 2][:, 0:keys], sc[i % 2][:].rearrange("p a t -> p (a t)")[:, 0:keys],
                                           ACT.Exp, bias=nmx[:, i:i + 1], scale=SCALE,
                                           accum_out=rs[:, i:i + 1]).then_inc(exp_ok, 1)
                    act.wait_ge(x3_ok, b * ST + ST)
                    act.dma_start(g.x3.rearrange("(b c p) d -> b p c d", c=ST, p=P)[b], x3[:]).then_inc(out, 16)
                act.wait_ge(out, 16 * B)

            @block.vector
            def _(dve):
                with dve.Fori(0, B // 2) as v:
                    for u in range(2):
                        b = v * 2 + u
                        dve.wait_ge(x_in[u], v * 16 + 16)
                        for c in range(ST):
                            dve.bn_stats(st[:, c, :], x2[u][:, c, :]).then_inc(stats, 1)
                        wait_alone(dve, g, stats, b * (2 * ST) + ST)
                        for c in range(ST):
                            dve.bn_aggr(mv[:, c, :], st[:, c, :]).then_inc(stats, 1)
                        dve.wait_ge(stats, b * (2 * ST) + 2 * ST)
                        dve.tensor_scalar(var[:], mv[:, :, 1], EPS, None, ALU.add).then_inc(var_ok, 1)
                        dve.wait_ge(std_ok, b + 1)
                        sharpen_rstd(dve, rstd_ok, b * 4, rstd, std, var, tmp)
                        for c in range(ST):
                            last = dve.tensor_scalar(xn[:, c, :], x2[u][:, c, :], mv[:, c, 0:1], rstd[:, c:c + 1],
                                                     ALU.subtract, ALU.mult)
                        last.then_inc(xn_ok, 1)
                        for n in range(4):
                            dve.wait_ge(pj_ok, b * 12 + n + 9)
                            dve.tensor_tensor(v_[:, 2 * n:2 * n + 2, :], sc[n // 2][:, n % 2, :].rearrange("p (a d) -> p a d", a=2),
                                              bv_row[:].unsqueeze(1).to_broadcast([P, 2, D]), ALU.add).then_inc(v_ok, 1)
                        for i in range(ST + 1):
                            n = i - 1
                            if n >= 4:
                                dve.wait_ge(pt_ok, b * ST + n + 1)
                                dve.wait_ge(z_ok, b * ST + n)
                                dve.tensor_copy(pT[:, 4:n + 1, :], pt[:, 1, 0:n - 3, :]).then_inc(pTb_ok, 1)
                            elif n >= 0:
                                dve.wait_ge(exp_ok, b * ST + n + 1)
                                dve.sem_inc(pTb_ok, 1)
                            if i < ST:
                                keys = P * (i + 1)
                                dve.wait_ge(sc_ok, b * ST + i + 1)
                                dve.tensor_reduce(mx[:, i:i + 1], sc[i % 2][:].rearrange("p a t -> p (a t)")[:, 0:keys],
                                                  AX.X, ALU.max).then_inc(mx_ok, 1)
                                dve.wait_ge(mx_ok, b * ST + i + 1)
                                dve.tensor_scalar(nmx[:, i:i + 1], mx[:, i:i + 1], -SCALE, None, ALU.mult).then_inc(nmx_ok, 1)
                            if i >= 1:
                                dve.reciprocal(rinv[:, n:n + 1], rs[:, n:n + 1]).then_inc(rinv_ok, 1)
                                dve.wait_ge(rinv_ok, b * ST + n + 1)
                                dve.wait_ge(z_ok, b * ST + n + 1)
                                if n == 0:
                                    dve.wait_ge(out, b * 16)
                                dve.scalar_tensor_tensor(out=x3[:, n, :], in0=z[:, n % 2, 0:D], scalar=rinv[:, n:n + 1],
                                                         in1=x2[u][:, n, :], op0=ALU.mult, op1=ALU.add).then_inc(x3_ok, 1)


E1 = 64
K2 = 2
MLP = 512
TILES = T * K2 // P + E1
QUAD = 4
DUMMY = K2 * T


def gate_top2(nc, g):
    with ExitStack() as ctx:
        sb = lambda n, s, d=F32: ctx.enter_context(nc.sbuf_tensor(n, s, d))
        gate = sb("i_gate", [P, DC, E1])
        x3 = [sb(f"i_x3_{u}", [P, ST, D]) for u in range(2)]
        xn, xnT = sb("i_xn", [P, ST, D]), sb("i_xnT", [P, DC, S])
        st, mv = sb("i_st", [P, ST, 6]), sb("i_mv", [P, ST, 2])
        var, std, rstd, tmp = (sb("i_" + n, [P, ST]) for n in ("var", "std", "rstd", "tmp"))
        lg = sb("i_lg", [P, ST, E1])
        top, at, atf = sb("i_top", [P, ST, 8]), sb("i_at", [P, ST, 8], U32), sb("i_atf", [P, ST, 8])
        dif, ex, ex1 = (sb("i_" + n, [P, ST]) for n in ("dif", "ex", "ex1"))
        w_ = sb("i_w", [P, 2, ST])
        hot = sb("i_hot", [P, K2, ST, E1])
        sel = sb("i_sel", [P, ST, E1])
        run = sb("i_run", [P, ST + 1, E1])
        rk, rkh = sb("i_rk", [P, ST, E1]), sb("i_rkh", [P, K2, ST, E1])
        tp = [ctx.enter_context(nc.psum_tensor(f"i_tp{i}", [P, 4, P], F32)) for i in range(2)]
        gp = ctx.enter_context(nc.psum_tensor("i_gp", [P, ST, E1], F32))
        rp = ctx.enter_context(nc.psum_tensor("i_rp", [P, ST, E1], F32))
        cp = ctx.enter_context(nc.psum_tensor("i_cp", [P, E1], F32))
        w_in, zero_ok = g.sem("i_w_in"), g.sem("i_zero")
        x_in = [g.sem(f"i_x_in{u}") for u in range(2)]
        (stats, var_ok, std_ok, rstd_ok, xn_ok, tp_ok, T_ok, gp_ok, step, ex_ok, sel_ok, rp_ok, out, fin) = (
            g.sem("i_" + n) for n in ("stats", "var", "std", "rstd", "xn", "tp", "T", "gp", "step", "ex", "sel", "rp",
                                      "out", "fin"))
        K = 18 + ST + 16
        tiles = lambda t: t.rearrange("(v u c p) d -> v u p c d", u=2, c=ST, p=P)
        with nc.Block() as block:
            @block.sync
            def _(sp):
                sp.dma_start(gate[:], split_load_w(g.gate1)).then_inc(w_in, 16)
                with sp.Fori(0, B // 2) as v:
                    for u in range(2):
                        sp.wait_ge(xn_ok, v * 2)
                        sp.dma_start(x3[u][:], tiles(g.x3)[v, u]).then_inc(x_in[u], 16)

            @block.gpsimd
            def _(pool):
                pool.memset(run[:, 0, :], 0.0).then_inc(zero_ok, 1)

            @block.tensor
            def _(pe):
                pe.wait_ge(w_in, 16)
                with pe.Fori(0, B) as b:
                    pe.wait_ge(xn_ok, b + 1)
                    for n in range(4):
                        pe.wait_ge(T_ok, b * 4 + max(n - 1, 0))
                        for a in range(4):
                            last = pe.transpose(tp[n % 2][:, a, :], xn[:, 4 * (n % 2) + a, P * (n // 2):P * (n // 2) + P],
                                                g.ident[:])
                        last.then_inc(tp_ok, 1)
                    pe.wait_ge(T_ok, b * 4 + 4)
                    pe.wait_ge(sel_ok, b)
                    for c in range(ST):
                        for k in range(DC):
                            last = pe.matmul(gp[:, c, :], xnT[:, k, P * c:P * c + P], gate[:, k, :],
                                             start=(k == 0), stop=(k == DC - 1))
                    last.then_inc(gp_ok, 1)
                    pe.wait_ge(sel_ok, b + 1)
                    for c in range(ST):
                        pe.matmul(rp[:, c, :], g.tri[:], sel[:, c, :], start=True, stop=False)
                        last = pe.matmul(rp[:, c, :], g.ones[:], run[:, c, :], start=False, stop=True)
                    last.then_inc(rp_ok, 1)
                pe.wait_ge(fin, 1)
                pe.matmul(cp[:], g.ones[:], run[:, 0, :], start=True, stop=True).then_inc(fin, 1)

            @block.scalar
            def _(act):
                with act.Fori(0, B) as b:
                    act.wait_ge(var_ok, b + 1)
                    act.activation(std[:], var[:], ACT.Sqrt).then_inc(std_ok, 1)
                    act.wait_ge(xn_ok, b + 1)
                    act.dma_start(g.xn3.rearrange("(b c p) d -> b p c d", c=ST, p=P)[b], xn[:]).then_inc(out, 16)
                    for n in range(4):
                        act.wait_ge(tp_ok, b * 4 + n + 1)
                        act.copy(xnT[:, n // 2, 512 * (n % 2):512 * (n % 2) + 512],
                                 tp[n % 2][:].rearrange("p a b -> p (a b)")).then_inc(T_ok, 1)
                    act.wait_ge(ex_ok, b * 2 + 1)
                    act.activation(ex[:], dif[:], ACT.Exp).then_inc(ex_ok, 1)
                    act.wait_ge(out, b * 16 + 16)

            @block.vector
            def _(dve):
                dve.wait_ge(zero_ok, 1)
                with dve.Fori(0, B // 2) as v:
                    for u in range(2):
                        b = v * 2 + u
                        n = 0

                        def then(ins, alone=False):
                            nonlocal n
                            n += 1
                            ins.then_inc(step, 1)
                            if alone:
                                wait_alone(dve, g, step, b * K + n)
                            else:
                                dve.wait_ge(step, b * K + n)
                        dve.wait_ge(x_in[u], v * 16 + 16)
                        for c in range(ST):
                            dve.bn_stats(st[:, c, :], x3[u][:, c, :]).then_inc(stats, 1)
                        wait_alone(dve, g, stats, b * (2 * ST) + ST)
                        for c in range(ST):
                            dve.bn_aggr(mv[:, c, :], st[:, c, :]).then_inc(stats, 1)
                        dve.wait_ge(stats, b * (2 * ST) + 2 * ST)
                        dve.tensor_scalar(var[:], mv[:, :, 1], EPS, None, ALU.add).then_inc(var_ok, 1)
                        dve.wait_ge(std_ok, b + 1)
                        sharpen_rstd(dve, rstd_ok, b * 4, rstd, std, var, tmp)
                        dve.wait_ge(out, b * 16)
                        for c in range(ST):
                            last = dve.tensor_scalar(xn[:, c, :], x3[u][:, c, :], mv[:, c, 0:1], rstd[:, c:c + 1],
                                                     ALU.subtract, ALU.mult)
                        last.then_inc(xn_ok, 1)
                        dve.wait_ge(gp_ok, b + 1)
                        then(dve.tensor_copy(lg[:], gp[:]), True)
                        for c in range(ST):
                            last = dve.max(top[:, c, :], lg[:, c, :])
                        then(last, True)
                        for c in range(ST):
                            last = dve.max_index(at[:, c, :], top[:, c, :], lg[:, c, :])
                        then(last)
                        then(dve.tensor_copy(atf[:], at[:]))
                        dve.wait_ge(ex_ok, b * 2)
                        dve.tensor_tensor(dif[:], top[:, :, 1], top[:, :, 0], ALU.subtract).then_inc(ex_ok, 1)
                        dve.wait_ge(rp_ok, b)
                        for k in range(K2):
                            then(dve.tensor_tensor(hot[:, k, :, :], atf[:, :, k].unsqueeze(2).to_broadcast([P, ST, E1]),
                                                   g.iota_f[:, 0:E1].unsqueeze(1).to_broadcast([P, ST, E1]), ALU.is_equal))
                        then(dve.tensor_tensor(sel[:], hot[:, 0, :, :], hot[:, 1, :, :], ALU.add))
                        for c in range(ST):
                            then(dve.tensor_tensor(run[:, c + 1, :], run[:, c, :], sel[:, c, :], ALU.add))
                        dve.sem_inc(sel_ok, 1)
                        dve.wait_ge(ex_ok, b * 2 + 2)
                        then(dve.tensor_scalar(ex1[:], ex[:], 1.0, None, ALU.add))
                        then(dve.reciprocal(w_[:, 0, :], ex1[:]))
                        then(dve.tensor_tensor(w_[:, 1, :], ex[:], w_[:, 0, :], ALU.mult))
                        dve.wait_ge(rp_ok, b + 1)
                        then(dve.tensor_copy(run[:, 0, :], run[:, ST, :]))
                        for k in range(K2):
                            then(dve.tensor_tensor(rkh[:, k, :, :], hot[:, k, :, :], rp[:], ALU.mult))
                            then(dve.tensor_copy(tiled(g.at_f, k, b), atf[:, :, k]))
                            then(dve.tensor_reduce(tiled(g.rank, k, b), rkh[:, k, :, :], AX.X, ALU.add))
                            then(dve.tensor_copy(tiled(g.w_tok, k, b), w_[:, k, :]))
                        assert n <= K
                        if n < K:
                            dve.sem_inc(step, K - n)
                dve.sem_inc(fin, 1)
                dve.wait_ge(fin, 2)
                dve.tensor_copy(g.count[:], cp[:]).then_inc(fin, 1)


def tiled(t, k, b):
    return t.rearrange("p k (b c) -> p k b c", b=B)[:, k, b, :]


def place_rows(nc, g):
    with ExitStack() as ctx:
        sb = lambda n, s, d=F32: ctx.enter_context(nc.sbuf_tensor(n, s, d))
        ci, ti = sb("j_ci", [P, E1], I32), sb("j_ti", [P, E1], I32)
        tf, one, end, beg = (sb("j_" + n, [P, E1]) for n in ("tf", "one", "end", "beg"))
        hit = sb("j_hit", [P, NT, E1])
        rowf = sb("j_rowf", [P, K2, NT])
        row = sb("j_row", [P, K2, NT], I32)
        tok = sb("j_tok", [P, K2, NT], I32)
        tile_f, te_f, cmp_ = sb("j_tile_f", [P, 2]), sb("j_te_f", [P, 2]), sb("j_cmp", [P, 2, E1])
        tile_i, te_i = sb("j_tile_i", [P, 2], I32), sb("j_te_i", [P, 2, 2], I32)
        end_i, quads = sb("j_end_i", [P, E1], I32), sb("j_quads", [P, 1], I32)
        dummy = sb("j_dummy", [TILES // 2, 2, P], I32)
        step, made, cleared, tabled, put = (g.sem("j_" + n) for n in ("step", "made", "cleared", "tabled", "put"))
        with nc.allow_non_contiguous_dma(reason="two short tables"), nc.Block() as block:
            @block.gpsimd
            def _(pool):
                pool.memset(dummy[:], DUMMY).then_inc(made, 1)
                pool.iota(tok[:], pattern=[[T, K2], [P, NT]], base=0, channel_multiplier=1).then_inc(made, 1)
                pool.iota(tile_i[:], pattern=[[P, 2]], base=0, channel_multiplier=1).then_inc(made, 1)
                pool.wait_ge(made, 3)
                pool.wait_ge(cleared, 16)
                pool.wait_ge(step, 6)
                for k in range(K2):
                    for c in range(NT):
                        pool.indirect_dma_start(
                            out=g.row_of, in_=tok[:, k, c:c + 1], in_offset=None,
                            out_offset=bass.IndirectOffsetOnAxis(ap=row[:, k, c:c + 1], axis=0)).then_inc(put, 16)
                pool.wait_ge(put, 16 * K2 * NT)

            @block.sync
            def _(sp):
                sp.wait_ge(made, 1)
                sp.dma_start(g.row_of.rearrange("(q a p) o -> q a (p o)", a=2, p=P), dummy[:]).then_inc(cleared, 16)
                sp.wait_ge(step, 14)
                sp.dma_start(g.tile_expert[:, 0:P, 0].rearrange("s p -> p s"), te_i[:, 0, :]).then_inc(tabled, 16)
                sp.dma_start(g.tile_expert[:, P:TILES, 0].rearrange("s p -> p s"), te_i[0:TILES - P, 1, :]).then_inc(tabled, 16)
                sp.dma_start(g.tile_end, end_i[0:1, :]).then_inc(tabled, 16)
                sp.dma_start(g.quads, quads[0:1, :]).then_inc(tabled, 16)
                sp.wait_ge(tabled, 64)
                sp.wait_ge(cleared, 16)

            @block.vector
            def _(dve):
                n = 0

                def then(ins):
                    nonlocal n
                    n += 1
                    ins.then_inc(step, 1)
                    dve.wait_ge(step, n)
                dve.memset(one[:], 1.0)
                then(dve.tensor_scalar(ci[:], g.count[:], float(P - 1), None, ALU.add))
                then(dve.tensor_scalar(ti[:], ci[:], 7, None, ALU.logical_shift_right))
                then(dve.tensor_copy(tf[:], ti[:]))
                then(dve.tensor_tensor_scan(end[:], one[:], tf[:], 0.0, ALU.mult, ALU.add))
                then(dve.tensor_tensor(beg[:], end[:], tf[:], ALU.subtract))
                for k in range(K2):
                    dve.tensor_tensor(hit[:], g.at_f[:, k, :].unsqueeze(2).to_broadcast([P, NT, E1]),
                                      g.iota_f[:, 0:E1].unsqueeze(1).to_broadcast([P, NT, E1]), ALU.is_equal).then_inc(g.hit_step, 1)
                    dve.wait_ge(g.hit_step, 3 * k + 1)
                    dve.tensor_tensor(hit[:], hit[:], beg[:].unsqueeze(1).to_broadcast([P, NT, E1]), ALU.mult).then_inc(g.hit_step, 1)
                    dve.wait_ge(g.hit_step, 3 * k + 2)
                    dve.tensor_reduce(rowf[:, k, :], hit[:], AX.X, ALU.add).then_inc(g.hit_step, 1)
                    dve.wait_ge(g.hit_step, 3 * k + 3)
                then(dve.scalar_tensor_tensor(out=row[:], in0=rowf[:], scalar=float(P), in1=g.rank, op0=ALU.mult, op1=ALU.add))
                dve.wait_ge(made, 3)
                then(dve.tensor_copy(tile_f[:], tile_i[:]))
                then(dve.tensor_tensor(cmp_[:], tile_f[:].unsqueeze(2).to_broadcast([P, 2, E1]),
                                       end[:].unsqueeze(1).to_broadcast([P, 2, E1]), ALU.is_ge))
                then(dve.tensor_reduce(te_f[:], cmp_[:], AX.X, ALU.add))
                then(dve.tensor_scalar(te_i[:, :, 0], te_f[:], float(E1 - 1), None, ALU.min))
                then(dve.tensor_scalar(te_i[:, :, 1], te_i[:, :, 0], QUAD - 1, None, ALU.bitwise_and))
                then(dve.tensor_copy(end_i[:], end[:]))
                then(dve.tensor_scalar(ci[:, 0:1], end[:, E1 - 1:E1], -1.0, None, ALU.add))
                then(dve.tensor_scalar(quads[:], ci[:, 0:1], 2, None, ALU.logical_shift_right))


def expert_rows(nc, g):
    MC = MLP // P
    R = QUAD
    with ExitStack() as ctx:
        g.ctx = ctx
        sb = lambda n, s, d=F32: ctx.enter_context(nc.sbuf_tensor(n, s, d))
        te = sb("k_te", [1, 2, TILES], I32)
        end = sb("k_end", [1, E1], I32)
        nq = sb("k_nq", [1, 1], I32)
        ids = sb("k_ids", [TILES // R, R, P], I32)
        idf = sb("k_idf", [TILES // R, R, P])
        dst = sb("k_dst", [P, TILES // R, R], I32)
        src = sb("k_src", [P, TILES // R, R], I32)
        di = [sb(f"k_di{u}", [P, 1], I32) for u in range(R)]
        si = [sb(f"k_si{u}", [P, 1], I32) for u in range(R)]
        w01 = sb("k_w01", [P, R, 2, DC, MLP])
        wo = sb("k_wo", [P, R, MC, D])
        xg = [sb(f"k_xg{u}", [P, D]) for u in range(R)]
        xT = [sb(f"k_xT{u}", [P, DC, P]) for u in range(2)]
        sl = sb("k_sl", [P, MLP])
        it = [sb(f"k_it{u}", [P, MLP]) for u in range(2)]
        iT = sb("k_iT", [P, MC, P])
        y = [sb(f"k_y{u}", [P, D]) for u in range(R)]
        xp = ctx.enter_context(nc.psum_tensor("k_xp", [P, 4, P], F32))
        h = [ctx.enter_context(nc.psum_tensor(f"k_h{u}", [P, 2, MLP], F32)) for u in range(2)]
        ip = ctx.enter_context(nc.psum_tensor("k_ip", [P, MC, P], F32))
        yp = [ctx.enter_context(nc.psum_tensor(f"k_yp{u}", [P, D], F32)) for u in range(2)]
        t_in, ids_f, id_ps, ids_ok = (g.sem("k_" + n) for n in ("t_in", "ids_f", "id_ps", "ids_ok"))
        w_in = g.sem("k_w_in")
        x_in = [g.sem(f"k_x_in{u}") for u in range(R)]
        put = [g.sem(f"k_put{u}") for u in range(R)]
        si_ok, di_ok, xp_ok, xT_ok, h_ok, sl_ok, it_ok, ip_ok, iT_ok, yp_ok, y_ok = (
            g.sem("k_" + n) for n in ("si", "di", "xp", "xT", "h", "sl", "it", "ip", "iT", "yp", "y"))
        W_DMAS = 3 * 16
        NTAB = 16 * 5

        def last_quad(eng):
            eng.wait_ge(t_in, NTAB)
            return eng.value_load(nq[0:1, 0:1], min_val=T * K2 // P // R - 1, max_val=TILES // R - 1)

        with nc.Block() as block:
            @block.sync
            def _(sp):
                sp.dma_start(te[:, 0, :], g.tile_expert[0].rearrange("t a -> a t")).then_inc(t_in, 16)
                sp.dma_start(te[:, 1, :], g.tile_expert[1].rearrange("t a -> a t")).then_inc(t_in, 16)
                sp.dma_start(end[:], g.tile_end).then_inc(t_in, 16)
                sp.dma_start(nq[:], g.quads).then_inc(t_in, 16)
                sp.dma_start(ids[:], g.row_of.rearrange("(q a p) o -> q a (p o)", a=R, p=P)).then_inc(t_in, 16)
                w0_e = g.w0.rearrange("(v u) (c p) n -> v u p c n", u=R, p=P)
                w1_e = g.w1.rearrange("(v u) (c p) n -> v u p c n", u=R, p=P)
                wo_e = g.wo.rearrange("(v u) (c p) n -> v u p c n", u=R, p=P)

                def load(v, u):
                    sp.dma_start(w01[:, u, 0, :, :], w0_e[v, u]).then_inc(w_in, 16)
                    sp.dma_start(w01[:, u, 1, :, :], w1_e[v, u]).then_inc(w_in, 16)
                    sp.dma_start(wo[:, u, :, :], wo_e[v, u]).then_inc(w_in, 16)
                for u in range(R):
                    if u:
                        sp.wait_ge(w_in, W_DMAS * u)
                    load(0, u)
                sp.wait_ge(t_in, NTAB)
                ends = end[:].rearrange("a (v u) -> a v u", u=R)
                with sp.Fori(1, E1 // R) as v:
                    for u in range(R):
                        last = sp.value_load(ends[:, v - 1, u:u + 1], min_val=0, max_val=TILES)
                        sp.wait_ge(yp_ok, last)
                        sp.wait_ge(w_in, (v * R + u) * W_DMAS)
                        load(v, u)
                sp.wait_ge(w_in, E1 * W_DMAS)

            @block.gpsimd
            def _(pool):
                def gather(q, u):
                    if isinstance(q, int):
                        pool.wait_ge(ids_ok, 2)
                    else:
                        wait_alone(pool, g, xp_ok, q * R + u - 3)
                    pool.tensor_copy(si[u][:], src[:, q, u:u + 1]).then_inc(si_ok, 1)
                    wait_alone(pool, g, si_ok, q * R + u + 1)
                    pool.indirect_dma_start(
                        out=xg[u][:], out_offset=None, in_=g.xn3,
                        in_offset=bass.IndirectOffsetOnAxis(ap=si[u][:], axis=0)).then_inc(x_in[u], 16)

                def store(q, u):
                    wait_alone(pool, g, put[u], q * 16)
                    pool.tensor_copy(di[u][:], dst[:, q, u:u + 1]).then_inc(di_ok, 1)
                    wait_alone(pool, g, di_ok, q * R + u + 1)
                    wait_alone(pool, g, y_ok, q * R + u + 1)
                    put_rows(pool, g, y[u], di[u], put[u])
                m = last_quad(pool)
                for u in range(R):
                    gather(0, u)
                with pool.Fori(1, m + 1) as q:
                    for u in range(R):
                        store(q - 1, u)
                        gather(q, u)
                for u in range(R):
                    store(m, u)
                for u in range(R):
                    wait_alone(pool, g, put[u], m * 16 + 16)

            @block.tensor
            def _(pe):
                pe.wait_ge(ids_f, 1)
                for a in range(R):
                    last = pe.transpose(xp[:, a, 0:TILES // R], idf[:, a, :], g.ident[0:TILES // R, 0:TILES // R])
                last.then_inc(id_ps, 1)
                pe.wait_ge(ids_ok, 2)
                m = last_quad(pe)

                def x_by_column(q, u):
                    pe.wait_ge(x_in[u], q * 16 + 16)
                    pe.wait_ge(xT_ok, q * R + u)
                    for k in range(DC):
                        last = pe.transpose(xp[:, k, :], xg[u][:, P * k:P * k + P], g.ident[:])
                    last.then_inc(xp_ok, 1)

                def last_product(i, q, u, place):
                    pe.wait_ge(iT_ok, i - 1)
                    pe.wait_ge(y_ok, max(i - 3, 0) if isinstance(i, int) else i - 3)
                    for k in range(MC):
                        last = pe.matmul(yp[u % 2][:], iT[:, k, :], wo[:, place, k, :], start=(k == 0), stop=(k == MC - 1))
                    last.then_inc(yp_ok, 1)

                def product_by_column(i, u):
                    pe.wait_ge(it_ok, i)
                    for k in range(MC):
                        last = pe.transpose(ip[:, k, :], it[u % 2][:, P * k:P * k + P], g.ident[:])
                    last.then_inc(ip_ok, 1)

                def first_products(q, u, e, place):
                    i = q * R + u
                    pe.wait_ge(xT_ok, i + 1)
                    pe.wait_ge(w_in, e * W_DMAS + W_DMAS)
                    for m in range(2):
                        for k in range(DC):
                            last = pe.matmul(h[u % 2][:, m, :], xT[u % 2][:, k, :], w01[:, place, m, k, :],
                                             start=(k == 0), stop=(k == DC - 1))
                    last.then_inc(h_ok, 1)

                def expert_of(q, u):
                    at = te[:].rearrange("o s (q u) -> o s q u", u=R)
                    return (pe.value_load(at[:, 0, q, u:u + 1], min_val=0, max_val=E1 - 1),
                            pe.value_load(at[:, 1, q, u:u + 1], min_val=0, max_val=R - 1))

                def place_before(q, u, back):
                    at = te[:].rearrange("o s (q u) -> o s q u", u=R)
                    q, u = (q, u - back) if u >= back else (q - 1, u - back + R)
                    return pe.value_load(at[:, 1, q, u:u + 1], min_val=0, max_val=R - 1)

                def tile(q, u, first=False):
                    e, place = expert_of(q, u)
                    if not first or u >= 2:
                        before = place_before(q, u, 2)
                    x_by_column(q, u)
                    if not first or u >= 2:
                        last_product(q * R + u, q, u, before)
                    if not first or u >= 1:
                        product_by_column(q * R + u, u + 1)
                    first_products(q, u, e, place)
                for u in range(R):
                    tile(0, u, True)
                with pe.Fori(1, m + 1) as q:
                    for u in range(R):
                        tile(q, u)
                last_product(m * R + R, m, 0, place_before(m, R, 2))
                product_by_column(m * R + R, 1)
                last_product(m * R + R + 1, m, 1, place_before(m, R + 1, 2))

            @block.scalar
            def _(act):
                m = last_quad(act)

                def by_column(i):
                    act.wait_ge(ip_ok, i)
                    act.copy(iT[:].rearrange("p a b -> p (a b)"), ip[:].rearrange("p a b -> p (a b)")).then_inc(iT_ok, 1)

                def tile(q, u, first=False):
                    i = q * R + u
                    if not first or u >= 1:
                        by_column(i)
                    act.wait_ge(h_ok, i + 1)
                    act.wait_ge(it_ok, i)
                    act.activation(sl[:], h[u % 2][:, 0, :], ACT.Silu).then_inc(sl_ok, 1)
                for u in range(R):
                    tile(0, u, True)
                with act.Fori(1, m + 1) as q:
                    for u in range(R):
                        tile(q, u)
                by_column(m * R + R)

            @block.vector
            def _(dve):
                dve.wait_ge(t_in, NTAB)
                dve.tensor_copy(idf[:], ids[:]).then_inc(ids_f, 1)
                dve.wait_ge(id_ps, 1)
                dve.tensor_copy(dst[:].rearrange("p q a -> p a q"), xp[:, :, 0:TILES // R]).then_inc(ids_ok, 1)
                dve.wait_ge(ids_ok, 1)
                dve.tensor_scalar(src[:], dst[:], T - 1, None, ALU.bitwise_and).then_inc(ids_ok, 1)
                dve.wait_ge(ids_ok, 2)
                m = last_quad(dve)

                def y_out(q, u):
                    dve.wait_ge(yp_ok, q * R + u + 1)
                    dve.wait_ge(put[u], q * 16)
                    dve.tensor_copy(y[u][:], yp[u % 2][:]).then_inc(y_ok, 1)

                def tile(q, u, first=False):
                    i = q * R + u
                    dve.wait_ge(xp_ok, i + 1)
                    dve.tensor_copy(xT[u % 2][:], xp[:, 0:DC, :]).then_inc(xT_ok, 1)
                    if not first or u >= 2:
                        y_out(*((q, u - 2) if u >= 2 else (q - 1, u + R - 2)))
                    dve.wait_ge(sl_ok, i + 1)
                    dve.tensor_tensor(it[u % 2][:], h[u % 2][:, 1, :], sl[:], ALU.mult).then_inc(it_ok, 1)
                for u in range(R):
                    tile(0, u, True)
                with dve.Fori(1, m + 1) as q:
                    for u in range(R):
                        tile(q, u)
                y_out(m, R - 2)
                y_out(m, R - 1)


def put_rows(pool, g, y, di, put):
    pool.indirect_dma_start(out=g.y_tok, in_=y[:], in_offset=None,
                            out_offset=bass.IndirectOffsetOnAxis(ap=di[:], axis=0),
                            bounds_check=K2 * T - 1, oob_is_err=False).then_inc(put, 16)


def combine(nc, g):
    with ExitStack() as ctx:
        sb = lambda n, s, d=F32: ctx.enter_context(nc.sbuf_tensor(n, s, d))
        x = [sb(f"l_x{u}", [P, ST, D]) for u in range(2)]
        ya = [sb(f"l_ya{u}", [P, ST, D]) for u in range(2)]
        yb = [sb(f"l_yb{u}", [P, ST, D]) for u in range(2)]
        wt = sb("l_wt", [P, K2, NT])
        in_ = [g.sem(f"l_in{u}") for u in range(2)]
        out = [g.sem(f"l_out{u}") for u in range(2)]
        one, two, wts = g.sem("l_one"), g.sem("l_two"), g.sem("l_wts")
        tiles = lambda t: t.rearrange("(v u c p) d -> v u p c d", u=2, c=ST, p=P)
        w_b = [sb(f"l_w{u}", [P, K2, ST]) for u in range(2)]
        with nc.Block() as block:
            @block.sync
            def _(sp):
                with sp.Fori(0, B // 2) as v:
                    for u in range(2):
                        sp.wait_ge(out[u], v * 16)
                        sp.dma_start(x[u][:], tiles(g.x3)[v, u]).then_inc(in_[u], 16)
                        sp.dma_start(ya[u][:], tiles(g.y_tok[0:T, :])[v, u]).then_inc(in_[u], 16)
                        sp.dma_start(yb[u][:], tiles(g.y_tok[T:2 * T, :])[v, u]).then_inc(in_[u], 16)

            @block.scalar
            def _(act):
                with act.Fori(0, B // 2) as v:
                    for u in range(2):
                        act.wait_ge(two, v * 2 + u + 1)
                        act.dma_start(tiles(g.out)[v, u], x[u][:]).then_inc(out[u], 16)
                for u in range(2):
                    act.wait_ge(out[u], 16 * (B // 2))

            @block.vector
            def _(dve):
                with dve.Fori(0, B // 2) as v:
                    for u in range(2):
                        b = v * 2 + u
                        dve.wait_ge(in_[u], v * 48 + 48)
                        for k in range(K2):
                            last = dve.tensor_copy(w_b[u][:, k, :], tiled(g.w_tok, k, b))
                        last.then_inc(wts, 1)
                        dve.wait_ge(wts, b + 1)
                        for c in range(ST):
                            last = dve.scalar_tensor_tensor(out=x[u][:, c, :], in0=ya[u][:, c, :], scalar=w_b[u][:, 0, c:c + 1],
                                                            in1=x[u][:, c, :], op0=ALU.mult, op1=ALU.add)
                        last.then_inc(one, 1)
                        dve.wait_ge(one, b + 1)
                        for c in range(ST):
                            last = dve.scalar_tensor_tensor(out=x[u][:, c, :], in0=yb[u][:, c, :], scalar=w_b[u][:, 1, c:c + 1],
                                                            in1=x[u][:, c, :], op0=ALU.mult, op1=ALU.add)
                        last.then_inc(two, 1)


def two_layers(nc, ins, out):
    with ExitStack() as ctx:
        def sb(name, shape, dt=F32):
            return ctx.enter_context(nc.sbuf_tensor(name, shape, dt))

        def dram(name, shape, dt=F32):
            return nc.dram_tensor(name, shape, dt, kind="Internal").ap()

        g = Shared()
        sems = []

        def sem(name):
            sems.append(nc.alloc_semaphore(name=name))
            return sems[-1]

        g.sem = sem
        g.passed = sem("passed")
        g.x, g.Wq, g.bq, g.Wk, g.bk, g.Wv, g.bv, g.Wo, g.bo, g.sample_idx = (
            ins["L0_attn_" + n] for n in ("x", "Wq", "bq", "Wk", "bk", "Wv", "bv", "Wo", "bo", "sample_idx"))
        g.gate, g.W1, g.b1, g.W2, g.b2, g.Ws1, g.bs1, g.Ws2, g.bs2 = (
            ins["L0_ffn_" + n] for n in ("gate", "W1", "b1", "W2", "b2", "Ws1", "bs1", "Ws2", "bs2"))
        g.Wq1, g.bq1, g.Wk1, g.bk1, g.Wv1, g.bv1 = (ins["L1_attn_" + n] for n in ("Wq", "bq", "Wk", "bk", "Wv", "bv"))
        g.gate1, g.w0, g.w1, g.wo = (ins["L1_ffn_" + n] for n in ("gate_kernel", "w0", "w1", "wo"))
        g.out = out.rearrange("b s d -> (b s) d")

        g.ident, g.ones, g.tri = sb("ident", [P, P]), sb("ones", [P, P]), sb("tri", [P, P])
        g.iota_i, g.iota_f = sb("iota_i", [P, P], I32), sb("iota_f", [P, P])
        g.part_i, g.part_f = sb("part_i", [P, 1], I32), sb("part_f", [P, 1])
        g.probs = sb("probs", [P, E0, NT])[:]
        g.elist = sb("elist", [P, E0, CAP // P], I32)
        g.at_f, g.rank, g.w_tok = (sb(n, [P, K2, NT])[:] for n in ("at_f", "rank", "w_tok"))
        g.count = sb("count", [P, E1])

        g.xnT = dram("xnT", (B, P, DC, S))
        g.q_rows = dram("q_rows", (T * H, HD))
        g.q16, g.k16 = dram("q16", (B, 2, D, S), F16), dram("k16", (B, 2, D, U), F16)
        g.m_rows, g.sel_rows = dram("m_rows", (P, S)), dram("sel_rows", (P * TOP, 1), I32)
        g.attn_rows = dram("attn_rows", (T * H, HD))
        g.x1, g.x2, g.x3 = (dram(n, (T, D)) for n in ("x1", "x2", "x3"))
        g.tab, g.xnT1 = dram("tab", (T, ROW)), dram("xnT1", (B, P, DC, S))
        g.xn3, g.y_tok = dram("xn3", (T, D)), dram("y_tok", (K2 * T, D))
        g.row_of, g.tile_expert = dram("row_of", (TILES * P, 1), I32), dram("tile_expert", (2, TILES, 1), I32)
        g.tile_end, g.quads = dram("tile_end", (1, E1), I32), dram("quads", (1, 1), I32)

        constants(nc, g)
        project_and_score(nc, g)
        pick_queries(nc, g)
        attend_selected(nc, g)
        add_attention_and_gate(nc, g)
        shared_ffn_and_choice(nc, g)
        expert_ffn(nc, g)
        nc.clear_and_free_semaphores(sems)
        nc.all_engine_barrier()
        g.passed, g.hit_step = sem("passed1"), sem("hit_step")
        causal_attention(nc, g)
        gate_top2(nc, g)
        place_rows(nc, g)
        expert_rows(nc, g)
        combine(nc, g)


_INS = (["L0_attn_" + n for n in ("x", "Wq", "bq", "Wk", "bk", "Wv", "bv", "Wo", "bo", "sample_idx")]
        + ["L0_ffn_" + n for n in ("gate", "W1", "b1", "W2", "b2", "Ws1", "bs1", "Ws2", "bs2")]
        + ["L1_attn_" + n for n in ("Wq", "bq", "Wk", "bk", "Wv", "bv")]
        + ["L1_ffn_" + n for n in ("gate_kernel", "w0", "w1", "wo")])
_OUT = ((8, 1024, 256), "float32")


def kernel(**inputs):
    import numpy as _np
    import concourse.bacc as _bacc
    from concourse import mybir as _mybir
    from concourse.bass_utils import run_bass_kernel_spmd as _run

    nc = _bacc.Bacc("TRN2", target_bir_lowering=False, num_devices=1)
    arrays, args = {}, {}
    for name in _INS:
        a = _np.ascontiguousarray(inputs[name])
        arrays[f"in_{name}_dram"] = a
        args[name] = nc.dram_tensor(f"in_{name}_dram", a.shape, _mybir.dt.from_np(a.dtype), kind="ExternalInput").ap()
    shape, dtype = _OUT
    out = nc.dram_tensor("out_0_dram", shape, _mybir.dt.from_np(_np.dtype(dtype)), kind="ExternalOutput").ap()
    two_layers(nc, args, out)
    r = _run(nc, [arrays], core_ids=[0])
    return r.results[0]["out_0_dram"]
```

```python
import concourse.bass as bass
from concourse import mybir
from contextlib import ExitStack

F32 = mybir.dt.float32
F16 = mybir.dt.float16
I32 = mybir.dt.int32
U32 = mybir.dt.uint32
ALU = mybir.AluOpType
ACT = mybir.ActivationFunctionType
AX = mybir.AxisListType


class Shared:
    pass


P = 128
B = 8
S = 1024
D = 256
DC = D // P
ST = S // P
T = B * S
NT = T // P
H = 16
HD = D // H
U = 512
UT = U // P
TOP = 34
EPS = 1e-5
QK = 16.0


WS = 256.0
PARTS = ((0, 0), (0, 1), (1, 0))


def product(pe, out, left, right, first, last_, parts=PARTS):
    for r, (i, j) in enumerate(parts):
        ins = pe.matmul(out, left[i], right[j], start=first and r == 0, stop=last_ and r == len(parts) - 1)
    return ins


def wait_alone(eng, g, sem, value):
    eng.wait_ge(sem, value)
    eng.sem_inc(g.passed, 1)


def load_ahead(eng, pairs, used, per, load):
    for u in range(2):
        load(0, u)
    with eng.Fori(1, pairs) as v:
        for u in range(2):
            eng.wait_ge(used, v * (2 * per) - (1 - u) * per)
            load(v, u)


def in_steps(eng, one):
    one(0, 0, 0)
    with eng.Fori(0, B // 2 - 1) as v:
        one(v * 2 + 1, 1, v)
        one(v * 2 + 2, 0, v + 1)
    one(B - 1, 1, B // 2 - 1)
    one(B, 0, B // 2)


def halves(b):
    return not isinstance(b, int) or b < B, not isinstance(b, int) or b > 0


def split_load_w(w):
    return w.rearrange("(c p) n -> p c n", p=P)


def sharpen_rstd(dve, sem, done, rstd, std, var, tmp):
    rstd, std, var, tmp = rstd[:], std[:], var[:], tmp[:]
    dve.reciprocal(rstd, std).then_inc(sem, 1)
    dve.wait_ge(sem, done + 1)
    dve.tensor_tensor(tmp, rstd, rstd, ALU.mult).then_inc(sem, 1)
    dve.wait_ge(sem, done + 2)
    dve.scalar_tensor_tensor(out=tmp, in0=tmp, scalar=-0.5, in1=var, op0=ALU.mult, op1=ALU.mult).then_inc(sem, 1)
    dve.wait_ge(sem, done + 3)
    dve.scalar_tensor_tensor(out=rstd, in0=tmp, scalar=1.5, in1=rstd, op0=ALU.add, op1=ALU.mult).then_inc(sem, 1)
    dve.wait_ge(sem, done + 4)


def constants(nc, g):
    made = g.sem("const_made")
    filled = g.sem("const_filled")
    with nc.Block() as block:
        @block.gpsimd
        def _(pool):
            pool.memset(g.ones[:], 1.0).then_inc(filled, 1)
            pool.memset(g.ident[:], 0.0).then_inc(filled, 1)
            pool.wait_ge(filled, 2)
            pool.affine_select(out=g.ident[:], in_=g.ident[:], compare_op=ALU.not_equal, fill=1.0, base=0,
                               pattern=[[-1, P]], channel_multiplier=1).then_inc(made, 1)
            pool.affine_select(out=g.tri[:], in_=g.ones[:], compare_op=ALU.is_gt, fill=0.0, base=0,
                               pattern=[[1, P]], channel_multiplier=-1).then_inc(made, 1)
            pool.iota(g.iota_i[:], pattern=[[1, P]], base=0, channel_multiplier=0).then_inc(made, 1)
            pool.iota(g.part_i[:], pattern=[[0, 1]], base=0, channel_multiplier=1).then_inc(made, 1)

        @block.vector
        def _(dve):
            dve.wait_ge(made, 4)
            dve.tensor_copy(g.iota_f[:], g.iota_i[:])
            dve.tensor_copy(g.part_f[:], g.part_i[:])


def project_and_score(nc, g):
    NX = ST + UT
    K3 = 3 * HD
    PARTS = ((0, 0), (0, 1), (1, 0))
    HG = 2
    NG = ST * H // HG
    with ExitStack() as ctx:
        sb = lambda n, s, d=F32: ctx.enter_context(nc.sbuf_tensor(n, s, d))
        wq = sb("a_wq", [P, DC, D])
        wk = sb("a_wk", [P, DC, D])
        wqs, wks = ([sb(f"a_{n}s{i}", [P, DC, D], F16) for i in range(2)] for n in ("wq", "wk"))
        bqk = sb("a_bqk", [P, 2, DC])
        bqk_s = sb("a_bqk_s", [P, 2, DC])
        idx = sb("a_idx", [P, UT], I32)
        xt = [sb(f"a_xt{u}", [P, NX, D]) for u in range(2)]
        xn = sb("a_xn", [P, NX, D])
        st = sb("a_st", [P, NX, 6])
        mv = sb("a_mv", [P, NX, 2])
        var = sb("a_var", [P, NX])
        std = sb("a_std", [P, NX])
        rstd = sb("a_rstd", [P, NX])
        tmp = sb("a_tmp", [P, NX])
        x32 = [sb(f"a_x32_{i}", [P, 512]) for i in range(2)]
        xs = [sb(f"a_xs{i}", [P, DC, NX * P], F16) for i in range(2)]
        q32 = sb("a_q32", [P, DC, S])
        q16 = [sb(f"a_q16_{i}", [P, DC, S], F16) for i in range(2)]
        k32 = sb("a_k32", [P, DC, U])
        kc = sb("a_kc", [P, DC, U])
        k16 = [sb(f"a_k16_{i}", [P, DC, U], F16) for i in range(2)]
        ksum = sb("a_ksum", [P, DC])
        kmean = sb("a_kmean", [P, DC])
        qrow = sb("a_qrow", [P, ST, D])
        qs = [sb(f"b_qs{u}", [K3, H, S], F16) for u in range(2)]
        ks = [sb(f"b_ks{u}", [K3, H, U], F16) for u in range(2)]
        m = [sb(f"b_m{u}", [P, ST, H]) for u in range(2)]
        mT = sb("b_mT", [H, S])
        tp = [ctx.enter_context(nc.psum_tensor(f"a_tp{i}", [P, 4, P], F32)) for i in range(2)]
        pj = [ctx.enter_context(nc.psum_tensor(f"a_pj{i}", [P, 512], F32)) for i in range(2)]
        sc = [ctx.enter_context(nc.psum_tensor(f"b_sc{i}", [P, HG, U], F32)) for i in range(2)]
        w_in, idx_in, idx_next = g.sem("a_w_in"), g.sem("a_idx_in"), g.sem("a_idx_next")
        x_in = [g.sem(f"a_x_in{u}") for u in range(2)]
        rows_in = g.sem("a_rows_in")
        bias_ok = g.sem("a_bias_ok")
        stats, var_ok, std_ok, rstd_ok, xn_ok = (g.sem("a_" + n) for n in ("stats", "var", "std", "rstd", "xn"))
        tp_ok, T_ok, pj_ok, q_ok, k_ok = (g.sem("a_" + n) for n in ("tp", "T", "pj", "q", "k"))
        lo_ok, stored = g.sem("a_lo"), g.sem("a_stored")
        w_hi, w_lo, x_lo = g.sem("a_w_hi"), g.sem("a_w_lo"), g.sem("a_x_lo")
        s_in = [g.sem(f"b_in{u}") for u in range(2)]
        sc_ok, m_ok, mtp_ok, mT_ok, mT_out = (g.sem("b_" + n) for n in ("sc", "m", "mtp", "mT", "mT_out"))
        NS = 7
        NTC = 16
        x_b = g.x.rearrange("(v u) (c p) d -> v u p c d", u=2, p=P)
        x_rows = g.x.rearrange("b s d -> (b s) d")
        q_rows_b = g.q_rows.rearrange("(b c p h) e -> b p c (h e)", b=B, p=P, h=H)
        qv = g.q16.rearrange("b i (h e) t -> b i e h t", e=HD)
        kv = g.k16.rearrange("b i (h e) t -> b i e h t", e=HD)
        PE_AT = [22 + i for i in range(6)] + [30 + 2 * i // 3 for i in range(12)] + [40 + i for i in range(4)]
        M_AT = (1, 2)

        def steps(one):
            one(0, None, 0, None)
            one(1, 0, 1, 0)
            return lambda v: (one(v * 2 + 2, v * 2 + 1, 0, 1), one(v * 2 + 3, v * 2 + 2, 1, 0))
        with nc.allow_non_contiguous_dma(reason="bias columns, 256 words"), nc.Block() as block:
            @block.sync
            def _(sp):
                sp.dma_start(wq[:], split_load_w(g.Wq)).then_inc(w_in, 16)
                sp.dma_start(wk[:], split_load_w(g.Wk)).then_inc(w_in, 16)
                sp.dma_start(bqk[:, 0, :], g.bq.rearrange("(c p) -> p c", p=P)).then_inc(w_in, 16)
                sp.dma_start(bqk[:, 1, :], g.bk.rearrange("(c p) -> p c", p=P)).then_inc(w_in, 16)
                sp.dma_start(idx[:], g.sample_idx.rearrange("(c p) -> p c", p=P)).then_inc(idx_in, 16)
                with sp.Fori(0, B // 2) as v:
                    for u in range(2):
                        sp.wait_ge(xn_ok, v * 2)
                        sp.dma_start(xt[u][:, 0:ST, :], x_b[v, u]).then_inc(x_in[u], 16)

            @block.gpsimd
            def _(pool):
                pool.wait_ge(idx_in, 16)
                with pool.Fori(0, B // 2) as v:
                    for u in range(2):
                        a = v * 2 + u
                        wait_alone(pool, g, xn_ok, v * 2)
                        for c in range(UT):
                            pool.indirect_dma_start(
                                out=xt[u][:, ST + c, :], out_offset=None, in_=x_rows,
                                in_offset=bass.IndirectOffsetOnAxis(ap=idx[:, c:c + 1], axis=0)).then_inc(rows_in, 16)
                        wait_alone(pool, g, rows_in, a * (16 * UT) + 16 * UT)
                        pool.tensor_scalar(idx[:], idx[:], float(S), None, ALU.add).then_inc(idx_next, 1)
                        wait_alone(pool, g, idx_next, a + 1)
                        for n in range(6):
                            wait_alone(pool, g, T_ok, a * NTC + 2 * n + 2)
                            at = (n // 3, slice(512 * (n % 3), 512 * (n % 3) + 512))
                            pool.tensor_tensor(xs[1][:, at[0], at[1]], x32[n % 2][:], xs[0][:, at[0], at[1]],
                                               ALU.subtract).then_inc(x_lo, 1)
                        pool.wait_ge(stored, a * (16 * NS))
                        for n in range(2):
                            pool.wait_ge(q_ok, a * 8 + 4 * n + 4)
                            pool.tensor_tensor(q16[1][:, n, :], q32[:, n, :], q16[0][:, n, :], ALU.subtract).then_inc(lo_ok, 1)
                        pool.wait_ge(k_ok, a * 7 + 7)
                        pool.tensor_tensor(k16[1][:], kc[:], k16[0][:], ALU.subtract).then_inc(lo_ok, 1)

            @block.tensor
            def _(pe):
                def piece(p, a):
                    if p < 6:
                        if p == 0:
                            pe.wait_ge(xn_ok, a + 1)
                        pe.wait_ge(T_ok, a * NTC + 2 * max(p - 1, 0))
                        for j in range(4):
                            last = pe.transpose(tp[p % 2][:, j, :], xn[:, 4 * (p % 3) + j, P * (p // 3):P * (p // 3) + P],
                                                g.ident[:])
                        last.then_inc(tp_ok, 1)
                    elif p < 18:
                        n, k = (p - 6) // 2, (p - 6) % 2
                        ws, mm = (wqs, n // 2) if n < 4 else (wks, n - 4)
                        t0 = 512 * (n % 2) if n < 4 else S
                        if p == 6:
                            pe.wait_ge(x_lo, a * 6 + 6)
                            pe.wait_ge(k_ok, a * 7)
                        if k == 0 and n >= 1:
                            pe.wait_ge(q_ok, a * 8 + 2 * min(n - 1, 4))
                            if n == 1:
                                pe.wait_ge(k_ok, a * 7)
                        last = product(pe, pj[n % 2][:], [w[:, k, P * mm:P * mm + P] for w in ws],
                                       [x[:, k, t0:t0 + 512] for x in xs], k == 0, k == DC - 1)
                        if k == DC - 1:
                            last.then_inc(pj_ok, 1)
                    else:
                        n = p - 18
                        pe.wait_ge(q_ok, a * 8 + 8)
                        pe.wait_ge(T_ok, a * NTC + (10, 12, 13, 14)[n])
                        for j in range(4):
                            c, k = 2 * n + j // 2, j % 2
                            last = pe.transpose(tp[n % 2][:, j, :], q32[:, k, P * c:P * c + P], g.ident[:])
                        last.then_inc(tp_ok, 1)

                def turn(n, b, ub):
                    if n == 0:
                        pe.wait_ge(m_ok, b * NG + NG)
                    pe.wait_ge(mT_ok, b * 2 + n)
                    for c in range(4):
                        last = pe.transpose(tp[n][0:H, c, :], m[ub][:, 4 * n + c, :], g.ident[:])
                    last.then_inc(mtp_ok, 1)

                def one(a, b, ua, ub):
                    if b is None:
                        for p in range(len(PE_AT)):
                            piece(p, a)
                        return
                    for t in range(NG):
                        c, h0 = t * HG // H, t * HG % H
                        if t == 0:
                            pe.wait_ge(s_in[ub], 96 * ((b - ub) // 2 + 1) if isinstance(b, int) else loads_of(b, ub))
                        pe.wait_ge(m_ok, b * NG + max(t - 1, 0))
                        for j in range(HG):
                            last = pe.matmul(sc[t % 2][:, j, :], qs[ub][:, h0 + j, P * c:P * c + P],
                                             ks[ub][:, h0 + j, :], start=True, stop=True)
                        last.then_inc(sc_ok, 1)
                        if t in M_AT and not (isinstance(b, int) and b == 0):
                            if t == M_AT[0]:
                                pe.wait_ge(T_ok, b * NTC + NTC)
                            turn(M_AT.index(t), b - 1, 1 - ub)
                        if t == PE_AT[0] and a is not None and not (isinstance(b, int) and b == 0):
                            pe.wait_ge(mT_ok, b * 2)
                        for p in range(len(PE_AT)):
                            if PE_AT[p] == t and a is not None:
                                piece(p, a)
                pe.wait_ge(w_lo, 2)
                loop = steps(one)
                with pe.Fori(0, B // 2 - 1) as v:
                    loads_of = lambda b, ub: v * 96 + (96 if ub else 192)
                    loop(v)
                one(None, B - 1, None, 1)
                turn(0, B - 1, 1)
                turn(1, B - 1, 1)

            @block.scalar
            def _(act):
                def turned(b):
                    act.wait_ge(mT_out, b * 16)
                    for n in range(2):
                        act.wait_ge(mtp_ok, b * 2 + n + 1)
                        act.copy(mT[:, 512 * n:512 * n + 512], tp[n][0:H, :, :].rearrange("p a b -> p (a b)")
                                 ).then_inc(mT_ok, 1)
                    act.wait_ge(mT_ok, b * 2 + 2)
                    act.dma_start(g.m_rows.rearrange("(b h) t -> b h t", b=B)[b], mT[:]).then_inc(mT_out, 16)

                def one(a, b, ua, ub):
                    if b is not None and not (isinstance(b, int) and b == 0):
                        turned(b - 1)
                    act.wait_ge(var_ok, a + 1)
                    act.activation(std[:], var[:], ACT.Sqrt).then_inc(std_ok, 1)
                    for n in range(6):
                        act.wait_ge(tp_ok, a * 10 + n + 1)
                        act.wait_ge(x_lo, a * 6 + max(n - 1, 0))
                        for dst in (xs[0][:, n // 3, 512 * (n % 3):512 * (n % 3) + 512], x32[n % 2][:]):
                            act.copy(dst, tp[n % 2][:].rearrange("p a b -> p (a b)")).then_inc(T_ok, 1)
                    act.wait_ge(lo_ok, a * 3)
                    for n in range(4):
                        act.wait_ge(pj_ok, a * 6 + n + 1)
                        for dst in (q32, q16[0]):
                            act.activation(dst[:, n // 2, 512 * (n % 2):512 * (n % 2) + 512], pj[n % 2][:], ACT.Identity,
                                           bias=bqk_s[:, 0, n // 2:n // 2 + 1], scale=QK / WS).then_inc(q_ok, 1)
                    for n in range(4, 6):
                        act.wait_ge(pj_ok, a * 6 + n + 1)
                        act.activation(k32[:, n - 4, :], pj[n % 2][:], ACT.Identity,
                                       bias=bqk_s[:, 1, n - 4:n - 3], scale=QK / WS,
                                       accum_out=ksum[:, n - 4:n - 3]).then_inc(k_ok, 1)
                    act.wait_ge(k_ok, a * 7 + 2)
                    act.mul(kmean[:], ksum[:], -1.0 / U).then_inc(k_ok, 1)
                    act.wait_ge(k_ok, a * 7 + 3)
                    for dst in (kc, k16[0]):
                        for n in range(DC):
                            act.activation(dst[:, n, :], k32[:, n, :], ACT.Identity, bias=kmean[:, n:n + 1]).then_inc(k_ok, 1)
                    for n in range(4):
                        act.wait_ge(tp_ok, a * 10 + n + 7)
                        act.mul(qrow[:, 2 * n:2 * n + 2, :].rearrange("p c d -> p (c d)"),
                                tp[n % 2][:].rearrange("p a b -> p (a b)"), 1.0 / QK).then_inc(T_ok, 1)
                    act.wait_ge(T_ok, a * NTC + NTC)
                    act.wait_ge(x_lo, a * 6 + 6)
                    for i in range(2):
                        act.dma_start(g.xs[a, i], xs[i][:, :, 0:S]).then_inc(stored, 16)
                    act.dma_start(q_rows_b[a], qrow[:]).then_inc(stored, 16)
                    act.wait_ge(q_ok, a * 8 + 8)
                    act.wait_ge(k_ok, a * 7 + 7)
                    act.wait_ge(lo_ok, a * 3 + 3)
                    for i in range(2):
                        act.dma_start(g.q16[a, i].rearrange("(c p) t -> p c t", p=P), q16[i][:]).then_inc(stored, 16)
                        act.dma_start(g.k16[a, i].rearrange("(c p) t -> p c t", p=P), k16[i][:]).then_inc(stored, 16)
                    act.wait_ge(stored, a * (16 * NS) + 16 * NS)
                    if b is not None:
                        act.wait_ge(sc_ok, b * NG)
                    for r, (iq, ik) in enumerate(PARTS):
                        act.dma_start(qs[ua][HD * r:HD * r + HD, :, :], qv[a, iq]).then_inc(s_in[ua], 16)
                        act.dma_start(ks[ua][HD * r:HD * r + HD, :, :], kv[a, ik]).then_inc(s_in[ua], 16)
                act.wait_ge(bias_ok, 1)
                for ws, w in ((wqs, wq), (wks, wk)):
                    act.mul(ws[0][:], w[:], WS).then_inc(w_hi, 1)
                loop = steps(one)
                with act.Fori(0, B // 2 - 1) as v:
                    loop(v)
                turned(B - 2)
                turned(B - 1)
                act.wait_ge(mT_out, 16 * B)

            @block.vector
            def _(dve):
                def piece(p, a, ua):
                    if p < NX:
                        if p == 0:
                            dve.wait_ge(x_in[ua], 16 * (a // 2 + 1) if isinstance(a, int) else x_loads(ua))
                            dve.wait_ge(rows_in, a * (16 * UT) + 16 * UT)
                        dve.bn_stats(st[:, p, :], xt[ua][:, p, :]).then_inc(stats, 1)
                    elif p == NX:
                        wait_alone(dve, g, stats, a * (2 * NX) + NX)
                        for c in range(NX):
                            dve.bn_aggr(mv[:, c, :], st[:, c, :]).then_inc(stats, 1)
                    elif p == NX + 1:
                        dve.wait_ge(stats, a * (2 * NX) + 2 * NX)
                        dve.tensor_scalar(var[:], mv[:, :, 1], EPS, None, ALU.add).then_inc(var_ok, 1)
                    elif p == NX + 3:
                        dve.wait_ge(std_ok, a + 1)
                        sharpen_rstd(dve, rstd_ok, a * 4, rstd, std, var, tmp)
                        dve.wait_ge(tp_ok, a * 10)
                    elif NX + 4 <= p < NX + 4 + NX // 2:
                        for c in (2 * (p - NX - 4), 2 * (p - NX - 4) + 1):
                            last = dve.tensor_scalar(xn[:, c, :], xt[ua][:, c, :], mv[:, c, 0:1], rstd[:, c:c + 1],
                                                     ALU.subtract, ALU.mult)
                        if c == NX - 1:
                            last.then_inc(xn_ok, 1)

                def one(a, b, ua, ub):
                    if b is None:
                        for p in range(NX + 4 + NX // 2):
                            piece(p, a, ua)
                        return
                    if not (isinstance(b, int) and b < 2):
                        dve.wait_ge(mtp_ok, b * 2 - 2)
                    for t in range(NG):
                        c, h0 = t * HG // H, t * HG % H
                        dve.wait_ge(sc_ok, b * NG + t + 1)
                        dve.tensor_reduce(m[ub][:, c, h0:h0 + HG], sc[t % 2][:], AX.X, ALU.max).then_inc(m_ok, 1)
                        if a is not None:
                            piece(t, a, ua)
                dve.wait_ge(w_in, 64)
                dve.tensor_scalar(bqk_s[:], bqk[:], QK, None, ALU.mult).then_inc(bias_ok, 1)
                for n, (ws, w) in enumerate(((wqs, wq), (wks, wk))):
                    dve.wait_ge(w_hi, n + 1)
                    dve.scalar_tensor_tensor(out=ws[1][:], in0=w[:], scalar=WS, in1=ws[0][:], op0=ALU.mult,
                                             op1=ALU.subtract).then_inc(w_lo, 1)
                loop = steps(one)
                with dve.Fori(0, B // 2 - 1) as v:
                    x_loads = lambda ua: v * 16 + 32
                    loop(v)
                one(None, B - 1, None, 1)


def pick_queries(nc, g):
    RND = -(-TOP // 8)
    with ExitStack() as ctx:
        sb = lambda n, s, d=F32: ctx.enter_context(nc.sbuf_tensor(n, s, d))
        m = [sb(f"c_m{i}", [P, S]) for i in range(2)]
        top = sb("c_top", [P, RND, 8])
        at = sb("c_at", [P, RND, 8], U32)
        atf = sb("c_atf", [P, RND * 8])
        base = sb("c_base", [P, 1], I32)
        basf = sb("c_basf", [P, 1])
        lowi = sb("c_lowi", [P, 1], I32)
        lowf = sb("c_lowf", [P, 1])
        rows = sb("c_rows", [P, RND * 8], I32)
        m_in, step, out = g.sem("c_in"), g.sem("c_step"), g.sem("c_out")
        with nc.Block() as block:
            @block.sync
            def _(sp):
                sp.dma_start(m[0][:], g.m_rows).then_inc(m_in, 16)
                sp.wait_ge(step, 3 * RND + 5)
                sp.dma_start(g.sel_rows.rearrange("(r j) a -> r (j a)", j=TOP), rows[:, 0:TOP]).then_inc(out, 16)
                sp.wait_ge(out, 16)

            @block.vector
            def _(dve):
                n = 0
                dve.wait_ge(m_in, 16)

                def then(ins):
                    nonlocal n
                    n += 1
                    ins.then_inc(step, 1)
                    dve.wait_ge(step, n)
                for r in range(RND):
                    then(dve.max(top[:, r, :], m[r % 2][:]))
                    then(dve.max_index(at[:, r, :], top[:, r, :], m[r % 2][:]))
                    then(dve.match_replace(m[1 - r % 2][:], top[:, r, :], m[r % 2][:], -3.0e38))
                then(dve.tensor_scalar(lowi[:], g.part_i[:], H - 1, None, ALU.bitwise_and))
                then(dve.tensor_copy(lowf[:], lowi[:]))
                then(dve.tensor_tensor(basf[:], g.part_f[:], lowf[:], ALU.subtract))
                then(dve.scalar_tensor_tensor(out=basf[:], in0=basf[:], scalar=float(S), in1=lowf[:],
                                              op0=ALU.mult, op1=ALU.add))
                then(dve.tensor_scalar(rows[:], at[:].rearrange("p r k -> p (r k)"), float(H), basf[:, 0:1],
                                       ALU.mult, ALU.add))


def attend_selected(nc, g):
    NCH = 6
    HH = H // 2
    CH = [(n // 3, 3 * (n % 3), min(3, HH - 3 * (n % 3))) for n in range(NCH)]
    RM = 3 * TOP
    with ExitStack() as ctx:
        sb = lambda n, s, d=F32: ctx.enter_context(nc.sbuf_tensor(n, s, d))
        wk, wv = sb("d_wk", [P, DC, D]), sb("d_wv", [P, DC, D])
        bk, bv_row = sb("d_bk", [P, DC]), sb("d_bv_row", [P, D])
        mask = sb("d_mask", [RM, 3, HH])
        wks, wvs = ([sb(f"d_{n}{i}", [P, DC, D], F16) for i in range(2)] for n in ("wks", "wvs"))
        xs = [[sb(f"d_xs{u}_{i}", [P, DC, S], F16) for i in range(2)] for u in range(2)]
        ks = [sb(f"d_ks{i}", [P, DC, S], F16) for i in range(2)]
        idx = [sb(f"d_idx{u}", [RM, NCH], I32) for u in range(2)]
        kT, v_ = sb("d_kT", [P, DC, S]), sb("d_v", [P, ST, D])
        vm = sb("d_vm", [P, D])
        qg = sb("d_qg", [RM, NCH, HD])
        e_ = sb("d_e", [RM, NCH, HH, HD])
        bd = [sb(f"d_bd{i}", [P, NCH, RM], F16) for i in range(2)]
        mx, nmx = sb("d_mx", [RM, NCH]), sb("d_nmx", [RM, NCH])
        rs, rinv = sb("d_rs", [RM, NCH]), sb("d_rinv", [RM, NCH])
        pm = [sb(f"d_pm{i}", [RM, S]) for i in range(2)]
        pT = sb("d_pT", [P, ST, RM])
        cm = sb("d_cm", [RM, HH, HD])
        cr = sb("d_cr", [RM, NCH, HD])
        sc = [ctx.enter_context(nc.psum_tensor(f"d_sc{i}", [P, 2, 512], F32)) for i in range(2)]
        pt = ctx.enter_context(nc.psum_tensor("d_pt", [P, 2, 4, P], F32))
        bdp = ctx.enter_context(nc.psum_tensor("d_bdp", [P, 3, P], F32))
        cx = ctx.enter_context(nc.psum_tensor("d_cx", [P, P], F32))
        w_in, ws_hi, ws_lo, k_lo, bd_lo = (g.sem("d_" + n) for n in ("w_in", "ws_hi", "ws_lo", "k_lo", "bd_lo"))
        x_in = [g.sem(f"d_x_in{u}") for u in range(2)]
        (pj_ok, kt_ok, v_ok, vm_ok, vm_out, qg_in, e_ok, bdp_ok, bd_ok, sc_ok, mx_ok, nmx_ok, exp_ok, pt_ok,
         pTa_ok, pTb_ok, cx_ok, rinv_ok, cm_ok, cr_ok, put) = (g.sem("d_" + n) for n in (
             "pj", "kt", "v", "vm", "vm_out", "qg", "e", "bdp", "bd", "sc", "mx", "nmx", "exp", "pt",
             "pTa", "pTb", "cx", "rinv", "cm", "cr", "put"))
        mask1, mask2, mask3 = g.sem("d_mask1"), g.sem("d_mask2"), g.sem("d_mask3")
        x_b = g.xs.rearrange("(v u) i p c t -> v u i p c t", u=2)
        sel_b = g.sel_rows.rearrange("(v u r) a -> v u r a", u=2, r=H * TOP)
        out_b = g.attn_rows.rearrange("(b c p h) e -> b p c (h e)", b=B, p=P, h=H)
        with nc.allow_non_contiguous_dma(reason="bias columns and row numbers"), nc.Block() as block:
            @block.sync
            def _(sp):
                sp.dma_start(wk[:], split_load_w(g.Wk)).then_inc(w_in, 16)
                sp.dma_start(wv[:], split_load_w(g.Wv)).then_inc(w_in, 16)
                sp.dma_start(bk[:], g.bk.rearrange("(c p) -> p c", p=P)).then_inc(w_in, 16)
                sp.dma_start(bv_row[:], g.bv.rearrange("(a n) -> a n", a=1).to_broadcast([P, D])).then_inc(w_in, 16)

                def load(v, u):
                    for i in range(2):
                        sp.dma_start(xs[u][i][:], x_b[v, u, i]).then_inc(x_in[u], 16)
                    for n, (hf, h0, nh) in enumerate(CH):
                        r0 = (hf * HH + h0) * TOP
                        sp.dma_start(idx[u][0:nh * TOP, n:n + 1],
                                     sel_b[v, u, r0:r0 + nh * TOP, :]).then_inc(x_in[u], 16)

                def means(b):
                    sp.wait_ge(vm_ok, b + 1)
                    sp.dma_start(out_b[b], vm[:].unsqueeze(1).to_broadcast([P, ST, D])).then_inc(vm_out, 16)
                load(0, 0)
                load(0, 1)
                means(0)
                with sp.Fori(0, B // 2 - 1) as v:
                    for u in range(2):
                        wait_alone(sp, g, pj_ok, v * 18 + 9 * u + 9)
                        wait_alone(sp, g, put, (v * 2 + u + 1) * (16 * NCH))
                        load(v + 1, u)
                        means(v * 2 + u + 1)
                means(B - 1)

            @block.tensor
            def _(pe):
                def scores(b, n):
                    hf, rows = CH[n][0], CH[n][2] * TOP
                    pe.wait_ge(bd_lo, b * NCH + n + 1)
                    if n == 0:
                        pe.wait_ge(k_lo, b * 2 + 2)
                    if n >= 2:
                        pe.wait_ge(exp_ok, b * NCH + n - 1)
                    for s in range(2):
                        last = product(pe, sc[n % 2][0:rows, s, :], [q[:, n, 0:rows] for q in bd],
                                       [k[:, hf, 512 * s:512 * s + 512] for k in ks], True, True)
                    last.then_inc(sc_ok, 1)

                pe.wait_ge(ws_lo, 2)
                with pe.Fori(0, B // 2) as v:
                    for u in range(2):
                        b = v * 2 + u
                        pe.wait_ge(x_in[u], v * 128 + 128)
                        pe.wait_ge(exp_ok, b * NCH)
                        for n in range(9):
                            out = sc[n % 4 // 2][:, n % 2, :]
                            if 4 <= n < 8:
                                pe.wait_ge(kt_ok, (b * 4 + n - 3) * 2)
                            if n < 4:
                                m, t0 = n // 2, 512 * (n % 2)
                                for k in range(DC):
                                    last = product(pe, out, [w[:, k, P * m:P * m + P] for w in wks],
                                                   [x[:, k, t0:t0 + 512] for x in xs[u]], k == 0, k == DC - 1)
                            elif n < 8:
                                for a in range(2):
                                    c = 2 * (n - 4) + a
                                    for k in range(DC):
                                        last = product(pe, out[:, D * a:D * a + D], [x[:, k, P * c:P * c + P] for x in xs[u]],
                                                       [w[:, k, :] for w in wvs], k == 0, k == DC - 1)
                            else:
                                pe.wait_ge(v_ok, b * 4 + 4)
                                for c in range(ST):
                                    last = pe.matmul(out[:, 0:D], g.ones[:], v_[:, c, :],
                                                     start=(c == 0), stop=(c == ST - 1))
                            last.then_inc(pj_ok, 1)
                        pe.wait_ge(e_ok, b * NCH + NCH)
                        for r in range(2):
                            pe.wait_ge(bd_lo, b * NCH + 3 * r)
                            for kk in range(3):
                                rows = CH[kk][2] * TOP
                                last = pe.transpose(bdp[:, kk, 0:rows],
                                                    e_[0:rows, 3 * r + kk, :, :].rearrange("r h e -> r (h e)"),
                                                    g.ident[0:rows, 0:rows])
                            last.then_inc(bdp_ok, 1)
                        pe.wait_ge(vm_ok, b + 1)
                        scores(b, 0)
                        scores(b, 1)
                        for n in range(NCH):
                            hf, rows = CH[n][0], CH[n][2] * TOP
                            pe.wait_ge(exp_ok, b * NCH + n + 1)
                            pe.wait_ge(pTa_ok, b * NCH + n)
                            pe.wait_ge(pTb_ok, b * NCH + n)
                            for c in range(ST):
                                last = pe.transpose(pt[:, c // 4, c % 4, 0:rows], pm[n % 2][0:rows, P * c:P * c + P],
                                                    g.ident[0:rows, 0:rows])
                            last.then_inc(pt_ok, 1)
                            if n + 2 < NCH:
                                scores(b, n + 2)
                            pe.wait_ge(pTa_ok, b * NCH + n + 1)
                            pe.wait_ge(pTb_ok, b * NCH + n + 1)
                            pe.wait_ge(cm_ok, b * NCH + n)
                            for c in range(ST):
                                last = pe.matmul(cx[0:rows, :], pT[:, c, 0:rows], v_[:, c, P * hf:P * hf + P],
                                                 start=(c == 0), stop=(c == ST - 1))
                            last.then_inc(cx_ok, 1)

            @block.scalar
            def _(act):
                def exps(b, n):
                    rows = CH[n][2] * TOP
                    act.wait_ge(nmx_ok, b * NCH + n + 1)
                    act.activation(pm[n % 2][0:rows, :], sc[n % 2][0:rows, :, :].rearrange("r a t -> r (a t)"),
                                   ACT.Exp, bias=nmx[0:rows, n:n + 1], scale=0.25,
                                   accum_out=rs[0:rows, n:n + 1]).then_inc(exp_ok, 1)

                act.wait_ge(w_in, 64)
                for ws, w in ((wks, wk), (wvs, wv)):
                    act.mul(ws[0][:], w[:], WS).then_inc(ws_hi, 1)
                with act.Fori(0, B) as b:
                    act.wait_ge(cx_ok, b * NCH)
                    act.wait_ge(k_lo, b * 2)
                    for n in range(4):
                        act.wait_ge(pj_ok, b * 9 + n + 1)
                        for dst in (kT, ks[0]):
                            act.activation(dst[:, n // 2, 512 * (n % 2):512 * (n % 2) + 512], sc[n // 2][:, n % 2, :],
                                           ACT.Identity, bias=bk[:, n // 2:n // 2 + 1], scale=1.0 / WS).then_inc(kt_ok, 1)
                    act.wait_ge(pj_ok, b * 9 + 9)
                    act.wait_ge(vm_out, b * 16)
                    act.mul(vm[:], sc[0][:, 0, 0:D], 1.0 / S).then_inc(vm_ok, 1)
                    for r in range(2):
                        act.wait_ge(bdp_ok, b * 2 + r + 1)
                        for kk in range(3):
                            rows = CH[kk][2] * TOP
                            act.copy(bd[0][:, 3 * r + kk, 0:rows], bdp[:, kk, 0:rows]).then_inc(bd_ok, 1)
                    exps(b, 0)
                    exps(b, 1)
                    for n in range(NCH):
                        rows = CH[n][2] * TOP
                        act.wait_ge(pt_ok, b * NCH + n + 1)
                        act.wait_ge(cx_ok, b * NCH + n)
                        act.copy(pT[:, 0:4, 0:rows], pt[:, 0, :, 0:rows]).then_inc(pTa_ok, 1)
                        if n + 2 < NCH:
                            exps(b, n + 2)

            @block.vector
            def _(dve):
                def maxima(b, n):
                    rows = CH[n][2] * TOP
                    dve.wait_ge(sc_ok, b * NCH + n + 1)
                    dve.tensor_reduce(mx[0:rows, n:n + 1], sc[n % 2][0:rows, :, :], AX.XY, ALU.max).then_inc(mx_ok, 1)
                    dve.wait_ge(mx_ok, b * NCH + n + 1)
                    dve.tensor_scalar(nmx[0:rows, n:n + 1], mx[0:rows, n:n + 1], -0.25, None,
                                      ALU.mult).then_inc(nmx_ok, 1)

                dve.wait_ge(w_in, 64)
                for n, (ws, w) in enumerate(((wks, wk), (wvs, wv))):
                    dve.wait_ge(ws_hi, n + 1)
                    dve.scalar_tensor_tensor(out=ws[1][:], in0=w[:], scalar=WS, in1=ws[0][:], op0=ALU.mult,
                                             op1=ALU.subtract).then_inc(ws_lo, 1)
                dve.wait_ge(mask3, 3)
                with dve.Fori(0, B) as b:
                    dve.wait_ge(cx_ok, b * NCH)
                    for n in range(4):
                        dve.wait_ge(pj_ok, b * 9 + n + 5)
                        dve.scalar_tensor_tensor(out=v_[:, 2 * n:2 * n + 2, :],
                                                 in0=sc[n // 2][:, n % 2, :].rearrange("p (a d) -> p a d", a=2),
                                                 scalar=1.0 / WS, in1=bv_row[:].unsqueeze(1).to_broadcast([P, 2, D]),
                                                 op0=ALU.mult, op1=ALU.add).then_inc(v_ok, 1)
                    dve.wait_ge(qg_in, b * (16 * NCH) + 16 * NCH)
                    for n, (hf, h0, nh) in enumerate(CH):
                        r = nh * TOP
                        dve.tensor_tensor(e_[0:r, n, :, :], qg[0:r, n, :].unsqueeze(1).to_broadcast([r, HH, HD]),
                                          mask[0:r, n % 3, :].unsqueeze(2).to_broadcast([r, HH, HD]),
                                          ALU.mult).then_inc(e_ok, 1)
                    for n in range(NCH):
                        rows = CH[n][2] * TOP
                        dve.wait_ge(bd_ok, b * NCH + 3 * (n // 3) + 3)
                        dve.tensor_tensor(bd[1][:, n, 0:rows], bdp[:, n % 3, 0:rows], bd[0][:, n, 0:rows],
                                          ALU.subtract).then_inc(bd_lo, 1)
                    maxima(b, 0)
                    maxima(b, 1)
                    for n in range(NCH):
                        rows = CH[n][2] * TOP
                        dve.wait_ge(pt_ok, b * NCH + n + 1)
                        dve.wait_ge(cx_ok, b * NCH + n)
                        dve.tensor_copy(pT[:, 4:8, 0:rows], pt[:, 1, :, 0:rows]).then_inc(pTb_ok, 1)
                        if n + 2 < NCH:
                            maxima(b, n + 2)
                        dve.reciprocal(rinv[0:rows, n:n + 1], rs[0:rows, n:n + 1]).then_inc(rinv_ok, 1)
                        dve.wait_ge(rinv_ok, b * NCH + n + 1)
                        dve.wait_ge(cx_ok, b * NCH + n + 1)
                        dve.scalar_tensor_tensor(out=cm[0:rows, :, :],
                                                 in0=cx[0:rows, :].rearrange("r (h e) -> r h e", h=HH),
                                                 scalar=rinv[0:rows, n:n + 1],
                                                 in1=mask[0:rows, n % 3, :].unsqueeze(2).to_broadcast([rows, HH, HD]),
                                                 op0=ALU.mult, op1=ALU.mult).then_inc(cm_ok, 1)
                        dve.wait_ge(cm_ok, b * NCH + n + 1)
                        dve.wait_ge(put, b * (16 * NCH))
                        dve.tensor_reduce(cr[0:rows, n, :], cm[0:rows, :, :].rearrange("r h e -> r e h"),
                                          AX.X, ALU.add).then_inc(cr_ok, 1)

            @block.gpsimd
            def _(pool):
                pool.memset(mask[:], 1.0).then_inc(mask1, 1)
                pool.wait_ge(mask1, 1)
                for kk in range(3):
                    pool.affine_select(out=mask[:, kk, :], in_=mask[:, kk, :], compare_op=ALU.is_ge, fill=0.0,
                                       base=TOP * 3 * kk, pattern=[[-TOP, HH]], channel_multiplier=1).then_inc(mask2, 1)
                pool.wait_ge(mask2, 3)
                for kk in range(3):
                    pool.affine_select(out=mask[:, kk, :], in_=mask[:, kk, :], compare_op=ALU.is_ge, fill=0.0,
                                       base=TOP - 1 - TOP * 3 * kk, pattern=[[TOP, HH]],
                                       channel_multiplier=-1).then_inc(mask3, 1)
                def batch(v, u):
                    b = v * 2 + u
                    pool.wait_ge(x_in[u], v * 128 + 128)
                    wait_alone(pool, g, e_ok, b * NCH)
                    for n, (hf, h0, nh) in enumerate(CH):
                        r = nh * TOP
                        pool.indirect_dma_start(
                            out=qg[0:r, n, :], out_offset=None, in_=g.q_rows,
                            in_offset=bass.IndirectOffsetOnAxis(ap=idx[u][0:r, n:n + 1], axis=0)).then_inc(qg_in, 16)
                    for m in range(DC):
                        wait_alone(pool, g, kt_ok, b * 8 + 4 * m + 4)
                        pool.tensor_tensor(ks[1][:, m, :], kT[:, m, :], ks[0][:, m, :], ALU.subtract).then_inc(k_lo, 1)
                    pool.wait_ge(vm_out, b * 16 + 16)
                    for n, (hf, h0, nh) in enumerate(CH):
                        r = nh * TOP
                        wait_alone(pool, g, cr_ok, b * NCH + n + 1)
                        pool.indirect_dma_start(
                            out=g.attn_rows, in_=cr[0:r, n, :], in_offset=None,
                            out_offset=bass.IndirectOffsetOnAxis(ap=idx[u][0:r, n:n + 1], axis=0)).then_inc(put, 16)
                with pool.Fori(0, B // 2) as v:
                    batch(v, 0)
                    batch(v, 1)
                pool.wait_ge(put, B * 16 * NCH)


def add_attention_and_gate(nc, g):
    E = 8
    with ExitStack() as ctx:
        sb = lambda n, s, d=F32: ctx.enter_context(nc.sbuf_tensor(n, s, d))
        wo, gate = sb("e_wo", [P, DC, D]), sb("e_gate", [P, DC, E])
        bo_row = sb("e_bo_row", [P, D])
        a_ = [sb(f"e_attn{u}", [P, ST, D]) for u in range(2)]
        x_ = [sb(f"e_xin{u}", [P, ST, D]) for u in range(2)]
        aT = sb("e_aT", [P, DC, S])
        x1 = [sb(f"e_x1_{u}", [P, ST, D]) for u in range(2)]
        xn = [sb(f"e_xn_{u}", [P, ST, D]) for u in range(2)]
        xnT = sb("e_xnT", [P, DC, S])
        st, mv = sb("e_st", [P, ST, 6]), sb("e_mv", [P, ST, 2])
        var, std, rstd, tmp = (sb("e_" + n, [P, ST]) for n in ("var", "std", "rstd", "tmp"))
        mx, den, rden = (sb("e_" + n, [P, ST]) for n in ("mx", "den", "rden"))
        lg, ex, pr = (sb("e_" + n, [P, ST, E]) for n in ("lg", "ex", "pr"))
        tp = [ctx.enter_context(nc.psum_tensor(f"e_tp{i}", [P, 4, P], F32)) for i in range(2)]
        pj = [ctx.enter_context(nc.psum_tensor(f"e_pj{i}", [P, 2, D], F32)) for i in range(4)]
        gt = ctx.enter_context(nc.psum_tensor("e_gt", [P, ST, E], F32))
        w_in = g.sem("e_w_in")
        in_ = [g.sem(f"e_in{u}") for u in range(2)]
        out = [g.sem(f"e_out{u}") for u in range(2)]
        (atp_ok, aT_ok, ntp_ok, nT_ok, xb_ok, pj_ok, x1_ok, stats, var_ok, std_ok, rstd_ok, xn_ok, gt_ok, sm, ex_ok,
         out_T) = (g.sem("e_" + n) for n in ("atp", "aT", "ntp", "nT", "xb", "pj", "x1", "stats", "var", "std", "rstd",
                                             "xn", "gt", "sm", "ex", "out_T"))
        SM = 6
        tiles = lambda t: t.rearrange("(v u c p) d -> v u p c d", u=2, c=ST, p=P)
        out_tiles = lambda t: t.rearrange("(b c p) d -> b p c d", c=ST, p=P)
        attn = tiles(g.attn_rows.rearrange("(t h) e -> t (h e)", h=H))
        x_b = tiles(g.x.rearrange("b s d -> (b s) d"))
        tab = out_tiles(g.tab)

        with nc.Block() as block:
            @block.sync
            def _(sp):
                sp.dma_start(wo[:], split_load_w(g.Wo)).then_inc(w_in, 16)
                sp.dma_start(gate[:], split_load_w(g.gate)).then_inc(w_in, 16)
                sp.dma_start(bo_row[:], g.bo.rearrange("(a n) -> a n", a=1).to_broadcast([P, D])).then_inc(w_in, 16)

                def load(v, u):
                    sp.dma_start(a_[u][:], attn[v, u]).then_inc(in_[u], 16)
                    sp.dma_start(x_[u][:], x_b[v, u]).then_inc(in_[u], 16)
                load_ahead(sp, B // 2, x1_ok, 4, load)

            @block.gpsimd
            def _(pool):
                pool.wait_ge(w_in, 48)
                with pool.Fori(0, B // 2) as v:
                    for u in range(2):
                        pool.wait_ge(in_[u], v * 32 + 32)
                        for c in range(ST):
                            last = pool.tensor_tensor(x_[u][:, c, :], x_[u][:, c, :], bo_row[:], ALU.add)
                        last.then_inc(xb_ok, 1)

            @block.tensor
            def _(pe):
                def turn(src, n, done):
                    for a in range(4):
                        last = pe.transpose(tp[n % 2][:, a, :], src[:, 4 * (n % 2) + a, P * (n // 2):P * (n // 2) + P],
                                            g.ident[:])
                    last.then_inc(done, 1)

                def one(b, u, v):
                    first, second = halves(b)
                    if first:
                        pe.wait_ge(in_[u], v * 32 + 32)
                        if second:
                            pe.wait_ge(nT_ok, (b - 1) * 4)
                        for n in range(4):
                            pe.wait_ge(aT_ok, b * 4 + max(n - 1, 0))
                            turn(a_[u], n, atp_ok)
                        pe.wait_ge(aT_ok, b * 4 + 4)
                        pe.wait_ge(x1_ok, b * 4)
                        for c in range(ST):
                            for k in range(DC):
                                last = pe.matmul(pj[c // 2][:, c % 2, :], aT[:, k, P * c:P * c + P], wo[:, k, :],
                                                 start=(k == 0), stop=(k == DC - 1))
                            if c % 2:
                                last.then_inc(pj_ok, 1)
                    if second:
                        pe.wait_ge(xn_ok, b)
                        for n in range(4):
                            pe.wait_ge(nT_ok, (b - 1) * 4 + max(n - 1, 0))
                            turn(xn[1 - u], n, ntp_ok)
                        pe.wait_ge(nT_ok, b * 4)
                        pe.wait_ge(sm, (b - 1) * SM)
                        for c in range(ST):
                            for k in range(DC):
                                last = pe.matmul(gt[:, c, :], xnT[:, k, P * c:P * c + P], gate[:, k, :],
                                                 start=(k == 0), stop=(k == DC - 1))
                        last.then_inc(gt_ok, 1)
                pe.wait_ge(w_in, 48)
                in_steps(pe, one)

            @block.scalar
            def _(act):
                def one(b, u, v):
                    first, second = halves(b)
                    if first:
                        act.wait_ge(pj_ok, b * 4)
                        for n in range(4):
                            act.wait_ge(atp_ok, b * 4 + n + 1)
                            act.copy(aT[:, n // 2, 512 * (n % 2):512 * (n % 2) + 512],
                                     tp[n % 2][:].rearrange("p a b -> p (a b)")).then_inc(aT_ok, 1)
                    if second:
                        act.wait_ge(out_T, (b - 1) * 32)
                        for n in range(4):
                            act.wait_ge(ntp_ok, (b - 1) * 4 + n + 1)
                            act.copy(xnT[:, n // 2, 512 * (n % 2):512 * (n % 2) + 512],
                                     tp[n % 2][:].rearrange("p a b -> p (a b)")).then_inc(nT_ok, 1)
                        act.wait_ge(nT_ok, b * 4)
                        act.dma_start(g.xnT1[b - 1], xnT[:]).then_inc(out_T, 16)
                    if first:
                        act.wait_ge(var_ok, b + 1)
                        act.activation(std[:], var[:], ACT.Sqrt).then_inc(std_ok, 1)
                        act.wait_ge(x1_ok, b * 4 + 4)
                        act.dma_start(out_tiles(g.x1)[b], x1[u][:]).then_inc(out[u], 16)
                    if second:
                        act.wait_ge(sm, (b - 1) * SM + 2)
                        act.activation(ex[:], lg[:], ACT.Exp).then_inc(ex_ok, 1)
                    if first:
                        act.wait_ge(xn_ok, b + 1)
                        act.dma_start(tab[b][:, :, 0:D], xn[u][:]).then_inc(out[u], 16)
                    if second:
                        act.wait_ge(sm, (b - 1) * SM + 5)
                        act.dma_start(tab[b - 1][:, :, D:D + E], pr[:]).then_inc(out_T, 16)
                in_steps(act, one)
                for u in range(2):
                    act.wait_ge(out[u], 32 * (B // 2))
                act.wait_ge(out_T, 32 * B)

            @block.vector
            def _(dve):
                def one(b, u, v):
                    first, second = halves(b)
                    if first:
                        dve.wait_ge(xb_ok, b + 1)
                        dve.wait_ge(out[u], v * 32)
                        for n in range(4):
                            dve.wait_ge(pj_ok, b * 4 + n + 1)
                            dve.tensor_tensor(x1[u][:, 2 * n:2 * n + 2, :], pj[n][:], x_[u][:, 2 * n:2 * n + 2, :],
                                              ALU.add).then_inc(x1_ok, 1)
                        dve.wait_ge(x1_ok, b * 4 + 4)
                        for c in range(ST):
                            dve.bn_stats(st[:, c, :], x1[u][:, c, :]).then_inc(stats, 1)
                        wait_alone(dve, g, stats, b * (2 * ST) + ST)
                        for c in range(ST):
                            dve.bn_aggr(mv[:, c, :], st[:, c, :]).then_inc(stats, 1)
                        dve.wait_ge(stats, b * (2 * ST) + 2 * ST)
                        dve.tensor_scalar(var[:], mv[:, :, 1], EPS, None, ALU.add).then_inc(var_ok, 1)
                    if second:
                        s0 = (b - 1) * SM
                        dve.wait_ge(gt_ok, b)
                        dve.tensor_reduce(mx[:], gt[:], AX.X, ALU.max).then_inc(sm, 1)
                        dve.wait_ge(sm, s0 + 1)
                        dve.tensor_tensor(lg[:], gt[:], mx[:].unsqueeze(2).to_broadcast([P, ST, E]),
                                          ALU.subtract).then_inc(sm, 1)
                    if first:
                        dve.wait_ge(std_ok, b + 1)
                        sharpen_rstd(dve, rstd_ok, b * 4, rstd, std, var, tmp)
                        for c in range(ST):
                            last = dve.tensor_scalar(xn[u][:, c, :], x1[u][:, c, :], mv[:, c, 0:1], rstd[:, c:c + 1],
                                                     ALU.subtract, ALU.mult)
                        last.then_inc(xn_ok, 1)
                    if second:
                        dve.wait_ge(ex_ok, b)
                        dve.tensor_reduce(den[:], ex[:], AX.X, ALU.add).then_inc(sm, 1)
                        dve.wait_ge(sm, s0 + 3)
                        dve.reciprocal(rden[:], den[:]).then_inc(sm, 1)
                        dve.wait_ge(sm, s0 + 4)
                        dve.wait_ge(out_T, (b - 1) * 32)
                        dve.tensor_tensor(pr[:], ex[:], rden[:].unsqueeze(2).to_broadcast([P, ST, E]),
                                          ALU.mult).then_inc(sm, 1)
                        dve.wait_ge(sm, s0 + 5)
                        dve.tensor_copy(g.probs.rearrange("p e (b c) -> p b e c", b=B)[:, b - 1, :, :],
                                        pr[:].rearrange("p c e -> p e c")).then_inc(sm, 1)
                in_steps(dve, one)

E0 = 8
CAP = T // E0
HID = 1024
HC = HID // P
BF16 = mybir.dt.bfloat16
ROW = D + E0


def as_float(t):
    return t[:].bitcast(F32)


def shared_ffn_and_choice(nc, g):
    G = 512
    NG = T // G
    W = CAP // P
    BITS = 30
    SG = 4
    SEARCH = -(-BITS // (2 * SG))
    with ExitStack() as ctx:
        sb = lambda n, s, d=F32: ctx.enter_context(nc.sbuf_tensor(n, s, d))
        w1, w2 = sb("s_w1", [P, DC, HID]), sb("s_w2", [P, HC, D])
        w1s = [sb(f"s_w1s{i}", [P, DC, HID], F16) for i in range(2)]
        w2s = [sb(f"s_w2s{i}", [P, HC, D], F16) for i in range(2)]
        b1, b2_row = sb("s_b1", [P, HC]), sb("s_b2_row", [P, D])
        xT = [sb(f"s_xT{u}", [P, DC, G]) for u in range(2)]
        x1 = [sb(f"s_x1_{u}", [P, 4, D]) for u in range(2)]
        xs = [[sb(f"s_xs{u}_{i}", [P, DC, G], F16) for i in range(2)] for u in range(2)]
        h32 = [sb(f"s_h32_{i}", [P, G]) for i in range(2)]
        hs = [sb(f"s_hs{i}", [P, HC, G], F16) for i in range(2)]
        y = [sb(f"s_y{u}", [P, 4, D]) for u in range(2)]
        thr, cand, keep = (sb("f_" + n, [P, E0], I32) for n in ("thr", "cand", "keep"))
        bit = sb("f_bit", [P, 1], I32)
        flag = sb("f_flag", [P, E0, NT])
        cnt, need = sb("f_cnt", [P, E0]), sb("f_need", [P, E0])
        eq, sel = sb("f_eq", [P, E0, NT]), sb("f_sel", [P, E0, NT])
        go_on = sb("f_go_on", [P, E0, NT])
        incl, pos = sb("f_incl", [P, E0, NT]), sb("f_pos", [P, E0, NT])
        posi, hi_i, lo_i = (sb("f_" + n, [P, E0, NT], I32) for n in ("posi", "hi_i", "lo_i"))
        hi_f, lo_f = sb("f_hi_f", [P, E0, NT]), sb("f_lo_f", [P, E0, NT])
        hot_lo = sb("f_hot_lo", [P, NT, P], BF16)
        hot_hi = sb("f_hot_hi", [P, NT, W])
        val = sb("f_val", [P, 2, NT, W], BF16)
        col_i, colf = sb("f_col_i", [P, NT], I32), sb("f_colf", [P, NT])
        lst = sb("f_lst", [P, W])
        hp = [ctx.enter_context(nc.psum_tensor(f"s_hp{i}", [P, G], F32)) for i in range(4)]
        yp = [ctx.enter_context(nc.psum_tensor(f"s_yp{i}", [P, 2, D], F32)) for i in range(2)]
        bank = [ctx.enter_context(nc.psum_tensor(f"f_bank{i}", [P, E0 * NT], F32)) for i in range(2)]
        tot = bank[0][:, 0:E0]
        pre, col = (bank[i][:].rearrange("p (e c) -> p e c", e=E0) for i in range(2))
        lp = bank[0][:, 0:2 * W].rearrange("p (i w) -> p i w", i=2)
        w_in, ws_ok, x_hi, x_lo = (g.sem("s_" + n) for n in ("w_in", "ws", "x_hi", "x_lo"))
        in_ = [g.sem(f"s_in{u}") for u in range(2)]
        hp_ok, h_ok, lo_ok, yp_ok, y_ok, xb_ok = (g.sem("s_" + n) for n in ("hp", "h", "lo", "yp", "y", "xb"))
        out = [g.sem(f"s_out{u}") for u in range(2)]
        ready, step, cnt_ok, tot_ok, pre_in, pre_ok, hot_ok, lp_ok, stepe = (
            g.sem("f_" + n) for n in ("ready", "step", "cnt", "tot", "pre_in", "pre", "hot", "lp", "stepe"))
        xT_g = g.xnT1.rearrange("v p c (u t) -> v u p c t", u=2)
        rows = lambda t: t.rearrange("(v u c p) d -> v u p c d", u=2, c=4, p=P)
        wide = lambda t: t.unsqueeze(2).to_broadcast([P, E0, NT])
        with nc.allow_non_contiguous_dma(reason="bias columns"), nc.Block() as block:
            @block.sync
            def _(sp):
                sp.dma_start(w1[:], split_load_w(g.Ws1)).then_inc(w_in, 16)
                sp.dma_start(w2[:], split_load_w(g.Ws2)).then_inc(w_in, 16)
                sp.dma_start(b1[:], g.bs1.rearrange("(c p) -> p c", p=P)).then_inc(w_in, 16)
                sp.dma_start(b2_row[:], g.bs2.rearrange("(a n) -> a n", a=1).to_broadcast([P, D])).then_inc(w_in, 16)

                def load(v, u):
                    sp.dma_start(xT[u][:], xT_g[v, u]).then_inc(in_[u], 16)
                    sp.dma_start(x1[u][:], rows(g.x1)[v, u]).then_inc(in_[u], 16)
                load_ahead(sp, NG // 2, y_ok, 2, load)

            @block.gpsimd
            def _(pool):
                pool.memset(bit[:], 1 << (BITS - 1)).then_inc(ready, 1)
                pool.memset(thr[:], 0).then_inc(ready, 1)
                pool.memset(go_on[:], 1.0).then_inc(ready, 1)
                pool.iota(col_i[:], pattern=[[1, NT]], base=0, channel_multiplier=0).then_inc(ready, 1)
                pool.wait_ge(w_in, 64)
                with pool.Fori(0, NG // 2) as v:
                    for u in range(2):
                        i = v * 2 + u
                        pool.wait_ge(in_[u], v * 32 + 32)
                        wait_alone(pool, g, hp_ok, v * (2 * HC))
                        pool.tensor_copy(xs[u][0][:], xT[u][:]).then_inc(x_hi, 1)
                        pool.wait_ge(x_hi, i + 1)
                        pool.tensor_tensor(xs[u][1][:], xT[u][:], xs[u][0][:], ALU.subtract).then_inc(x_lo, 1)
                        for c in range(4):
                            last = pool.tensor_tensor(x1[u][:, c, :], x1[u][:, c, :], b2_row[:], ALU.add)
                        last.then_inc(xb_ok, 1)

            @block.tensor
            def _(pe):
                def count(n):
                    pe.wait_ge(cnt_ok, n + 1)
                    pe.matmul(tot, g.ones[:], cnt[:], start=True, stop=True).then_inc(tot_ok, 1)

                def sums(r, src):
                    pe.wait_ge(pre_in, r + 1)
                    flat = src[:].rearrange("p e c -> p (e c)")
                    pe.matmul(bank[0][:], g.tri[:], flat, start=True, stop=True)
                    pe.matmul(bank[1][:], g.ones[:], flat, start=True, stop=True).then_inc(pre_ok, 1)

                def make_list(e):
                    pe.wait_ge(hot_ok, e + 1)
                    for c in range(NT):
                        last = pe.matmul(lp, hot_lo[:, c, :], val[:, :, c, :], start=(c == 0), stop=(c == NT - 1))
                    last.then_inc(lp_ok, 1)

                def group(v, u, choice):
                    i = v * 2 + u
                    pe.wait_ge(x_lo, i + 1)
                    for j in range(HC):
                        pe.wait_ge(h_ok, (i * HC + max(j - 3, 0)) * 2)
                        for k in range(DC):
                            last = product(pe, hp[j % 4][:], [w[:, k, P * j:P * j + P] for w in w1s],
                                           [x[:, k, :] for x in xs[u]], k == 0, k == DC - 1)
                        last.then_inc(hp_ok, 1)
                        choice(j)
                    pe.wait_ge(y_ok, i * 2)
                    for a in range(2):
                        for c in range(2):
                            t0 = P * (2 * a + c)
                            for parts in (PARTS[:2], PARTS[2:]) if a == 0 and c == 0 else (PARTS,):
                                for k in range(HC):
                                    if a == 0 and c == 0 and parts == PARTS[:2]:
                                        pe.wait_ge(h_ok, (i * HC + k + 1) * 2)
                                    elif a == 0 and c == 0:
                                        pe.wait_ge(lo_ok, i * HC + k + 1)
                                    last = product(pe, yp[a][:, c, :], [h[:, k, t0:t0 + P] for h in hs],
                                                   [w[:, k, :] for w in w2s], k == 0 and parts[0] == PARTS[0],
                                                   k == HC - 1 and parts[-1] == PARTS[-1], parts)
                            if c == 1:
                                last.then_inc(yp_ok, 1)
                            choice(HC + 2 * a + c)

                pe.wait_ge(ws_ok, 4)
                with pe.Fori(0, SEARCH) as v:
                    for u in range(2):
                        def searching(j):
                            if j % 2 == 0 and 2 <= j <= 2 * SG:
                                count((v * 2 + u) * SG + j // 2 - 1)
                        group(v, u, searching)

                def summing(j):
                    if j == 1:
                        count(2 * SG * SEARCH)
                    elif j in (3, 9):
                        sums(j // 8, (eq, sel)[j // 8])
                group(SEARCH, 0, summing)

                def first_lists(j):
                    if j in (8, 11):
                        make_list((j - 8) // 3)
                group(SEARCH, 1, first_lists)
                with pe.Fori(SEARCH + 1, NG // 2) as v:
                    for u in range(2):
                        def listing(j):
                            if j == 9:
                                make_list(v * 2 + u - 2 * SEARCH)
                        group(v, u, listing)

            @block.scalar
            def _(act):
                act.wait_ge(w_in, 64)
                act.mul(w1s[0][:], w1[:], WS).then_inc(ws_ok, 1)
                act.mul(w2s[0][:], w2[:], WS).then_inc(ws_ok, 1)
                with act.Fori(0, NG // 2) as v:
                    for u in range(2):
                        i = v * 2 + u
                        act.wait_ge(yp_ok, i * 2)
                        for j in range(HC):
                            act.wait_ge(hp_ok, i * HC + j + 1)
                            act.wait_ge(lo_ok, i * HC + max(j - 1, 0))
                            for dst in (h32[j % 2][:], hs[0][:, j, :]):
                                act.activation(dst, hp[j % 4][:], ACT.Gelu_apprx_tanh,
                                               bias=b1[:, j:j + 1], scale=1.0 / WS).then_inc(h_ok, 1)
                        act.wait_ge(y_ok, i * 2 + 2)
                        act.dma_start(rows(g.x2)[v, u], y[u][:]).then_inc(out[u], 16)
                for u in range(2):
                    act.wait_ge(out[u], 16 * (NG // 2))

            @block.vector
            def _(dve):
                def y_out(v, u, a):
                    i = v * 2 + u
                    if a == 0:
                        dve.wait_ge(xb_ok, i + 1)
                        dve.wait_ge(out[u], v * 16)
                    dve.wait_ge(yp_ok, i * 2 + a + 1)
                    dve.scalar_tensor_tensor(out=y[u][:, 2 * a:2 * a + 2, :], in0=yp[a][:], scalar=1.0 / WS,
                                             in1=x1[u][:, 2 * a:2 * a + 2, :], op0=ALU.mult, op1=ALU.add).then_inc(y_ok, 1)

                def low(i, js):
                    for j in js:
                        dve.wait_ge(h_ok, (i * HC + j + 1) * 2)
                        dve.tensor_tensor(hs[1][:, j, :], h32[j % 2][:], hs[0][:, j, :], ALU.subtract).then_inc(lo_ok, 1)

                KS = 5

                def search(i, js):
                    def chain(ins, k):
                        ins.then_inc(step, 1)
                        dve.wait_ge(step, i * KS + k)
                    chain(dve.tensor_tensor(cand[:], thr[:], bit[:].to_broadcast([P, E0]), ALU.bitwise_or), 1)
                    chain(dve.tensor_tensor(flag[:], g.probs, wide(as_float(cand)), ALU.is_ge), 2)
                    dve.tensor_reduce(cnt[:], flag[:], AX.X, ALU.add).then_inc(cnt_ok, 1)
                    low(*js)
                    dve.wait_ge(tot_ok, i + 1)
                    chain(dve.scalar_tensor_tensor(out=keep[:], in0=tot, scalar=float(CAP),
                                                   in1=bit[:].to_broadcast([P, E0]), op0=ALU.is_ge, op1=ALU.mult), 3)
                    chain(dve.tensor_tensor(thr[:], thr[:], keep[:], ALU.bitwise_or), 4)
                    chain(dve.tensor_scalar(bit[:], bit[:], 1, None, ALU.logical_shift_right), 5)

                KE = 5

                def hot_rows(e, i):
                    def chain(ins, k):
                        ins.then_inc(stepe, 1)
                        dve.wait_ge(stepe, e * KE + k)
                    dve.wait_ge(lp_ok, e)
                    QT = NT // 4
                    for q in range(4):
                        last = dve.tensor_tensor(hot_lo[:, QT * q:QT * q + QT, :],
                                                 lo_f[:, e, QT * q:QT * q + QT].unsqueeze(2).to_broadcast([P, QT, P]),
                                                 g.iota_f[:].unsqueeze(1).to_broadcast([P, QT, P]), ALU.is_equal)
                        if q == 3:
                            last.then_inc(stepe, 1)
                        if i is not None:
                            low(i, (2 * q, 2 * q + 1))
                    chain(dve.tensor_tensor(hot_hi[:], hi_f[:, e, :].unsqueeze(2).to_broadcast([P, NT, W]),
                                            g.iota_f[:, 0:W].unsqueeze(1).to_broadcast([P, NT, W]), ALU.is_equal), 2)
                    chain(dve.tensor_scalar(val[:, 0, :, :], hot_hi[:], g.part_f[:, 0:1], None, ALU.mult), 3)
                    dve.tensor_tensor(val[:, 1, :, :], hot_hi[:], colf[:].unsqueeze(2).to_broadcast([P, NT, W]),
                                      ALU.mult).then_inc(hot_ok, 1)

                def list_out(e):
                    dve.wait_ge(lp_ok, e + 1)
                    dve.tensor_copy(lst[:], lp[:, 0, :]).then_inc(stepe, 1)
                    dve.wait_ge(stepe, e * KE + 4)
                    dve.scalar_tensor_tensor(out=g.elist[:, e, :], in0=lp[:, 1, :], scalar=float(P), in1=lst[:],
                                             op0=ALU.mult, op1=ALU.add).then_inc(stepe, 1)
                    dve.wait_ge(stepe, e * KE + 5)

                dve.wait_ge(w_in, 64)
                for n, (ws, w) in enumerate(((w1s, w1), (w2s, w2))):
                    dve.wait_ge(ws_ok, 1 if n == 0 else 3)
                    dve.scalar_tensor_tensor(out=ws[1][:], in0=w[:], scalar=WS, in1=ws[0][:], op0=ALU.mult,
                                             op1=ALU.subtract).then_inc(ws_ok, 1)
                dve.wait_ge(ready, 4)
                with dve.Fori(0, SEARCH) as v:
                    for u in range(2):
                        for s in range(SG):
                            search((v * 2 + u) * SG + s, (v * 2 + u, (2 * s, 2 * s + 1)))
                        for a in range(2):
                            y_out(v, u, a)
                n = 2 * SG * SEARCH * KS

                def then(ins):
                    nonlocal n
                    n += 1
                    ins.then_inc(step, 1)
                    dve.wait_ge(step, n)
                i8 = 2 * SEARCH
                then(dve.tensor_copy(colf[:], col_i[:]))
                then(dve.memset(go_on[:, :, 0:1], 0.0))
                then(dve.tensor_tensor(sel[:], g.probs, wide(as_float(thr)), ALU.is_gt))
                then(dve.tensor_tensor(eq[:], g.probs, wide(as_float(thr)), ALU.is_equal))
                dve.tensor_reduce(cnt[:], sel[:], AX.X, ALU.add).then_inc(cnt_ok, 1)
                dve.wait_ge(tot_ok, 2 * SG * SEARCH + 1)
                then(dve.tensor_scalar(need[:], tot, -1.0, float(CAP), ALU.mult, ALU.add))
                dve.sem_inc(pre_in, 1)
                low(i8, range(4))

                def place():
                    then(dve.tensor_copy(flag[:], col))
                    then(dve.tensor_tensor_scan(incl[:].rearrange("p e c -> p (e c)"),
                                                go_on[:].rearrange("p e c -> p (e c)"),
                                                flag[:].rearrange("p e c -> p (e c)"), 0.0, ALU.mult, ALU.add))
                    then(dve.tensor_tensor(pos[:], incl[:], flag[:], ALU.subtract))
                    then(dve.tensor_tensor(pos[:], pos[:], pre, ALU.add))
                dve.wait_ge(pre_ok, 1)
                low(i8, range(4, HC))
                place()
                then(dve.tensor_tensor(flag[:], pos[:], wide(need[:]), ALU.is_lt))
                then(dve.tensor_tensor(flag[:], flag[:], eq[:], ALU.mult))
                then(dve.tensor_tensor(sel[:], sel[:], flag[:], ALU.add))
                dve.sem_inc(pre_in, 1)
                dve.wait_ge(pre_ok, 2)
                place()
                for a in range(2):
                    y_out(SEARCH, 0, a)
                then(dve.scalar_tensor_tensor(out=pos[:], in0=pos[:], scalar=1.0, in1=sel[:], op0=ALU.add, op1=ALU.mult))
                then(dve.tensor_scalar(posi[:], pos[:], -1.0, None, ALU.add))
                then(dve.tensor_scalar(lo_i[:], posi[:], P - 1, None, ALU.bitwise_and))
                then(dve.tensor_scalar(hi_i[:], posi[:], 7, None, ALU.arith_shift_right))
                then(dve.tensor_copy(lo_f[:], lo_i[:]))
                then(dve.tensor_copy(hi_f[:], hi_i[:]))
                for a in range(2):
                    hot_rows(a, i8 + 1 if a == 0 else None)
                    if a == 1:
                        y_out(SEARCH, 1, 0)
                    list_out(a)
                y_out(SEARCH, 1, 1)
                with dve.Fori(SEARCH + 1, NG // 2) as v:
                    for u in range(2):
                        e = v * 2 + u - 2 * SEARCH
                        hot_rows(e, v * 2 + u)
                        list_out(e)
                        for a in range(2):
                            y_out(v, u, a)


def expert_ffn(nc, g):
    G = 512
    GE = CAP // G
    NG = E0 * GE
    with ExitStack() as ctx:
        sb = lambda n, s, d=F32: ctx.enter_context(nc.sbuf_tensor(n, s, d))
        w1, w2 = sb("g_w1", [P, DC, HID]), sb("g_w2", [P, HC, D])
        w1s = [[sb(f"g_w1s{u}_{i}", [P, DC, HID], F16) for i in range(2)] for u in range(2)]
        w2s = [[sb(f"g_w2s{u}_{i}", [P, HC, D], F16) for i in range(2)] for u in range(2)]
        b2_row = [sb(f"g_b2_row{u}", [P, D]) for u in range(2)]
        b1_rows = sb("g_b1_rows", [E0 * HC, P])
        b1 = sb("g_b1", [P, E0, HC])
        b1u = [sb(f"g_b1u{u}", [P, HC]) for u in range(2)]
        eidx = [sb(f"g_eidx{u}", [P, CAP // P], I32) for u in range(2)]
        tk = [sb(f"g_tk{i}", [P, 4, ROW]) for i in range(2)]
        pr = [sb(f"g_pr{i}", [P, 4]) for i in range(2)]
        xs = [[sb(f"g_xs{u}_{i}", [P, DC, G], F16) for i in range(2)] for u in range(2)]
        h32 = [sb(f"g_h32_{i}", [P, G]) for i in range(2)]
        hs = [sb(f"g_hs{i}", [P, HC, G], F16) for i in range(2)]
        yb = sb("g_yb", [P, 4, D])
        y = [sb(f"g_y{i}", [P, 4, D]) for i in range(2)]
        tp = [ctx.enter_context(nc.psum_tensor(f"g_tp{i}", [P, 4, P], F32)) for i in range(2)]
        hp = [ctx.enter_context(nc.psum_tensor(f"g_hp{i}", [P, G], F32)) for i in range(4)]
        yp = [ctx.enter_context(nc.psum_tensor(f"g_yp{i}", [P, 2, D], F32)) for i in range(2)]
        b_in, b_T, b_ok = g.sem("g_b_in"), g.sem("g_b_T"), g.sem("g_b_ok")
        w_in, b2_in = g.sem("g_w_in"), [g.sem(f"g_b2_in{u}") for u in range(2)]
        w_hi, w_lo, x_hi, lo_ok = (g.sem("g_" + n) for n in ("w_hi", "w_lo", "x_hi", "lo"))
        tk_in = [g.sem(f"g_tk_in{i}") for i in range(2)]
        (idx_ok, tp_ok, T_ok, hp_ok, h_ok, yp_ok, yb_ok, y_ok, pr_ok, put) = (
            g.sem("g_" + n) for n in ("idx", "tp", "T", "hp", "h", "yp", "yb", "y", "pr", "put"))
        w1_e = g.W1.rearrange("(v u) (c p) n -> v u p c n", u=2, p=P)
        w2_e = g.W2.rearrange("(v u) (c p) n -> v u p c n", u=2, p=P)
        b2_e = g.b2.rearrange("(v u a) n -> v u a n", u=2, a=1)
        STEPS = [(u, q) for u in range(2) for q in range(GE)]
        with nc.Block() as block:
            @block.sync
            def _(sp):
                sp.dma_start(b1_rows[:], g.b1.rearrange("e (j p) -> (e j) p", p=P)).then_inc(b_in, 16)

                with sp.Fori(0, E0 // 2) as v:
                    for u in range(2):
                        wait_alone(sp, g, w_lo, (v * 2 + u) * 2)
                        sp.dma_start(w1[:], w1_e[v, u]).then_inc(w_in, 16)
                        sp.dma_start(w2[:], w2_e[v, u]).then_inc(w_in, 16)
                        sp.wait_ge(yb_ok, v * (2 * GE * 4))
                        sp.dma_start(b2_row[u][:], b2_e[v, u].to_broadcast([P, D])).then_inc(b2_in[u], 16)

            @block.gpsimd
            def _(pool):
                def gather(v, s):
                    u, q = STEPS[s]
                    pool.wait_ge(idx_ok, v * 2 + u + 1)
                    if not (isinstance(v, int) and v == 0 and s < 2):
                        wait_alone(pool, g, pr_ok, v * (2 * GE) + s - 1)
                    for c in range(4):
                        pool.indirect_dma_start(
                            out=tk[s % 2][:, c, :], out_offset=None, in_=g.tab,
                            in_offset=bass.IndirectOffsetOnAxis(ap=eidx[u][:, 4 * q + c:4 * q + c + 1],
                                                                axis=0)).then_inc(tk_in[s % 2], 16)

                def add(v, s):
                    u, q = STEPS[s]
                    gi = v * (2 * GE) + s
                    wait_alone(pool, g, y_ok, gi * 4 + 4)
                    wait_alone(pool, g, put, gi * 64)
                    for c in range(4):
                        pool.indirect_dma_start(
                            out=g.x2, in_=y[s % 2][:, c, :], in_offset=None, compute_op=ALU.add,
                            out_offset=bass.IndirectOffsetOnAxis(ap=eidx[u][:, 4 * q + c:4 * q + c + 1],
                                                                 axis=0)).then_inc(put, 16)

                def pair(v, last=False):
                    for s in range(len(STEPS)):
                        if s + 2 < len(STEPS):
                            gather(v, s + 2)
                        elif not last:
                            gather(v + 1, s + 2 - len(STEPS))
                        add(v, s)
                gather(0, 0)
                gather(0, 1)
                with pool.Fori(0, E0 // 2 - 1) as v:
                    pair(v)
                pair(E0 // 2 - 1, True)
                pool.wait_ge(put, NG * 64)

            @block.tensor
            def _(pe):
                pe.wait_ge(b_in, 16)
                pe.transpose(tp[0][:, 0, 0:E0 * HC], b1_rows[:], g.ident[0:E0 * HC, 0:E0 * HC]).then_inc(b_T, 1)
                pe.wait_ge(b_ok, 1)
                def turn(v, s):
                    gi = v * (2 * GE) + s
                    pe.wait_ge(tk_in[s % 2], v * (64 * GE) + 64 * (s // 2 + 1))
                    pe.wait_ge(T_ok, gi * 2)
                    for k in range(DC):
                        for a in range(4):
                            last = pe.transpose(tp[k][:, a, :], tk[s % 2][:, a, P * k:P * k + P], g.ident[:])
                        last.then_inc(tp_ok, 1)

                def pair(v, last_pair=False):
                    for s, (u, q) in enumerate(STEPS):
                        gi = v * (2 * GE) + s
                        pe.wait_ge(T_ok, gi * 2 + 2)
                        if q == 0:
                            pe.wait_ge(w_lo, (v * 2 + u) * 2 + 2)
                        for j in range(HC):
                            pe.wait_ge(h_ok, (gi * HC + max(j - 3, 0)) * 2)
                            for k in range(DC):
                                last = product(pe, hp[j % 4][:], [w[:, k, P * j:P * j + P] for w in w1s[u]],
                                               [x[:, k, :] for x in xs[s % 2]], k == 0, k == DC - 1)
                            last.then_inc(hp_ok, 1)
                        if s + 1 < len(STEPS):
                            turn(v, s + 1)
                        elif not last_pair:
                            turn(v + 1, 0)
                        pe.wait_ge(yb_ok, gi * 4)
                        for a in range(2):
                            for c in range(2):
                                t0 = P * (2 * a + c)
                                for parts in (PARTS[:2], PARTS[2:]) if a == 0 and c == 0 else (PARTS,):
                                    for k in range(HC):
                                        if a == 0 and c == 0 and parts == PARTS[:2]:
                                            pe.wait_ge(h_ok, (gi * HC + k + 1) * 2)
                                        elif a == 0 and c == 0:
                                            pe.wait_ge(lo_ok, gi * HC + k + 1)
                                        last = product(pe, yp[a][:, c, :], [h[:, k, t0:t0 + P] for h in hs],
                                                       [w[:, k, :] for w in w2s[u]], k == 0 and parts[0] == PARTS[0],
                                                       k == HC - 1 and parts[-1] == PARTS[-1], parts)
                            last.then_inc(yp_ok, 1)
                turn(0, 0)
                with pe.Fori(0, E0 // 2 - 1) as v:
                    pair(v)
                pair(E0 // 2 - 1, True)

            @block.scalar
            def _(act):
                act.wait_ge(b_T, 1)
                act.copy(b1[:].rearrange("p e j -> p (e j)"), tp[0][:, 0, 0:E0 * HC]).then_inc(b_ok, 1)
                def split(e, u):
                    act.wait_ge(w_in, e * 32 + 32)
                    act.mul(w1s[u][0][:], w1[:], WS).then_inc(w_hi, 1)
                    act.mul(w2s[u][0][:], w2[:], WS).then_inc(w_hi, 1)

                def pair(v, last_pair=False):
                    for s, (u, q) in enumerate(STEPS):
                        gi = v * (2 * GE) + s
                        act.wait_ge(idx_ok, v * 2 + u + 1)
                        act.wait_ge(yp_ok, gi * 2)
                        for j in range(HC):
                            act.wait_ge(hp_ok, gi * HC + j + 1)
                            act.wait_ge(lo_ok, gi * HC + max(j - 1, 0))
                            for dst in (h32[j % 2][:], hs[0][:, j, :]):
                                act.activation(dst, hp[j % 4][:], ACT.Gelu_apprx_tanh,
                                               bias=b1u[u][:, j:j + 1], scale=1.0 / WS).then_inc(h_ok, 1)
                        if q == 0 and not (last_pair and u == 1):
                            split(v * 2 + u + 1, 1 - u)
                split(0, 0)
                with act.Fori(0, E0 // 2 - 1) as v:
                    pair(v)
                pair(E0 // 2 - 1, True)

            @block.vector
            def _(dve):
                def renew(e, u):
                    dve.tensor_copy(eidx[u][:], g.elist[:, e, :])
                    dve.tensor_copy(b1u[u][:], b1[:, e, :]).then_inc(idx_ok, 1)

                def by_column(gi, i):
                    for k in range(DC):
                        dve.wait_ge(tp_ok, gi * 2 + k + 1)
                        dve.tensor_copy(xs[i][0][:, k, :], tp[k][:].rearrange("p a b -> p (a b)")).then_inc(x_hi, 1)
                        dve.wait_ge(x_hi, gi * 2 + k + 1)
                        dve.tensor_tensor(xs[i][1][:, k, :], tp[k][:].rearrange("p a b -> p (a b)"), xs[i][0][:, k, :],
                                          ALU.subtract).then_inc(T_ok, 1)

                def split(e, u):
                    for n, (ws, w) in enumerate(((w1s, w1), (w2s, w2))):
                        dve.wait_ge(w_hi, e * 2 + n + 1)
                        dve.scalar_tensor_tensor(out=ws[u][1][:], in0=w[:], scalar=WS, in1=ws[u][0][:], op0=ALU.mult,
                                                 op1=ALU.subtract).then_inc(w_lo, 1)

                def pair(v, last=False):
                    for s, (u, q) in enumerate(STEPS):
                        gi = v * (2 * GE) + s
                        dve.tensor_copy(pr[s % 2][:], tk[s % 2][:, :, D:ROW].rearrange("p c (v u) -> p v u c", u=2)[:, v, u, :]
                                        ).then_inc(pr_ok, 1)
                        for j in range(HC):
                            dve.wait_ge(h_ok, (gi * HC + j + 1) * 2)
                            dve.tensor_tensor(hs[1][:, j, :], h32[j % 2][:], hs[0][:, j, :], ALU.subtract).then_inc(lo_ok, 1)
                        if s == 0:
                            dve.wait_ge(put, v * (2 * GE * 64))
                            renew(v * 2 + 1, 1)
                        if s == 2 and not last:
                            dve.wait_ge(put, v * (2 * GE * 64) + GE * 64)
                            renew(v * 2 + 2, 0)
                        if s + 1 < len(STEPS):
                            by_column(gi + 1, (s + 1) % 2)
                        elif not last:
                            by_column(gi + 1, 0)
                        if q == 0 and not (last and u == 1):
                            split(v * 2 + u + 1, 1 - u)
                        dve.wait_ge(pr_ok, gi + 1)
                        dve.wait_ge(b2_in[u], v * 16 + 16)
                        for a in range(2):
                            dve.wait_ge(yp_ok, gi * 2 + a + 1)
                            dve.scalar_tensor_tensor(out=yb[:, 2 * a:2 * a + 2, :], in0=yp[a][:], scalar=1.0 / WS,
                                                     in1=b2_row[u][:].unsqueeze(1).to_broadcast([P, 2, D]),
                                                     op0=ALU.mult, op1=ALU.add).then_inc(yb_ok, 2)
                        dve.wait_ge(yb_ok, gi * 4 + 4)
                        dve.wait_ge(put, v * (2 * GE * 64) + 64 * max(s - 1, 0))
                        for c in range(4):
                            dve.tensor_scalar(y[s % 2][:, c, :], yb[:, c, :], pr[s % 2][:, c:c + 1], None,
                                              ALU.mult).then_inc(y_ok, 1)
                dve.wait_ge(b_ok, 1)
                renew(0, 0)
                by_column(0, 0)
                split(0, 0)
                with dve.Fori(0, E0 // 2 - 1) as v:
                    pair(v)
                pair(E0 // 2 - 1, True)


E1 = 64
K2 = 2
ROW1 = D + K2


def attention_and_top2(nc, g):
    SCALE = 1.0 / 16.0
    with ExitStack() as ctx:
        sb = lambda n, s, d=F32: ctx.enter_context(nc.sbuf_tensor(n, s, d))
        w_rows = sb("h_w_rows", [P, 3, DC, D])
        ws = [sb(f"h_ws{i}", [P, 3, DC, D], F16) for i in range(2)]
        b_col, bv_row = sb("h_b_col", [P, 2, DC]), sb("h_bv_row", [P, D])
        above = sb("h_above", [P, P])
        zero = sb("h_zero", [P, P])
        x2 = [sb(f"h_x2_{u}", [P, ST, D]) for u in range(2)]
        xn = sb("h_xn", [P, ST, D])
        xs = [sb(f"h_xs{i}", [P, DC, S], F16) for i in range(2)]
        st, mv = sb("h_st", [P, 2 * ST, 6]), sb("h_mv", [P, 2 * ST, 2])
        var, std, rstd, tmp = (sb("h_" + n, [P, 2 * ST]) for n in ("var", "std", "rstd", "tmp"))
        qkT, v_ = sb("h_qkT", [P, 2, DC, S]), sb("h_v", [P, ST, D])
        qs, ks = ([sb(f"h_{n}s{i}", [P, DC, S], F16) for i in range(2)] for n in "qk")
        mx, nmx, rs, rinv = (sb("h_" + n, [P, ST]) for n in ("mx", "nmx", "rs", "rinv"))
        pm = [sb(f"h_pm{i}", [P, S]) for i in range(2)]
        pT = sb("h_pT", [P, ST, P])
        x3 = [sb(f"h_x3_{u}", [P, ST, D]) for u in range(2)]
        gate = sb("i_gate", [P, DC, E1])
        gxn, gxnT = sb("i_xn", [P, ST, D]), sb("i_xnT", [P, DC, S])
        lg = sb("i_lg", [P, ST, E1])
        top, at, atf = sb("i_top", [P, ST, 8]), sb("i_at", [P, ST, 8], U32), sb("i_atf", [P, ST, 8])
        dif, ex, ex1 = (sb("i_" + n, [P, ST]) for n in ("dif", "ex", "ex1"))
        w_ = sb("i_w", [P, ST, K2])
        hot = sb("i_hot", [P, K2, ST, E1])
        sel = sb("i_sel", [P, ST, E1])
        run = sb("i_run", [P, ST + 1, E1])
        rkh = sb("i_rkh", [P, K2, ST, E1])
        sc = [ctx.enter_context(nc.psum_tensor(f"h_sc{i}", [P, 2, 512], F32)) for i in range(2)]
        pt = ctx.enter_context(nc.psum_tensor("h_pt", [P, 2, 4, P], F32))
        z = ctx.enter_context(nc.psum_tensor("h_z", [P, 512], F32))
        gb = ctx.enter_context(nc.psum_tensor("i_gb", [P, 512], F32))
        gtp = gb[:].rearrange("p (a t) -> p a t", a=4)
        gp = gb[:].rearrange("p (c e) -> p c e", c=ST)
        w_in, wp_ok, zero_ok, above_ok = (g.sem("h_" + n) for n in ("w_in", "wp", "zero", "above"))
        x_in = [g.sem(f"h_x_in{u}") for u in range(2)]
        w_hi, w_lo, lo_ok, qk_lo = (g.sem("h_" + n) for n in ("w_hi", "w_lo", "x_lo", "qk_lo"))
        (var_ok, std_ok, rstd_ok, xn_ok, tp_ok, T_ok, pj_ok, qk_ok, v_ok, sc_ok, mx_ok, nmx_ok, exp_ok, pt_ok,
         pTa_ok, pTb_ok, z_ok, rinv_ok, x3_ok, x_stats) = (g.sem("h_" + n) for n in (
             "var", "std", "rstd", "xn", "tp", "T", "pj", "qk", "v", "sc", "mx", "nmx", "exp", "pt",
             "pTa", "pTb", "z", "rinv", "x3", "x_stats"))
        out = [g.sem(f"h_out{u}") for u in range(2)]
        (g_stats, gxn_ok, gtp_ok, gT_ok, gp_ok, step, ex_ok, sel_ok, rp_ok, done, gout, wout, fin, zero2_ok) = (
            g.sem("i_" + n) for n in ("stats", "xn", "tp", "T", "gp", "step", "ex", "sel", "rp", "done", "out", "wout",
                                      "fin", "zero"))
        K = 4 + 3 + ST + 3 + 1 + 3 * K2
        tiles = lambda t: t.rearrange("(v u c p) d -> v u p c d", u=2, c=ST, p=P)
        VAR_AT, LOGITS_AT, TOP2_AT = 3, 2, (2, 3, 4, 5, ST - 1)

        def norms(b):
            return (0 if halves(b)[1] else ST), (2 * ST if not isinstance(b, int) or b < B - 1 else ST)
        with nc.allow_non_contiguous_dma(reason="bias columns"), nc.Block() as block:
            @block.sync
            def _(sp):
                for i, w in enumerate((g.Wq1, g.Wk1, g.Wv1)):
                    sp.dma_start(w_rows[:, i, :, :], split_load_w(w)).then_inc(w_in, 16)
                for i, b in enumerate((g.bq1, g.bk1)):
                    sp.dma_start(b_col[:, i, :], b.rearrange("(c p) -> p c", p=P)).then_inc(w_in, 16)
                sp.dma_start(bv_row[:], g.bv1.rearrange("(a n) -> a n", a=1).to_broadcast([P, D])).then_inc(w_in, 16)
                sp.dma_start(gate[:], split_load_w(g.gate1)).then_inc(w_in, 16)
                load_ahead(sp, B // 2, x3_ok, ST,
                           lambda v, u: sp.dma_start(x2[u][:], tiles(g.x2)[v, u]).then_inc(x_in[u], 16))

            @block.gpsimd
            def _(pool):
                pool.memset(zero[:], 0.0).then_inc(zero_ok, 1)
                pool.wait_ge(zero_ok, 1)
                pool.affine_select(out=above[:], in_=zero[:], compare_op=ALU.is_ge, fill=-1.0e30, base=0,
                                   pattern=[[-1, P]], channel_multiplier=1).then_inc(above_ok, 1)
                pool.memset(run[:, 0, :], 0.0).then_inc(zero2_ok, 1)
                with pool.Fori(0, B) as b:
                    pool.wait_ge(sc_ok, b * ST)
                    for n in range(8):
                        i, m, t0 = n // 4, n % 4 // 2, 512 * (n % 2)
                        wait_alone(pool, g, qk_ok, (b * 8 + n + 1) * 2)
                        pool.tensor_tensor((qs, ks)[i][1][:, m, t0:t0 + 512], qkT[:, i, m, t0:t0 + 512],
                                           (qs, ks)[i][0][:, m, t0:t0 + 512], ALU.subtract).then_inc(qk_lo, 1)

            @block.tensor
            def _(pe):
                pe.wait_ge(w_in, 112)
                for i in range(3):
                    if i:
                        pe.wait_ge(w_lo, i)
                    for dc in range(DC):
                        for kc in range(DC):
                            last = pe.transpose(pt[:, 0, dc * DC + kc, :], w_rows[:, i, kc, P * dc:P * dc + P], g.ident[:])
                    last.then_inc(wp_ok, 1)
                pe.wait_ge(w_lo, 3)
                pe.wait_ge(above_ok, 1)
                def turn(b, n):
                    if n == 0:
                        pe.wait_ge(gxn_ok, b + 1)
                        pe.wait_ge(done, b)
                    else:
                        pe.wait_ge(gT_ok, b * 4 + n)
                    for a in range(4):
                        last = pe.transpose(gtp[:, a, :], gxn[:, 4 * (n % 2) + a, P * (n // 2):P * (n // 2) + P], g.ident[:])
                    last.then_inc(gtp_ok, 1)

                def logits(b):
                    pe.wait_ge(gT_ok, b * 4 + 4)
                    for c in range(ST):
                        for k in range(DC):
                            last = pe.matmul(gp[:, c, :], gxnT[:, k, P * c:P * c + P], gate[:, k, :],
                                             start=(k == 0), stop=(k == DC - 1))
                    last.then_inc(gp_ok, 1)

                def ranks(b):
                    pe.wait_ge(sel_ok, b + 1)
                    for c in range(ST):
                        pe.matmul(gp[:, c, :], g.tri[:], sel[:, c, :], start=True, stop=False)
                        last = pe.matmul(gp[:, c, :], g.ones[:], run[:, c, :], start=False, stop=True)
                    last.then_inc(rp_ok, 1)

                def turn_x(b):
                    pe.wait_ge(xn_ok, b + 1)
                    pe.wait_ge(pTa_ok, b * ST)
                    pe.wait_ge(pTb_ok, b * ST)
                    for n in range(4):
                        pe.wait_ge(lo_ok, b * 4 + max(n - 1, 0))
                        for a in range(4):
                            last = pe.transpose(pt[:, n % 2, a, :], xn[:, 4 * (n % 2) + a, P * (n // 2):P * (n // 2) + P],
                                                g.ident[:])
                        last.then_inc(tp_ok, 1)

                def scores(b, i):
                    if i >= 2:
                        pe.wait_ge(exp_ok, b * ST + i - 1)
                    keys = P * (i + 1)
                    for s in range(0, keys, 512):
                        w = min(512, keys - s)
                        diag = s + w == keys
                        for k in range(DC):
                            last = product(pe, sc[i % 2][:, s // 512, 0:w], [q[:, k, P * i:P * i + P] for q in qs],
                                           [t[:, k, s:s + w] for t in ks], k == 0, k == DC - 1 and not diag)
                        if diag:
                            last = pe.matmul(sc[i % 2][:, s // 512, w - P:w], g.ident[:], above[:],
                                             start=False, stop=True)
                    last.then_inc(sc_ok, 1)

                def one(b, u, v):
                    first, second = halves(b)
                    if not first:
                        for n in range(4):
                            turn(b - 1, n)
                        logits(b - 1)
                        ranks(b - 1)
                        return
                    pe.wait_ge(lo_ok, b * 4 + 4)
                    pe.wait_ge(exp_ok, b * ST)
                    for n in range(12):
                        out_ = sc[n % 4 // 2][:, n % 2, :]
                        if n >= 4:
                            pe.wait_ge(qk_ok, (b * 8 + min(n - 3, 8)) * 2)
                        if n < 8:
                            i, m, t0 = n // 4, n % 4 // 2, 512 * (n % 2)
                            for k in range(DC):
                                last = product(pe, out_, [w[:, i, k, P * m:P * m + P] for w in ws],
                                               [x[:, k, t0:t0 + 512] for x in xs], k == 0, k == DC - 1)
                        else:
                            for a in range(2):
                                c = 2 * (n - 8) + a
                                for k in range(DC):
                                    last = product(pe, out_[:, D * a:D * a + D], [x[:, k, P * c:P * c + P] for x in xs],
                                                   [w[:, 2, k, :] for w in ws], k == 0, k == DC - 1)
                        last.then_inc(pj_ok, 1)
                    pe.wait_ge(v_ok, b * 4 + 4)
                    pe.wait_ge(qk_lo, b * 8 + 8)
                    scores(b, 0)
                    scores(b, 1)
                    for n in range(ST):
                        pe.wait_ge(exp_ok, b * ST + n + 1)
                        pe.wait_ge(pTa_ok, b * ST + n)
                        pe.wait_ge(pTb_ok, b * ST + n)
                        for c in range(n + 1):
                            last = pe.transpose(pt[:, c // 4, c % 4, :], pm[n % 2][:, P * c:P * c + P], g.ident[:])
                        last.then_inc(pt_ok, 1)
                        if second and n < 2:
                            turn(b - 1, 2 * n)
                        if n + 2 < ST:
                            scores(b, n + 2)
                        if second and n < 2:
                            turn(b - 1, 2 * n + 1)
                        if second and n == LOGITS_AT:
                            logits(b - 1)
                        if second and n == ST - 1:
                            ranks(b - 1)
                        pe.wait_ge(pTa_ok, b * ST + n + 1)
                        pe.wait_ge(pTb_ok, b * ST + n + 1)
                        pe.wait_ge(x3_ok, b * ST + n)
                        for c in range(n + 1):
                            last = pe.matmul(z[:, 0:D], pT[:, c, :], v_[:, c, :], start=(c == 0), stop=(c == n))
                        last.then_inc(z_ok, 1)
                    if not isinstance(b, int) or b < B - 1:
                        turn_x(b + 1)
                turn_x(0)
                in_steps(pe, one)
                pe.wait_ge(fin, 1)
                pe.matmul(gb[:, 0:E1], g.ones[:], run[:, 0, :], start=True, stop=True).then_inc(fin, 1)

            @block.scalar
            def _(act):
                act.wait_ge(w_in, 112)
                for i in range(3):
                    act.wait_ge(wp_ok, i + 1)
                    act.mul(ws[0][:, i, :, :].rearrange("p c n -> p (c n)"), pt[:, 0, :, :].rearrange("p a b -> p (a b)"),
                            WS).then_inc(w_hi, 1)
                def root(i):
                    act.wait_ge(var_ok, i + 1)
                    return lambda lo, hi: act.activation(std[:, lo:hi], var[:, lo:hi], ACT.Sqrt).then_inc(std_ok, 1)

                def turned(b, n):
                    act.wait_ge(gtp_ok, b * 4 + n + 1)
                    act.copy(gxnT[:, n // 2, 512 * (n % 2):512 * (n % 2) + 512], gb[:]).then_inc(gT_ok, 1)

                def store_xn3(b):
                    act.wait_ge(gxn_ok, b + 1)
                    act.dma_start(g.xn3.rearrange("(b c p) d -> b p c d", c=ST, p=P)[b][:, :, 0:D], gxn[:]).then_inc(gout, 16)

                def store_weights(b):
                    act.wait_ge(done, b + 1)
                    act.dma_start(g.xn3.rearrange("(b c p) d -> b p c d", c=ST, p=P)[b][:, :, D:ROW1], w_[:]).then_inc(wout, 16)

                def weight(b):
                    act.wait_ge(ex_ok, b * 2 + 1)
                    act.activation(ex[:], dif[:], ACT.Exp).then_inc(ex_ok, 1)

                def turned_x(b):
                    act.wait_ge(pj_ok, b * 12)
                    for n in range(4):
                        act.wait_ge(tp_ok, b * 4 + n + 1)
                        act.copy(xs[0][:, n // 2, 512 * (n % 2):512 * (n % 2) + 512],
                                 pt[:, n % 2, :, :].rearrange("p a b -> p (a b)")).then_inc(T_ok, 1)

                def exps(b, i):
                    keys = P * (i + 1)
                    act.wait_ge(nmx_ok, b * ST + i + 1)
                    act.activation(pm[i % 2][:, 0:keys], sc[i % 2][:].rearrange("p a t -> p (a t)")[:, 0:keys],
                                   ACT.Exp, bias=nmx[:, i:i + 1], scale=SCALE, accum_out=rs[:, i:i + 1]).then_inc(exp_ok, 1)

                def one(b, u, v):
                    first, second = halves(b)
                    if not first:
                        root(b + 1)(0, ST)
                        for n in range(4):
                            turned(b - 1, n)
                        store_xn3(b - 1)
                        weight(b - 1)
                        store_weights(b - 1)
                        return
                    for n in range(8):
                        act.wait_ge(pj_ok, b * 12 + n + 1)
                        i, m = n // 4, n % 4 // 2
                        t0 = 512 * (n % 2)
                        if n == 0:
                            act.wait_ge(qk_lo, b * 8)
                            act.wait_ge(sc_ok, b * ST)
                        for dst in (qkT[:, i, m, t0:t0 + 512], (qs, ks)[i][0][:, m, t0:t0 + 512]):
                            act.activation(dst, sc[n % 4 // 2][:, n % 2, :], ACT.Identity, bias=b_col[:, i, m:m + 1],
                                           scale=1.0 / WS).then_inc(qk_ok, 1)
                        if n == VAR_AT:
                            root(b + 1)(*norms(b))
                    if second:
                        store_xn3(b - 1)
                    exps(b, 0)
                    exps(b, 1)
                    for n in range(ST):
                        act.wait_ge(pt_ok, b * ST + n + 1)
                        act.wait_ge(z_ok, b * ST + n)
                        w = min(4, n + 1)
                        act.copy(pT[:, 0:w, :], pt[:, 0, 0:w, :]).then_inc(pTa_ok, 1)
                        if second and n < 2:
                            turned(b - 1, 2 * n)
                        if n + 2 < ST:
                            exps(b, n + 2)
                        if second and n < 2:
                            turned(b - 1, 2 * n + 1)
                        if second and n == ST - 2:
                            weight(b - 1)
                    if not isinstance(b, int) or b < B - 1:
                        turned_x(b + 1)
                    if second:
                        store_weights(b - 1)
                    act.wait_ge(x3_ok, b * ST + ST)
                    act.dma_start(g.x3.rearrange("(b c p) d -> b p c d", c=ST, p=P)[b], x3[u][:]).then_inc(out[u], 16)
                root(0)(ST, 2 * ST)
                turned_x(0)
                in_steps(act, one)
                for u in range(2):
                    act.wait_ge(out[u], 16 * (B // 2))
                act.wait_ge(gout, 16 * B)
                act.wait_ge(wout, 16 * B)

            @block.vector
            def _(dve):
                def norm_stats(src, lo, sem):
                    for c in range(ST):
                        dve.bn_stats(st[:, lo + c, :], src[:, c, :]).then_inc(sem, 1)

                def next_stats(b, loads, u):
                    dve.wait_ge(x_in[u], loads * 16)
                    norm_stats(x2[u], ST, x_stats)

                def variances(step_, before, after):
                    for b, lo, sem in ((before, 0, g_stats), (after, ST, x_stats)):
                        if b is not None:
                            wait_alone(dve, g, sem, b * (2 * ST) + ST)
                            for c in range(ST):
                                dve.bn_aggr(mv[:, lo + c, :], st[:, lo + c, :]).then_inc(sem, 1)
                    for b, sem in ((before, g_stats), (after, x_stats)):
                        if b is not None:
                            wait_alone(dve, g, sem, b * (2 * ST) + 2 * ST)
                    lo, hi = 0 if before is not None else ST, 2 * ST if after is not None else ST
                    dve.tensor_scalar(var[:, lo:hi], mv[:, lo:hi, 1], EPS, None, ALU.add).then_inc(var_ok, 1)

                def sharpen(step_, lo, hi):
                    dve.wait_ge(std_ok, step_ + 1)
                    sharpen_rstd(dve, rstd_ok, step_ * 4, rstd[:, lo:hi], std[:, lo:hi], var[:, lo:hi], tmp[:, lo:hi])

                def norm(dst, src, lo, ok):
                    for c in range(ST):
                        last = dve.tensor_scalar(dst[:, c, :], src[:, c, :], mv[:, lo + c, 0:1], rstd[:, lo + c:lo + c + 1],
                                                 ALU.subtract, ALU.mult)
                    last.then_inc(ok, 1)

                def norm_x3(b, x3_b):
                    dve.wait_ge(gout, b * 16)
                    norm(gxn, x3_b, 0, gxn_ok)

                def norm_x2(b, x2_b):
                    dve.wait_ge(T_ok, b * 4)
                    norm(xn, x2_b, ST, xn_ok)

                def top2(b, part):
                    n = (0, 2, 4, 7, 7 + ST)[part]

                    def then(ins, alone=False):
                        nonlocal n
                        n += 1
                        ins.then_inc(step, 1)
                        if alone:
                            wait_alone(dve, g, step, b * K + n)
                        else:
                            dve.wait_ge(step, b * K + n)
                    if part == 0:
                        dve.wait_ge(gp_ok, b + 1)
                        then(dve.tensor_copy(lg[:], gp), True)
                        for c in range(ST):
                            last = dve.max(top[:, c, :], lg[:, c, :])
                        then(last)
                    elif part == 1:
                        for c in range(ST):
                            last = dve.max_index(at[:, c, :], top[:, c, :], lg[:, c, :])
                        then(last)
                        then(dve.tensor_copy(atf[:], at[:]))
                        dve.tensor_tensor(dif[:], top[:, :, 1], top[:, :, 0], ALU.subtract).then_inc(ex_ok, 1)
                    elif part == 2:
                        for k in range(K2):
                            then(dve.tensor_tensor(hot[:, k, :, :], atf[:, :, k].unsqueeze(2).to_broadcast([P, ST, E1]),
                                                   g.iota_f[:, 0:E1].unsqueeze(1).to_broadcast([P, ST, E1]), ALU.is_equal))
                        then(dve.tensor_tensor(sel[:], hot[:, 0, :, :], hot[:, 1, :, :], ALU.add))
                    elif part == 3:
                        for c in range(ST):
                            then(dve.tensor_tensor(run[:, c + 1, :], run[:, c, :], sel[:, c, :], ALU.add))
                        dve.sem_inc(sel_ok, 1)
                    else:
                        dve.wait_ge(ex_ok, b * 2 + 2)
                        then(dve.tensor_scalar(ex1[:], ex[:], 1.0, None, ALU.add))
                        wait_alone(dve, g, wout, b * 16)
                        then(dve.reciprocal(w_[:, :, 0], ex1[:]))
                        then(dve.tensor_tensor(w_[:, :, 1], ex[:], w_[:, :, 0], ALU.mult))
                        dve.wait_ge(rp_ok, b + 1)
                        then(dve.tensor_copy(run[:, 0, :], run[:, ST, :]))
                        for k in range(K2):
                            then(dve.tensor_tensor(rkh[:, k, :, :], hot[:, k, :, :], gp, ALU.mult))
                            if k == K2 - 1:
                                dve.sem_inc(done, 1)
                            then(dve.tensor_copy(tiled(g.at_f, k, b), atf[:, :, k]))
                            then(dve.tensor_reduce(tiled(g.rank, k, b), rkh[:, k, :, :], AX.X, ALU.add))
                        assert n == K

                def low_x(b):
                    for n in range(4):
                        dve.wait_ge(T_ok, b * 4 + n + 1)
                        dve.tensor_tensor(xs[1][:, n // 2, 512 * (n % 2):512 * (n % 2) + 512],
                                          pt[:, n % 2, :, :].rearrange("p a b -> p (a b)"),
                                          xs[0][:, n // 2, 512 * (n % 2):512 * (n % 2) + 512], ALU.subtract).then_inc(lo_ok, 1)

                def maxima(b, i):
                    keys = P * (i + 1)
                    dve.wait_ge(sc_ok, b * ST + i + 1)
                    dve.tensor_reduce(mx[:, i:i + 1], sc[i % 2][:].rearrange("p a t -> p (a t)")[:, 0:keys],
                                      AX.X, ALU.max).then_inc(mx_ok, 1)
                    dve.wait_ge(mx_ok, b * ST + i + 1)
                    dve.tensor_scalar(nmx[:, i:i + 1], mx[:, i:i + 1], -SCALE, None, ALU.mult).then_inc(nmx_ok, 1)

                def one(b, u, v):
                    first, second = halves(b)
                    if not first:
                        norm_stats(x3[1 - u], 0, g_stats)
                        variances(b + 1, b - 1, None)
                        sharpen(b + 1, 0, ST)
                        norm_x3(b - 1, x3[1 - u])
                        for part in range(len(TOP2_AT)):
                            top2(b - 1, part)
                        return
                    following = not isinstance(b, int) or b < B - 1
                    if second:
                        dve.wait_ge(x3_ok, b * ST)
                        norm_stats(x3[1 - u], 0, g_stats)
                    if following:
                        next_stats(b + 1, v + 1 + u, 1 - u)
                    variances(b + 1, b - 1 if second else None, b + 1 if following else None)
                    sharpen(b + 1, *norms(b))
                    if second:
                        norm_x3(b - 1, x3[1 - u])
                    if following:
                        norm_x2(b + 1, x2[1 - u])
                    for n in range(4):
                        dve.wait_ge(pj_ok, b * 12 + n + 9)
                        dve.scalar_tensor_tensor(out=v_[:, 2 * n:2 * n + 2, :],
                                                 in0=sc[n // 2][:, n % 2, :].rearrange("p (a d) -> p a d", a=2),
                                                 scalar=1.0 / WS, in1=bv_row[:].unsqueeze(1).to_broadcast([P, 2, D]),
                                                 op0=ALU.mult, op1=ALU.add).then_inc(v_ok, 1)
                    maxima(b, 0)
                    maxima(b, 1)
                    for n in range(ST):
                        if n >= 4:
                            dve.wait_ge(pt_ok, b * ST + n + 1)
                            dve.wait_ge(z_ok, b * ST + n)
                            dve.tensor_copy(pT[:, 4:n + 1, :], pt[:, 1, 0:n - 3, :]).then_inc(pTb_ok, 1)
                        else:
                            dve.wait_ge(exp_ok, b * ST + n + 1)
                            dve.sem_inc(pTb_ok, 1)
                        if n + 2 < ST:
                            maxima(b, n + 2)
                        dve.reciprocal(rinv[:, n:n + 1], rs[:, n:n + 1]).then_inc(rinv_ok, 1)
                        dve.wait_ge(rinv_ok, b * ST + n + 1)
                        dve.wait_ge(z_ok, b * ST + n + 1)
                        if n == 0:
                            dve.wait_ge(out[u], v * 16)
                        dve.scalar_tensor_tensor(out=x3[u][:, n, :], in0=z[:, 0:D], scalar=rinv[:, n:n + 1],
                                                 in1=x2[u][:, n, :], op0=ALU.mult, op1=ALU.add).then_inc(x3_ok, 1)
                        if n == ST - 1 and following:
                            low_x(b + 1)
                        if second and n in TOP2_AT:
                            top2(b - 1, TOP2_AT.index(n))
                dve.wait_ge(zero2_ok, 1)
                for i in range(3):
                    dve.wait_ge(w_hi, i + 1)
                    dve.scalar_tensor_tensor(out=ws[1][:, i, :, :].rearrange("p c n -> p (c n)"),
                                             in0=pt[:, 0, :, :].rearrange("p a b -> p (a b)"), scalar=WS,
                                             in1=ws[0][:, i, :, :].rearrange("p c n -> p (c n)"),
                                             op0=ALU.mult, op1=ALU.subtract).then_inc(w_lo, 1)
                next_stats(0, 1, 0)
                variances(0, None, 0)
                sharpen(0, ST, 2 * ST)
                norm_x2(0, x2[0])
                low_x(0)
                in_steps(dve, one)
                dve.sem_inc(fin, 1)
                dve.wait_ge(fin, 2)
                dve.tensor_copy(g.count[:], gb[:, 0:E1]).then_inc(fin, 1)


def tiled(t, k, b):
    return t.rearrange("p k (b c) -> p k b c", b=B)[:, k, b, :]


MLP = 512
TILES = T * K2 // P + E1
QUAD = 4
DUMMY = K2 * T


W_DMAS = 3 * 16
NTAB = 16 * 4


def load_expert(sp, g, v, u):
    w0_e = g.w0.rearrange("(v u) (c p) n -> v u p c n", u=QUAD, p=P)
    w1_e = g.w1.rearrange("(v u) (c p) n -> v u p c n", u=QUAD, p=P)
    wo_e = g.wo.rearrange("(v u) (c p) n -> v u p c n", u=QUAD, p=P)
    sp.dma_start(g.w01_sb[:, u, 0, :, :], w0_e[v, u]).then_inc(g.w_in, 16)
    sp.dma_start(g.w01_sb[:, u, 1, :, :], w1_e[v, u]).then_inc(g.w_in, 16)
    sp.dma_start(g.wo_sb[:, u, :, :], wo_e[v, u]).then_inc(g.w_in, 16)


def second_mixture(nc, g):
    with ExitStack() as ctx:
        sb = lambda n, s, d=F32: ctx.enter_context(nc.sbuf_tensor(n, s, d))
        g.w01_sb = sb("k_w01", [P, QUAD, 2, DC, MLP])
        g.wo_sb = sb("k_wo", [P, QUAD, MLP // P, D])
        g.te = sb("k_te", [1, 2, TILES], I32)
        g.end_row = sb("k_end", [1, E1], I32)
        g.nq = sb("k_nq", [1, 1], I32)
        g.w_in, g.t_in = g.sem("k_w_in"), g.sem("k_t_in")
        place_rows(nc, g)
        expert_rows(nc, g)


def place_rows(nc, g):
    N = K2 * NT
    CG = 8
    with ExitStack() as ctx:
        sb = lambda n, s, d=F32: ctx.enter_context(nc.sbuf_tensor(n, s, d))
        ci, ti = sb("j_ci", [P, E1], I32), sb("j_ti", [P, E1], I32)
        tf, one, end, beg = (sb("j_" + n, [P, E1]) for n in ("tf", "one", "end", "beg"))
        hit = sb("j_hit", [P, NT, E1], BF16)
        at_b, beg_b = sb("j_at_b", [P, K2, NT], BF16), sb("j_beg_b", [P, E1], BF16)
        rowf = sb("j_rowf", [P, K2, NT])
        row = sb("j_row", [P, K2, NT], I32)
        part = sb("j_part", [P, 2, N], I32)
        part_f = sb("j_part_f", [P, 3, N])
        col = sb("j_col", [P, N], I32)
        at = [sb(f"j_at{u}", [P, 3, CG]) for u in range(2)]
        tiles_i, tiles_b = sb("j_tiles_i", [P, TILES], I32), sb("j_tiles_b", [P, TILES], BF16)
        hot_at = [sb(f"j_hot_at{u}", [P, CG, P], BF16) for u in range(2)]
        hot_num = [sb(f"j_hot_num{u}", [P, 2, CG, P], BF16) for u in range(2)]
        hot_tile = [sb(f"j_hot_tile{u}", [P, CG, TILES], BF16) for u in range(2)]
        zero = sb("j_zero", [P, 2 * TILES], BF16)
        low, neg, num = sb("j_low", [P, TILES]), sb("j_neg", [P, TILES]), sb("j_num", [P, TILES])
        num_i = sb("j_num_i", [P, TILES], I32)
        tile_f, te_f, cmp_ = sb("j_tile_f", [P, 2]), sb("j_te_f", [P, 2]), sb("j_cmp", [P, 2, E1])
        tile_i, te_i = sb("j_tile_i", [P, 2], I32), sb("j_te_i", [P, 2, 2], I32)
        end_i, quads = sb("j_end_i", [P, E1], I32), sb("j_quads", [P, 1], I32)
        acc = ctx.enter_context(nc.psum_tensor("j_acc", [P, 2, TILES], F32))
        step, made, tabled, at_ok, hot_ok, num_ok, used, summed = (
            g.sem("j_" + n) for n in ("step", "made", "tabled", "at", "hot", "num", "used", "summed"))
        with nc.allow_non_contiguous_dma(reason="two short tables"), nc.Block() as block:
            @block.gpsimd
            def _(pool):
                pool.iota(tile_i[:], pattern=[[P, 2]], base=0, channel_multiplier=1).then_inc(made, 1)
                pool.iota(col[:], pattern=[[1, N]], base=1, channel_multiplier=0).then_inc(made, 1)
                pool.iota(tiles_i[:], pattern=[[1, TILES]], base=0, channel_multiplier=0).then_inc(made, 1)
                pool.memset(zero[:], 0.0).then_inc(made, 1)

            @block.sync
            def _(sp):
                for u in range(QUAD):
                    if u:
                        sp.wait_ge(g.w_in, W_DMAS * u)
                    load_expert(sp, g, 0, u)
                sp.wait_ge(step, 13)
                sp.dma_start(g.tile_expert[:, 0:P, 0].rearrange("s p -> p s"), te_i[:, 0, :]).then_inc(tabled, 16)
                sp.dma_start(g.tile_expert[:, P:TILES, 0].rearrange("s p -> p s"), te_i[0:TILES - P, 1, :]).then_inc(tabled, 16)
                sp.dma_start(g.tile_end, end_i[0:1, :]).then_inc(tabled, 16)
                sp.dma_start(g.quads, quads[0:1, :]).then_inc(tabled, 16)
                sp.wait_ge(tabled, 64)
                sp.dma_start(g.te[:, 0, :], g.tile_expert[0].rearrange("t a -> a t")).then_inc(g.t_in, 16)
                sp.dma_start(g.te[:, 1, :], g.tile_expert[1].rearrange("t a -> a t")).then_inc(g.t_in, 16)
                sp.dma_start(g.end_row[:], g.tile_end).then_inc(g.t_in, 16)
                sp.dma_start(g.nq[:], g.quads).then_inc(g.t_in, 16)

            @block.tensor
            def _(pe):
                flat = acc[:].rearrange("p i t -> p (i t)")
                pe.wait_ge(made, 4)
                pe.matmul(flat, zero[:, 0:P], zero[:], start=True, stop=False).then_inc(used, 1)
                with pe.Fori(0, N // CG // 2) as v:
                    for u in range(2):
                        pe.wait_ge(num_ok, (v * 2 + u) * (CG + 1) + CG + 1)
                        for c in range(CG):
                            for i in range(2):
                                last = pe.matmul(acc[:, i, :], hot_num[u][:, i, c, :], hot_tile[u][:, c, :],
                                                 start=False, stop=False)
                        last.then_inc(used, 1)
                pe.matmul(flat, zero[:, 0:P], zero[:], start=False, stop=True).then_inc(summed, 1)

            @block.scalar
            def _(act):
                with act.Fori(0, N // CG // 2) as v:
                    for u in range(2):
                        act.wait_ge(hot_ok, v * 2 + u + 1)
                        act.mul(hot_num[u][:, 1, :, :], hot_at[u][:], g.part_f[:, 0:1]).then_inc(num_ok, 1)
                        for c in range(CG):
                            act.mul(hot_num[u][:, 0, c, :], hot_at[u][:, c, :], at[u][:, 2, c:c + 1]).then_inc(num_ok, 1)

            @block.vector
            def _(dve):
                n = 0

                def then(ins):
                    nonlocal n
                    n += 1
                    ins.then_inc(step, 1)
                    dve.wait_ge(step, n)
                dve.memset(one[:], 1.0)
                then(dve.tensor_scalar(ci[:], g.count[:], float(P - 1), None, ALU.add))
                then(dve.tensor_scalar(ti[:], ci[:], 7, None, ALU.logical_shift_right))
                then(dve.tensor_copy(tf[:], ti[:]))
                then(dve.tensor_tensor_scan(end[:], one[:], tf[:], 0.0, ALU.mult, ALU.add))
                then(dve.tensor_tensor(beg[:], end[:], tf[:], ALU.subtract))
                dve.wait_ge(made, 4)
                then(dve.tensor_copy(tile_f[:], tile_i[:]))
                then(dve.tensor_tensor(cmp_[:], tile_f[:].unsqueeze(2).to_broadcast([P, 2, E1]),
                                       end[:].unsqueeze(1).to_broadcast([P, 2, E1]), ALU.is_ge))
                then(dve.tensor_reduce(te_f[:], cmp_[:], AX.X, ALU.add))
                then(dve.tensor_scalar(te_i[:, :, 0], te_f[:], float(E1 - 1), None, ALU.min))
                then(dve.tensor_scalar(te_i[:, :, 1], te_i[:, :, 0], QUAD - 1, None, ALU.bitwise_and))
                then(dve.tensor_copy(end_i[:], end[:]))
                then(dve.tensor_scalar(ci[:, 0:1], end[:, E1 - 1:E1], -1.0, None, ALU.add))
                then(dve.tensor_scalar(quads[:], ci[:, 0:1], 2, None, ALU.logical_shift_right))
                then(dve.tensor_copy(tiles_b[:], tiles_i[:]))
                then(dve.tensor_copy(beg_b[:], beg[:]))
                then(dve.tensor_copy(at_b[:], g.at_f))
                for k in range(K2):
                    dve.tensor_tensor(hit[:], at_b[:, k, :].unsqueeze(2).to_broadcast([P, NT, E1]),
                                      tiles_b[:, 0:E1].unsqueeze(1).to_broadcast([P, NT, E1]), ALU.is_equal).then_inc(g.hit_step, 1)
                    dve.wait_ge(g.hit_step, 3 * k + 1)
                    dve.tensor_tensor(hit[:], hit[:], beg_b[:].unsqueeze(1).to_broadcast([P, NT, E1]), ALU.mult).then_inc(g.hit_step, 1)
                    dve.wait_ge(g.hit_step, 3 * k + 2)
                    dve.tensor_reduce(rowf[:, k, :], hit[:], AX.X, ALU.add).then_inc(g.hit_step, 1)
                    dve.wait_ge(g.hit_step, 3 * k + 3)
                then(dve.scalar_tensor_tensor(out=row[:], in0=rowf[:], scalar=float(P), in1=g.rank, op0=ALU.mult, op1=ALU.add))
                flat = row[:].rearrange("p k c -> p (k c)")
                then(dve.tensor_scalar(part[:, 0, :], flat, P - 1, None, ALU.bitwise_and))
                then(dve.tensor_scalar(part[:, 1, :], flat, 7, None, ALU.logical_shift_right))
                then(dve.tensor_copy(part_f[:, 0:2, :], part[:]))
                then(dve.tensor_copy(part_f[:, 2, :], col[:]))
                columns = part_f[:].rearrange("p i (v u c) -> p v u i c", u=2, c=CG)
                with dve.Fori(0, N // CG // 2) as v:
                    for u in range(2):
                        i = v * 2 + u
                        dve.wait_ge(used, i)
                        dve.tensor_copy(at[u][:], columns[:, v, u, :, :]).then_inc(at_ok, 1)
                        wait_alone(dve, g, at_ok, i + 1)
                        for c in range(CG):
                            scalar = lambda k: at[u][:, k, c:c + 1]
                            dve.tensor_scalar(hot_at[u][:, c, :], tiles_b[:, 0:P], scalar(0), None, ALU.is_equal)
                            last = dve.tensor_scalar(hot_tile[u][:, c, :], tiles_b[:], scalar(1), None, ALU.is_equal)
                        last.then_inc(hot_ok, 1)
                dve.wait_ge(summed, 1)
                then(dve.tensor_scalar(low[:], acc[:, 1, :], -float(P), None, ALU.add))
                then(dve.scalar_tensor_tensor(out=num[:], in0=acc[:, 0, :], scalar=float(P), in1=low[:], op0=ALU.mult, op1=ALU.add))
                then(dve.tensor_scalar(neg[:], num[:], 0.0, float(DUMMY + P), ALU.is_lt, ALU.mult))
                then(dve.tensor_tensor(num[:], num[:], neg[:], ALU.add))
                then(dve.tensor_copy(num_i[:], num[:]))
                src = g.row_src[:].rearrange("p q a -> p (q a)")
                then(dve.tensor_scalar(src, num_i[:], T - 1, None, ALU.bitwise_and))
                then(dve.tensor_scalar(neg[:], num[:], float(DUMMY), float(T), ALU.is_ge, ALU.mult))
                then(dve.tensor_tensor(g.row_dst[:].rearrange("p q a -> p (q a)"), src, neg[:], ALU.add))
                choice = g.row_choice[:].rearrange("p q a k -> p (q a) k")
                then(dve.tensor_scalar(choice[:, :, 0], num[:], float(T), None, ALU.is_lt))
                then(dve.tensor_scalar(choice[:, :, 1], num[:], float(T), None, ALU.is_ge))


def expert_rows(nc, g):
    MC = MLP // P
    R = QUAD
    with ExitStack() as ctx:
        g.ctx = ctx
        sb = lambda n, s, d=F32: ctx.enter_context(nc.sbuf_tensor(n, s, d))
        te, end, nq, w01, wo = g.te, g.end_row, g.nq, g.w01_sb, g.wo_sb
        di = [sb(f"k_di{u}", [P, 1], I32) for u in range(R)]
        si = [sb(f"k_si{u}", [P, 1], I32) for u in range(R)]
        xg = [sb(f"k_xg{u}", [P, ROW1]) for u in range(R)]
        wk = [sb(f"k_wk{u}", [P, K2]) for u in range(R)]
        wr = [sb(f"k_wr{u}", [P, 1]) for u in range(R)]
        xT = [sb(f"k_xT{u}", [P, DC, P]) for u in range(2)]
        sl = sb("k_sl", [P, MLP])
        it = [sb(f"k_it{u}", [P, MLP]) for u in range(2)]
        iT = sb("k_iT", [P, MC, P])
        y = [sb(f"k_y{u}", [P, D]) for u in range(R)]
        xp = ctx.enter_context(nc.psum_tensor("k_xp", [P, 4, P], F32))
        h = [ctx.enter_context(nc.psum_tensor(f"k_h{u}", [P, 2, MLP], F32)) for u in range(2)]
        ip = ctx.enter_context(nc.psum_tensor("k_ip", [P, MC, P], F32))
        yp = [ctx.enter_context(nc.psum_tensor(f"k_yp{u}", [P, D], F32)) for u in range(2)]
        t_in, w_in = g.t_in, g.w_in
        x_in = [g.sem(f"k_x_in{u}") for u in range(R)]
        put = [g.sem(f"k_put{u}") for u in range(R)]
        wk_ok, wr_ok, si_ok, di_ok, xp_ok, xT_ok, h_ok, sl_ok, it_ok, ip_ok, iT_ok, yp_ok, y_ok = (
            g.sem("k_" + n) for n in ("wk", "wr", "si", "di", "xp", "xT", "h", "sl", "it", "ip", "iT", "yp", "y"))

        def last_quad(eng):
            eng.wait_ge(t_in, NTAB)
            return eng.value_load(nq[0:1, 0:1], min_val=T * K2 // P // R - 1, max_val=TILES // R - 1)

        with nc.Block() as block:
            @block.sync
            def _(sp):
                sp.wait_ge(t_in, NTAB)
                ends = end[:].rearrange("a (v u) -> a v u", u=R)
                with sp.Fori(1, E1 // R) as v:
                    for u in range(R):
                        last = sp.value_load(ends[:, v - 1, u:u + 1], min_val=0, max_val=TILES)
                        sp.wait_ge(yp_ok, last)
                        sp.wait_ge(w_in, (v * R + u) * W_DMAS)
                        load_expert(sp, g, v, u)
                sp.wait_ge(w_in, E1 * W_DMAS)

            @block.gpsimd
            def _(pool):
                def gather(q, u):
                    if not isinstance(q, int):
                        wait_alone(pool, g, wk_ok, q * R + u - 3)
                    pool.tensor_copy(si[u][:], g.row_src[:, q, u:u + 1]).then_inc(si_ok, 1)
                    wait_alone(pool, g, si_ok, q * R + u + 1)
                    pool.indirect_dma_start(
                        out=xg[u][:], out_offset=None, in_=g.xn3,
                        in_offset=bass.IndirectOffsetOnAxis(ap=si[u][:], axis=0)).then_inc(x_in[u], 16)

                def add(q, u):
                    wait_alone(pool, g, put[u], q * 16)
                    pool.tensor_copy(di[u][:], g.row_dst[:, q, u:u + 1]).then_inc(di_ok, 1)
                    wait_alone(pool, g, di_ok, q * R + u + 1)
                    wait_alone(pool, g, y_ok, q * R + u + 1)
                    if u >= 1:
                        wait_alone(pool, g, put[u - 1], q * 16 + 16)
                    else:
                        wait_alone(pool, g, put[R - 1], q * 16)
                    add_rows(pool, g, y[u], di[u], put[u])
                m = last_quad(pool)
                for u in range(R):
                    gather(0, u)
                with pool.Fori(1, m + 1) as q:
                    for u in range(R):
                        add(q - 1, u)
                        gather(q, u)
                for u in range(R):
                    add(m, u)
                for u in range(R):
                    wait_alone(pool, g, put[u], m * 16 + 16)

            @block.tensor
            def _(pe):
                m = last_quad(pe)

                def x_by_column(q, u):
                    pe.wait_ge(x_in[u], q * 16 + 16)
                    pe.wait_ge(xT_ok, q * R + u)
                    for k in range(DC):
                        last = pe.transpose(xp[:, k, :], xg[u][:, P * k:P * k + P], g.ident[:])
                    last.then_inc(xp_ok, 1)

                def last_product(i, q, u, place):
                    pe.wait_ge(iT_ok, i - 1)
                    pe.wait_ge(y_ok, max(i - 3, 0) if isinstance(i, int) else i - 3)
                    for k in range(MC):
                        last = pe.matmul(yp[u % 2][:], iT[:, k, :], wo[:, place, k, :], start=(k == 0), stop=(k == MC - 1))
                    last.then_inc(yp_ok, 1)

                def product_by_column(i, u):
                    pe.wait_ge(it_ok, i)
                    for k in range(MC):
                        last = pe.transpose(ip[:, k, :], it[u % 2][:, P * k:P * k + P], g.ident[:])
                    last.then_inc(ip_ok, 1)

                def first_products(q, u, e, place):
                    i = q * R + u
                    pe.wait_ge(xT_ok, i + 1)
                    pe.wait_ge(w_in, e * W_DMAS + W_DMAS)
                    for m in range(2):
                        for k in range(DC):
                            last = pe.matmul(h[u % 2][:, m, :], xT[u % 2][:, k, :], w01[:, place, m, k, :],
                                             start=(k == 0), stop=(k == DC - 1))
                    last.then_inc(h_ok, 1)

                def expert_of(q, u):
                    at = te[:].rearrange("o s (q u) -> o s q u", u=R)
                    return (pe.value_load(at[:, 0, q, u:u + 1], min_val=0, max_val=E1 - 1),
                            pe.value_load(at[:, 1, q, u:u + 1], min_val=0, max_val=R - 1))

                def place_before(q, u, back):
                    at = te[:].rearrange("o s (q u) -> o s q u", u=R)
                    q, u = (q, u - back) if u >= back else (q - 1, u - back + R)
                    return pe.value_load(at[:, 1, q, u:u + 1], min_val=0, max_val=R - 1)

                def tile(q, u, first=False):
                    e, place = expert_of(q, u)
                    if not first or u >= 2:
                        before = place_before(q, u, 2)
                    x_by_column(q, u)
                    if not first or u >= 2:
                        last_product(q * R + u, q, u, before)
                    if not first or u >= 1:
                        product_by_column(q * R + u, u + 1)
                    first_products(q, u, e, place)
                for u in range(R):
                    tile(0, u, True)
                with pe.Fori(1, m + 1) as q:
                    for u in range(R):
                        tile(q, u)
                last_product(m * R + R, m, 0, place_before(m, R, 2))
                product_by_column(m * R + R, 1)
                last_product(m * R + R + 1, m, 1, place_before(m, R + 1, 2))

            @block.scalar
            def _(act):
                m = last_quad(act)

                def by_column(i):
                    act.wait_ge(ip_ok, i)
                    act.copy(iT[:].rearrange("p a b -> p (a b)"), ip[:].rearrange("p a b -> p (a b)")).then_inc(iT_ok, 1)

                def tile(q, u, first=False):
                    i = q * R + u
                    if not first or u >= 1:
                        by_column(i)
                    act.wait_ge(h_ok, i + 1)
                    act.wait_ge(it_ok, i)
                    act.activation(sl[:], h[u % 2][:, 0, :], ACT.Silu).then_inc(sl_ok, 1)
                for u in range(R):
                    tile(0, u, True)
                with act.Fori(1, m + 1) as q:
                    for u in range(R):
                        tile(q, u)
                by_column(m * R + R)

            @block.vector
            def _(dve):
                m = last_quad(dve)

                def y_out(q, u):
                    dve.wait_ge(yp_ok, q * R + u + 1)
                    dve.wait_ge(put[u], q * 16)
                    dve.tensor_scalar(y[u][:], yp[u % 2][:], wr[u][:, 0:1], None, ALU.mult).then_inc(y_ok, 1)

                def tile(q, u, first=False):
                    i = q * R + u
                    dve.wait_ge(xp_ok, i + 1)
                    dve.tensor_copy(xT[u % 2][:], xp[:, 0:DC, :]).then_inc(xT_ok, 1)
                    dve.tensor_tensor(wk[u][:], xg[u][:, D:ROW1], g.row_choice[:, q, u, :], ALU.mult).then_inc(wk_ok, 1)
                    if not first or u >= 2:
                        y_out(*((q, u - 2) if u >= 2 else (q - 1, u + R - 2)))
                    dve.wait_ge(wk_ok, i + 1)
                    dve.tensor_tensor(wr[u][:], wk[u][:, 0:1], wk[u][:, 1:2], ALU.add).then_inc(wr_ok, 1)
                    wait_alone(dve, g, wr_ok, i + 1)
                    dve.wait_ge(sl_ok, i + 1)
                    dve.tensor_tensor(it[u % 2][:], h[u % 2][:, 1, :], sl[:], ALU.mult).then_inc(it_ok, 1)
                for u in range(R):
                    tile(0, u, True)
                with dve.Fori(1, m + 1) as q:
                    for u in range(R):
                        tile(q, u)
                y_out(m, R - 2)
                y_out(m, R - 1)


def add_rows(pool, g, y, di, put):
    pool.indirect_dma_start(out=g.out, in_=y[:], in_offset=None, compute_op=ALU.add,
                            out_offset=bass.IndirectOffsetOnAxis(ap=di[:], axis=0),
                            bounds_check=T - 1, oob_is_err=False).then_inc(put, 16)




def two_layers(nc, ins, out):
    with ExitStack() as ctx:
        def sb(name, shape, dt=F32):
            return ctx.enter_context(nc.sbuf_tensor(name, shape, dt))

        def dram(name, shape, dt=F32):
            return nc.dram_tensor(name, shape, dt, kind="Internal").ap()

        g = Shared()
        sems = []

        def sem(name):
            sems.append(nc.alloc_semaphore(name=name))
            return sems[-1]

        g.sem = sem
        g.passed = sem("passed")
        g.x, g.Wq, g.bq, g.Wk, g.bk, g.Wv, g.bv, g.Wo, g.bo, g.sample_idx = (
            ins["L0_attn_" + n] for n in ("x", "Wq", "bq", "Wk", "bk", "Wv", "bv", "Wo", "bo", "sample_idx"))
        g.gate, g.W1, g.b1, g.W2, g.b2, g.Ws1, g.bs1, g.Ws2, g.bs2 = (
            ins["L0_ffn_" + n] for n in ("gate", "W1", "b1", "W2", "b2", "Ws1", "bs1", "Ws2", "bs2"))
        g.Wq1, g.bq1, g.Wk1, g.bk1, g.Wv1, g.bv1 = (ins["L1_attn_" + n] for n in ("Wq", "bq", "Wk", "bk", "Wv", "bv"))
        g.gate1, g.w0, g.w1, g.wo = (ins["L1_ffn_" + n] for n in ("gate_kernel", "w0", "w1", "wo"))
        g.out = out.rearrange("b s d -> (b s) d")

        g.ident, g.ones, g.tri = sb("ident", [P, P]), sb("ones", [P, P]), sb("tri", [P, P])
        g.iota_i, g.iota_f = sb("iota_i", [P, P], I32), sb("iota_f", [P, P])
        g.part_i, g.part_f = sb("part_i", [P, 1], I32), sb("part_f", [P, 1])
        g.probs = sb("probs", [P, E0, NT])[:]
        g.elist = sb("elist", [P, E0, CAP // P], I32)
        g.at_f, g.rank = (sb(n, [P, K2, NT])[:] for n in ("at_f", "rank"))
        g.count = sb("count", [P, E1])
        g.row_dst, g.row_src = (sb(n, [P, TILES // QUAD, QUAD], I32) for n in ("row_dst", "row_src"))
        g.row_choice = sb("row_choice", [P, TILES // QUAD, QUAD, K2])

        g.xs = dram("xs", (B, 2, P, DC, S), F16)
        g.q_rows = dram("q_rows", (T * H, HD))
        g.q16, g.k16 = dram("q16", (B, 2, D, S), F16), dram("k16", (B, 2, D, U), F16)
        g.m_rows, g.sel_rows = dram("m_rows", (P, S)), dram("sel_rows", (P * TOP, 1), I32)
        g.attn_rows = dram("attn_rows", (T * H, HD))
        g.x1, g.x2 = (dram(n, (T, D)) for n in ("x1", "x2"))
        g.x3 = g.out
        g.tab, g.xnT1 = dram("tab", (T, ROW)), dram("xnT1", (B, P, DC, S))
        g.xn3 = dram("xn3", (T, ROW1))
        g.tile_expert = dram("tile_expert", (2, TILES, 1), I32)
        g.tile_end, g.quads = dram("tile_end", (1, E1), I32), dram("quads", (1, 1), I32)

        constants(nc, g)
        project_and_score(nc, g)
        pick_queries(nc, g)
        attend_selected(nc, g)
        add_attention_and_gate(nc, g)
        shared_ffn_and_choice(nc, g)
        expert_ffn(nc, g)
        nc.clear_and_free_semaphores(sems)
        nc.all_engine_barrier()
        g.passed, g.hit_step = sem("passed1"), sem("hit_step")
        attention_and_top2(nc, g)
        second_mixture(nc, g)


_INS = (["L0_attn_" + n for n in ("x", "Wq", "bq", "Wk", "bk", "Wv", "bv", "Wo", "bo", "sample_idx")]
        + ["L0_ffn_" + n for n in ("gate", "W1", "b1", "W2", "b2", "Ws1", "bs1", "Ws2", "bs2")]
        + ["L1_attn_" + n for n in ("Wq", "bq", "Wk", "bk", "Wv", "bv")]
        + ["L1_ffn_" + n for n in ("gate_kernel", "w0", "w1", "wo")])
_OUT = ((8, 1024, 256), "float32")


def kernel(**inputs):
    import numpy as _np
    import concourse.bacc as _bacc
    from concourse import mybir as _mybir
    from concourse.bass_utils import run_bass_kernel_spmd as _run

    nc = _bacc.Bacc("TRN2", target_bir_lowering=False, num_devices=1)
    arrays, args = {}, {}
    for name in _INS:
        a = _np.ascontiguousarray(inputs[name])
        arrays[f"in_{name}_dram"] = a
        args[name] = nc.dram_tensor(f"in_{name}_dram", a.shape, _mybir.dt.from_np(a.dtype), kind="ExternalInput").ap()
    shape, dtype = _OUT
    out = nc.dram_tensor("out_0_dram", shape, _mybir.dt.from_np(_np.dtype(dtype)), kind="ExternalOutput").ap()
    two_layers(nc, args, out)
    r = _run(nc, [arrays], core_ids=[0])
    return r.results[0]["out_0_dram"]
```
